# Optimizing a Trainium2 kernel written in Bass

```python
import numpy as np
import jax
import jax.numpy as jnp

def _softmax(x, axis=-1):
    return jax.nn.softmax(x, axis=axis)

def _gelu(x):
    return jax.nn.gelu(x, approximate=True)

def _silu(x):
    return jax.nn.silu(x)

def _sigmoid(x):
    return jax.nn.sigmoid(x)

def _layernorm(x, axis=-1, eps=1e-05):
    m = jnp.mean(x, axis=axis, keepdims=True)
    v = jnp.var(x, axis=axis, keepdims=True)
    return (x - m) / jnp.sqrt(v + eps)

def _scatter_add(tgt, idx, src, axis=0):
    return tgt.at[idx].add(src)

def _segment_sum(src, seg, n):
    return jax.ops.segment_sum(src, seg, n)
kernel_name = 'mk_macaron_d2_jaxref_r8_51414b'

def setup_inputs(seed: int=0):
    np.random.seed(seed)
    _w = jnp.asarray

    def _L0_attn_setup():
        import jax, jax.numpy as jnp
        import numpy as np
        B, T, D_MODEL = (2, 256, 128)
        EXPAND, D_STATE, D_CONV = (2, 16, 4)
        D_INNER = EXPAND * D_MODEL
        DT_RANK = (D_MODEL + 15) // 16

        def _mamba(x, W_in, conv_w, conv_b, W_xproj, W_dt, b_dt, A_log, D, W_out):
            Bsz, Tlen, _ = x.shape
            xz = x @ W_in
            u, z = jnp.split(xz, 2, axis=-1)
            up = jnp.pad(u, ((0, 0), (D_CONV - 1, 0), (0, 0)))
            uc = conv_b + sum((up[:, k:k + Tlen, :] * conv_w[:, k] for k in range(D_CONV)))
            uc = jax.nn.silu(uc)
            proj = uc @ W_xproj
            dt, Bm, Cm = jnp.split(proj, [DT_RANK, DT_RANK + D_STATE], axis=-1)
            delta = jax.nn.softplus(dt @ W_dt + b_dt)
            A = -jnp.exp(A_log)
            dA = jnp.exp(delta[..., None] * A)
            dBu = delta[..., None] * Bm[:, :, None, :] * uc[..., None]

            def step(h, inp):
                dA_t, dBu_t, C_t = inp
                h = dA_t * h + dBu_t
                y = jnp.einsum('bdn,bn->bd', h, C_t)
                return (h, y)
            h0 = jnp.zeros((Bsz, D_INNER, D_STATE), x.dtype)
            _, ys = jax.lax.scan(step, h0, (dA.transpose(1, 0, 2, 3), dBu.transpose(1, 0, 2, 3), Cm.transpose(1, 0, 2)))
            y = ys.transpose(1, 0, 2) + uc * D
            y = y * jax.nn.silu(z)
            return y @ W_out
        key = jax.random.key(seed)
        ks = jax.random.split(key, 8)
        g = lambda k, shape, s: jax.random.normal(k, shape, dtype=jnp.float32) * s
        x = jax.random.normal(ks[0], (B, T, D_MODEL), dtype=jnp.float32)
        W_in = g(ks[1], (D_MODEL, 2 * D_INNER), 0.02)
        conv_w = g(ks[2], (D_INNER, D_CONV), 0.1)
        conv_b = jnp.zeros((D_INNER,), jnp.float32)
        W_xproj = g(ks[3], (D_INNER, DT_RANK + 2 * D_STATE), 0.02)
        W_dt = g(ks[4], (DT_RANK, D_INNER), 0.1)
        dt = jnp.exp(jax.random.uniform(ks[5], (D_INNER,), jnp.float32) * (np.log(0.1) - np.log(0.001)) + np.log(0.001))
        b_dt = dt + jnp.log(-jnp.expm1(-dt))
        A_log = jnp.log(jnp.broadcast_to(jnp.arange(1, D_STATE + 1, dtype=jnp.float32), (D_INNER, D_STATE)))
        D = jnp.ones((D_INNER,), jnp.float32)
        W_out = g(ks[6], (D_INNER, D_MODEL), 0.02)
        return dict(x=x, W_in=W_in, conv_w=conv_w, conv_b=conv_b, W_xproj=W_xproj, W_dt=W_dt, b_dt=b_dt, A_log=A_log, D=D, W_out=W_out)
    _L0_attn_in = _L0_attn_setup()

    def _L0_ffn_setup():
        import jax, jax.numpy as jnp
        import numpy as np
        B, S, D = (2, 256, 128)
        E, K, H = (8, 2, 512)
        CAP_FACTOR = 1.0

        def _moe_forward(x, wg, w1, b1, w2, b2):
            Bb, Ss, Dd = x.shape
            T = Bb * Ss
            cap = int(K * CAP_FACTOR * ((T + E - 1) // E))
            xt = x.reshape(T, Dd)
            logits = xt @ wg
            scores = jax.nn.softmax(logits, axis=-1)
            gates_k, idx_k = jax.lax.top_k(scores, K)
            gates_k = gates_k / jnp.sum(gates_k, axis=-1, keepdims=True)
            masks = jax.nn.one_hot(idx_k, E, dtype=jnp.int32)
            m = jnp.transpose(masks, (1, 0, 2)).reshape(K * T, E)
            locs_full = jnp.cumsum(m, axis=0) - 1
            loc = jnp.sum(locs_full * m, axis=-1)
            loc = loc.reshape(K, T).T
            valid = (loc < cap).astype(xt.dtype)
            loc_c = jnp.clip(loc, 0, cap - 1)
            contrib = (xt[:, None, :] * valid[:, :, None]).reshape(T * K, Dd)
            disp = jnp.zeros((E, cap, Dd), xt.dtype)
            disp = disp.at[idx_k.reshape(-1), loc_c.reshape(-1)].add(contrib)
            h = jax.nn.relu(jnp.einsum('ecd,edh->ech', disp, w1) + b1[:, None, :])
            out = jnp.einsum('ech,ehd->ecd', h, w2) + b2[:, None, :]
            gathered = out[idx_k, loc_c]
            y = jnp.einsum('tk,tkd->td', gates_k * valid, gathered)
            return y.reshape(Bb, Ss, Dd)
        key = jax.random.key(seed)
        ks = jax.random.split(key, 6)
        scale_in = 1.0 / np.sqrt(D)
        scale_h = 1.0 / np.sqrt(H)
        return {'x': jax.random.normal(ks[0], (B, S, D), jnp.float32), 'wg': jax.random.normal(ks[1], (D, E), jnp.float32) * scale_in, 'w1': jax.random.normal(ks[2], (E, D, H), jnp.float32) * scale_in, 'b1': jnp.zeros((E, H), jnp.float32), 'w2': jax.random.normal(ks[3], (E, H, D), jnp.float32) * scale_h, 'b2': jnp.zeros((E, D), jnp.float32)}
    _L0_ffn_in = _L0_ffn_setup()

    def _L1_attn_setup():
        import jax, jax.numpy as jnp
        import numpy as np
        B, N, E, H = (2, 256, 128, 16)
        D = E // H
        EPS = 1e-05
        SCALE = D ** (-0.5)
        STD = 0.02
        key = jax.random.key(seed)
        ks = jax.random.split(key, 10)
        rn = lambda k, shape: jax.random.normal(k, shape, dtype=jnp.float32)
        x = rn(ks[0], (B, N, E))
        Wq = rn(ks[1], (E, E)) * STD
        Wk = rn(ks[2], (E, E)) * STD
        Wv = rn(ks[3], (E, E)) * STD
        Wo = rn(ks[4], (E, E)) * STD
        Wf1 = rn(ks[5], (E, D)) * STD
        Wf2 = rn(ks[6], (D, E)) * STD
        Wg1 = rn(ks[7], (E, D)) * STD
        Wg2 = rn(ks[8], (D, E)) * STD
        norm_weight = jnp.ones((E,), dtype=jnp.float32)
        return dict(x=x, Wq=Wq, Wk=Wk, Wv=Wv, Wo=Wo, Wf1=Wf1, Wf2=Wf2, Wg1=Wg1, Wg2=Wg2, norm_weight=norm_weight)
    _L1_attn_in = _L1_attn_setup()

    def _L1_ffn_setup():
        import jax, jax.numpy as jnp
        import numpy as np
        T, Z, D_DIM = (8, 256, 128)
        N_EXP, P_SLOT, H = (64, 32, 128)
        LN_EPS = 1e-05
        key = jax.random.key(seed)
        k = jax.random.split(key, 5)
        s = 0.02
        return {'x': jax.random.normal(k[0], (T, Z, D_DIM), dtype=jnp.float32), 'phi_w': jax.random.normal(k[1], (N_EXP * P_SLOT, D_DIM), dtype=jnp.float32) * s, 'phi_b': jax.random.normal(k[2], (N_EXP * P_SLOT,), dtype=jnp.float32) * s, 'expert_w': jax.random.normal(k[3], (N_EXP, D_DIM, H), dtype=jnp.float32) * s, 'expert_b': jax.random.normal(k[4], (N_EXP, H), dtype=jnp.float32) * s}
    _L1_ffn_in = _L1_ffn_setup()
    _d = {'L0_attn_x': _L0_attn_in['x'], 'L0_attn_W_in': _L0_attn_in['W_in'], 'L0_attn_conv_w': _L0_attn_in['conv_w'], 'L0_attn_conv_b': _L0_attn_in['conv_b'], 'L0_attn_W_xproj': _L0_attn_in['W_xproj'], 'L0_attn_W_dt': _L0_attn_in['W_dt'], 'L0_attn_b_dt': _L0_attn_in['b_dt'], 'L0_attn_A_log': _L0_attn_in['A_log'], 'L0_attn_D': _L0_attn_in['D'], 'L0_attn_W_out': _L0_attn_in['W_out'], 'L0_ffn_wg': _L0_ffn_in['wg'], 'L0_ffn_w1': _L0_ffn_in['w1'], 'L0_ffn_b1': _L0_ffn_in['b1'], 'L0_ffn_w2': _L0_ffn_in['w2'], 'L0_ffn_b2': _L0_ffn_in['b2'], 'L1_attn_Wq': _L1_attn_in['Wq'], 'L1_attn_Wk': _L1_attn_in['Wk'], 'L1_attn_Wv': _L1_attn_in['Wv'], 'L1_attn_Wo': _L1_attn_in['Wo'], 'L1_attn_Wf1': _L1_attn_in['Wf1'], 'L1_attn_Wf2': _L1_attn_in['Wf2'], 'L1_attn_Wg1': _L1_attn_in['Wg1'], 'L1_attn_Wg2': _L1_attn_in['Wg2'], 'L1_attn_norm_weight': _L1_attn_in['norm_weight'], 'L1_ffn_phi_w': _L1_ffn_in['phi_w'], 'L1_ffn_phi_b': _L1_ffn_in['phi_b'], 'L1_ffn_expert_w': _L1_ffn_in['expert_w'], 'L1_ffn_expert_b': _L1_ffn_in['expert_b']}
    _x0 = _d['L0_attn_x']
    _d['L0_attn_x'] = jax.random.normal(jax.random.fold_in(jax.random.key(seed), 1), (4, 1024, 128), dtype=_x0.dtype)
    del _x0
    return _d

def reference(L0_attn_x, L0_attn_W_in, L0_attn_conv_w, L0_attn_conv_b, L0_attn_W_xproj, L0_attn_W_dt, L0_attn_b_dt, L0_attn_A_log, L0_attn_D, L0_attn_W_out, L0_ffn_wg, L0_ffn_w1, L0_ffn_b1, L0_ffn_w2, L0_ffn_b2, L1_attn_Wq, L1_attn_Wk, L1_attn_Wv, L1_attn_Wo, L1_attn_Wf1, L1_attn_Wf2, L1_attn_Wg1, L1_attn_Wg2, L1_attn_norm_weight, L1_ffn_phi_w, L1_ffn_phi_b, L1_ffn_expert_w, L1_ffn_expert_b):

    def _L0_attn_ref(x, W_in, conv_w, conv_b, W_xproj, W_dt, b_dt, A_log, D, W_out):
        import jax, jax.numpy as jnp
        import numpy as np
        B, T, D_MODEL = (2, 256, 128)
        EXPAND, D_STATE, D_CONV = (2, 16, 4)
        D_INNER = EXPAND * D_MODEL
        DT_RANK = (D_MODEL + 15) // 16

        def _mamba(x, W_in, conv_w, conv_b, W_xproj, W_dt, b_dt, A_log, D, W_out):
            Bsz, Tlen, _ = x.shape
            xz = x @ W_in
            u, z = jnp.split(xz, 2, axis=-1)
            up = jnp.pad(u, ((0, 0), (D_CONV - 1, 0), (0, 0)))
            uc = conv_b + sum((up[:, k:k + Tlen, :] * conv_w[:, k] for k in range(D_CONV)))
            uc = jax.nn.silu(uc)
            proj = uc @ W_xproj
            dt, Bm, Cm = jnp.split(proj, [DT_RANK, DT_RANK + D_STATE], axis=-1)
            delta = jax.nn.softplus(dt @ W_dt + b_dt)
            A = -jnp.exp(A_log)
            dA = jnp.exp(delta[..., None] * A)
            dBu = delta[..., None] * Bm[:, :, None, :] * uc[..., None]

            def step(h, inp):
                dA_t, dBu_t, C_t = inp
                h = dA_t * h + dBu_t
                y = jnp.einsum('bdn,bn->bd', h, C_t)
                return (h, y)
            h0 = jnp.zeros((Bsz, D_INNER, D_STATE), x.dtype)
            _, ys = jax.lax.scan(step, h0, (dA.transpose(1, 0, 2, 3), dBu.transpose(1, 0, 2, 3), Cm.transpose(1, 0, 2)))
            y = ys.transpose(1, 0, 2) + uc * D
            y = y * jax.nn.silu(z)
            return y @ W_out
        return _mamba(x, W_in, conv_w, conv_b, W_xproj, W_dt, b_dt, A_log, D, W_out)

    def _L0_ffn_ref(x, wg, w1, b1, w2, b2):
        import jax, jax.numpy as jnp
        import numpy as np
        B, S, D = (2, 256, 128)
        E, K, H = (8, 2, 512)
        CAP_FACTOR = 1.0

        def _moe_forward(x, wg, w1, b1, w2, b2):
            Bb, Ss, Dd = x.shape
            T = Bb * Ss
            cap = int(K * CAP_FACTOR * ((T + E - 1) // E))
            xt = x.reshape(T, Dd)
            logits = xt @ wg
            scores = jax.nn.softmax(logits, axis=-1)
            gates_k, idx_k = jax.lax.top_k(scores, K)
            gates_k = gates_k / jnp.sum(gates_k, axis=-1, keepdims=True)
            masks = jax.nn.one_hot(idx_k, E, dtype=jnp.int32)
            m = jnp.transpose(masks, (1, 0, 2)).reshape(K * T, E)
            locs_full = jnp.cumsum(m, axis=0) - 1
            loc = jnp.sum(locs_full * m, axis=-1)
            loc = loc.reshape(K, T).T
            valid = (loc < cap).astype(xt.dtype)
            loc_c = jnp.clip(loc, 0, cap - 1)
            contrib = (xt[:, None, :] * valid[:, :, None]).reshape(T * K, Dd)
            disp = jnp.zeros((E, cap, Dd), xt.dtype)
            disp = disp.at[idx_k.reshape(-1), loc_c.reshape(-1)].add(contrib)
            h = jax.nn.relu(jnp.einsum('ecd,edh->ech', disp, w1) + b1[:, None, :])
            out = jnp.einsum('ech,ehd->ecd', h, w2) + b2[:, None, :]
            gathered = out[idx_k, loc_c]
            y = jnp.einsum('tk,tkd->td', gates_k * valid, gathered)
            return y.reshape(Bb, Ss, Dd)
        return _moe_forward(x, wg, w1, b1, w2, b2)

    def _L1_attn_ref(x, Wq, Wk, Wv, Wo, Wf1, Wf2, Wg1, Wg2, norm_weight):
        import jax, jax.numpy as jnp
        import numpy as np
        B, N, E, H = (2, 256, 128, 16)
        D = E // H
        EPS = 1e-05
        SCALE = D ** (-0.5)
        STD = 0.02
        b, n, e = x.shape
        q = jax.nn.silu(x @ Wq).reshape(b, n, H, D)
        k = jax.nn.silu(x @ Wk).reshape(b, n, H, D)
        v = (x @ Wv).reshape(b, n, H, D)
        f = jax.nn.sigmoid(x @ Wf1 @ Wf2).reshape(b, n, H, D)

        def step(S, qkvf):
            qt, kt, vt, ft = qkvf
            S = ft[..., :, None] * S + kt[..., :, None] * vt[..., None, :]
            ot = jnp.einsum('bhk,bhkv->bhv', qt, S)
            return (S, ot)
        S0 = jnp.zeros((b, H, D, D), x.dtype)
        xs = (jnp.moveaxis(q, 1, 0) * SCALE, jnp.moveaxis(k, 1, 0), jnp.moveaxis(v, 1, 0), jnp.moveaxis(f, 1, 0))
        _, o = jax.lax.scan(step, S0, xs)
        o = jnp.moveaxis(o, 0, 1).reshape(b, n, e)
        g = jax.nn.sigmoid(x @ Wg1 @ Wg2)
        og = (o * g).reshape(b, n, H, D)
        og = og * jax.lax.rsqrt(jnp.mean(og * og, axis=-1, keepdims=True) + EPS)
        o = og.reshape(b, n, e) * norm_weight
        return o @ Wo

    def _L1_ffn_ref(x, phi_w, phi_b, expert_w, expert_b):
        import jax, jax.numpy as jnp
        import numpy as np
        T, Z, D_DIM = (8, 256, 128)
        N_EXP, P_SLOT, H = (64, 32, 128)
        LN_EPS = 1e-05
        t, z, d = x.shape
        n = expert_w.shape[0]
        p = phi_w.shape[0] // n
        logits = (jnp.einsum('tzd,ed->tze', x, phi_w) + phi_b).reshape(t, z, n, p)
        D = jax.nn.softmax(logits, axis=3)
        C = jax.nn.softmax(logits, axis=2)
        X_tilde = jnp.einsum('tznp,tzd->npd', D, x)
        X_tilde = jnp.clip(X_tilde, -33000.0, 65000.0)
        mu = jnp.mean(X_tilde, axis=-1, keepdims=True)
        var = jnp.mean(jnp.square(X_tilde - mu), axis=-1, keepdims=True)
        X_tilde = (X_tilde - mu) * jax.lax.rsqrt(var + LN_EPS)
        X_tilde = jnp.tanh(X_tilde)
        Y_tilde = jnp.einsum('npd,ndH->npH', X_tilde, expert_w) + expert_b[:, None, :]
        Y = jnp.einsum('tznp,npH->tzH', C, Y_tilde)
        return Y
    x = L0_attn_x
    x = x + 0.5 * _L0_ffn_ref(_layernorm(x, axis=-1), L0_ffn_wg, L0_ffn_w1, L0_ffn_b1, L0_ffn_w2, L0_ffn_b2)
    x = x + _L0_attn_ref(_layernorm(x, axis=-1), L0_attn_W_in, L0_attn_conv_w, L0_attn_conv_b, L0_attn_W_xproj, L0_attn_W_dt, L0_attn_b_dt, L0_attn_A_log, L0_attn_D, L0_attn_W_out)
    x = x + 0.5 * _L0_ffn_ref(_layernorm(x, axis=-1), L0_ffn_wg, L0_ffn_w1, L0_ffn_b1, L0_ffn_w2, L0_ffn_b2)
    x = x + 0.5 * _L1_ffn_ref(_layernorm(x, axis=-1), L1_ffn_phi_w, L1_ffn_phi_b, L1_ffn_expert_w, L1_ffn_expert_b)
    x = x + _L1_attn_ref(_layernorm(x, axis=-1), L1_attn_Wq, L1_attn_Wk, L1_attn_Wv, L1_attn_Wo, L1_attn_Wf1, L1_attn_Wf2, L1_attn_Wg1, L1_attn_Wg2, L1_attn_norm_weight)
    x = x + 0.5 * _L1_ffn_ref(_layernorm(x, axis=-1), L1_ffn_phi_w, L1_ffn_phi_b, L1_ffn_expert_w, L1_ffn_expert_b)
    return x

_drawn_inputs = setup_inputs


def setup_inputs(seed=0):
    import zlib

    import numpy as np

    out = dict(_drawn_inputs(seed))
    spreads = {'L0_attn_conv_b': (0.0, 0.1),
     'L0_attn_D': (1.0, 0.2),
     'L0_ffn_b1': (0.0, 0.1),
     'L0_ffn_b2': (0.0, 0.1),
     'L1_attn_norm_weight': (1.0, 0.2)}
    factors = {}
    for name, (base, spread) in spreads.items():
        noise = np.random.default_rng([zlib.crc32(name.encode()), seed]).standard_normal(out[name].shape)
        drawn = base * np.exp(spread * noise) if base else spread * noise
        out[name] = jnp.asarray(drawn.astype(out[name].dtype))
    for name, factor in factors.items():
        out[name] = (out[name] * factor).astype(out[name].dtype)
    return out
```

```python
from contextlib import ExitStack

import numpy as np

import concourse.bass as bass
from concourse import mybir

F32 = mybir.dt.float32
BF16 = mybir.dt.bfloat16
U32 = mybir.dt.uint32
ALU = mybir.AluOpType
ACT = mybir.ActivationFunctionType
AX = mybir.AxisListType.X

P = 128
CHUNK = 512
EPS = 1e-5
LOWEST = -3.0e38

BATCH, TIME, D = 4, 1024, 128
TOKENS = BATCH * TIME
TILES = TOKENS // P
PER_BATCH = TIME // P
HALVES = TIME // CHUNK
CHUNKS = TOKENS // CHUNK
PER_CHUNK = CHUNK // P
E, K, H = 8, 2, 512
HB = H // P
CAP = K * (TOKENS // E)
SLOTS = E * CAP
EC = CAP // CHUNK
FAR = float(1 << 20)
DI, DS, DCONV, RANK = 256, 16, 4, 8
DT = DI // P
CONV_PAD = DCONV - 1
HEADS, HD = 16, 8
NEXP, PSLOT = 64, 32
SOFT = NEXP * PSLOT
ST = SOFT // P
EPT = P // PSLOT
NH = NEXP // 2
UNITS = 2 * TILES
RING = 4
HW = SOFT // 2
GROUP = 4
ENGINES = 5
KEPT = (0, 2, 3, 5)


def build(nc, a, out, disp, yexp):
    with ExitStack() as ctx:
        def sb(name, shape, dt=F32):
            return ctx.enter_context(nc.sbuf_tensor(name, shape, dt))

        sems = {}

        def sem(name):
            if name not in sems:
                sems[name] = ctx.enter_context(nc.semaphore(name))
            return sems[name]

        def ds(start, size):
            return bass.ds(start, size)

        def repeat(eng, n, body):
            body(0, True)
            with eng.Fori(1, n) as i:
                body(i, False)

        X = sb("X", [P, TILES, D])
        XN = sb("XN", [P, TILES, D])
        XT = sb("XT", [P, BATCH, CONV_PAD + TIME])
        ps = ctx.enter_context(nc.psum_tensor("ps", [P, 8, CHUNK], F32))

        loads = [[], []]

        def resident(name, shape, src, dt=F32):
            t = sb("c_" + name, shape, dt)
            full = t[tuple(slice(None) for _ in shape)]
            loads[name not in ("ident", "rev", "wg")].append((full, src))
            return t

        ident = resident("ident", [P, P], a["k_ident"])
        rev = resident("rev", [P, E], a["k_rev"])
        wg = resident("wg", [P, E], a["L0_ffn_wg"])
        b1 = resident("b1", [P, E, HB], a["h_b1"])
        b2 = resident("b2", [P, E, D], a["L0_ffn_b2"].partition_broadcast(P))
        W_in = resident("W_in", [P, 2 * DI], a["L0_attn_W_in"])
        conv_w = resident("conv_w", [P, DT, DCONV], a["L0_attn_conv_w"].rearrange("(k p) n -> p k n", p=P))
        conv_b = resident("conv_b", [P, DT], a["h_conv_b"])
        W_x = resident("W_x", [P, DT, RANK + 2 * DS], a["L0_attn_W_xproj"].rearrange("(k p) n -> p k n", p=P))
        W_dt = resident("W_dt", [RANK, DI], a["L0_attn_W_dt"])
        b_dt = resident("b_dt", [P, DT], a["h_b_dt"])
        A_log = resident("A_log", [P, DT, DS], a["L0_attn_A_log"].rearrange("(k p) n -> p k n", p=P))
        D_skip = resident("D_skip", [P, DT], a["h_D"])
        W_out = resident("W_out", [P, DT, D], a["L0_attn_W_out"].rearrange("(k p) n -> p k n", p=P))
        phiT = resident("phiT", [P, SOFT], a["h_phi_wT"])
        phi_bc = resident("phi_bc", [P, ST], a["h_phi_b"])
        same_p = resident("same_p", [P, P], a["k_same_p"])
        Wq = resident("Wq", [P, D], a["L1_attn_Wq"])
        Wk = resident("Wk", [P, D], a["L1_attn_Wk"])
        Wv = resident("Wv", [P, D], a["L1_attn_Wv"])
        Wo = resident("Wo", [P, D], a["L1_attn_Wo"])
        Wf1 = resident("Wf1", [P, HD], a["L1_attn_Wf1"])
        Wg1 = resident("Wg1", [P, HD], a["L1_attn_Wg1"])
        Wf2 = resident("Wf2", [HD, D], a["L1_attn_Wf2"])
        Wg2 = resident("Wg2", [HD, D], a["L1_attn_Wg2"])
        norm_w = resident("norm_w", [P, 1], a["h_norm_w"])
        head_mean = resident("head_mean", [P, P], a["k_head_mean"])

        tri = sb("tri", [P, P], BF16)
        identb = sb("identb", [P, P], BF16)
        row32 = sb("row32", [96, 32], BF16)
        onesb = sb("onesb", [P, P], BF16)
        mean_w = sb("mean_w", [P, P])
        ones64 = sb("ones64", [P, K * TILES])
        eps = sb("eps", [P, 1])
        W_bc3 = sb("W_bc3", [P, DT, 96 + RANK])
        A_neg = sb("A_neg", [P, DT, DS])
        phi_b3 = sb("phi_b3", [3, SOFT], BF16)
        row128 = sb("row128", [64, P], BF16)

        stats = sb("stats", [P, TILES, 6])
        ln_s = sb("ln_s", [P, 9, TILES])
        stage = sb("stage", [P, HALVES, CHUNK])

        ARENA = 120 * 256
        arena = sb("arena", [P, ARENA])

        class Cut:
            def __init__(self):
                self.at = 0

            def __call__(self, shape, dt=F32):
                n = int(np.prod(shape))
                words = n if dt != BF16 else (n + 1) // 2
                words = (words + 7) // 8 * 8
                assert self.at + words <= ARENA, (self.at + words, ARENA)
                t = arena[:, self.at:self.at + words]
                self.at += words
                if dt != F32:
                    t = t.bitcast(dt)
                t = t[:, 0:n]
                if len(shape) == 2:
                    t = t.rearrange("p (a b) -> p a b", b=shape[1])
                if len(shape) == 3:
                    t = t.rearrange("p (a b c) -> p a b c", b=shape[1], c=shape[2])
                return t

        cut = Cut()
        cut.at = ARENA - 9 * SOFT // 2 - 3 * D
        setup_at = cut.at
        zero = cut([D])
        phi_b3f, row, rest, acc = (cut([SOFT])[0:3, :] for _ in range(4))
        part = cut([SOFT], BF16)[0:3, :]
        tri_f = cut([P])
        row32_f = cut([32])[0:96, :]
        loads[0].append((tri_f, a["k_tri"]))
        loads[1].append((row32_f, a["k_row32"]))
        loads[1].append((phi_b3f, a["L1_ffn_phi_b"].partition_broadcast(3)))

        cut = Cut()
        w1s = cut([2, H])
        w2s = cut([2, HB, D])
        dtile = cut([EC, PER_CHUNK, D])
        dT = cut([EC, CHUNK])
        hT = cut([EC, HB, CHUNK])
        yo = cut([EC, PER_CHUNK, D])
        yg = cut([TILES, K, D])
        g8 = [cut([TILES, E]) for _ in range(3)]
        g1 = [cut([TILES]) for _ in range(10)]
        mask = cut([K, TILES * E], BF16)
        run = [cut([K * TILES * E]) for _ in range(3)]
        g64 = [cut([K * TILES]) for _ in range(8)]
        gate = cut([K, TILES])
        rank = cut([K, TILES])
        put_at = cut([K * TILES], U32)
        get_at = cut([K * TILES], U32)
        assert cut.at <= setup_at, (cut.at, setup_at)

        cut = Cut()
        uc = cut([DT, BATCH, TIME])
        zs = cut([DT, BATCH, TIME])
        delta = XN[:, :, :].rearrange("p a b -> p (a b)")
        delta2 = cut([BATCH * TIME])
        BCs = cut([TOKENS], BF16)
        pre = cut.at
        bcf = [cut([CHUNK]) for _ in range(2)]
        bch = cut([CHUNK], BF16)
        bcm = cut([CHUNK], BF16)
        dts = cut([BATCH, TIME])
        sp = [cut([CHUNK]) for _ in range(4)]
        assert cut.at <= ARENA
        u_pad = delta[:, 0:DT * (CONV_PAD + TIME)].rearrange("p (d t) -> p d t", d=DT)
        cacc = delta[:, 2560:2560 + DT * CHUNK].rearrange("p (d t) -> p d t", d=DT)
        cut.at = pre
        dtu = XT[:, 0:DT, CONV_PAD:]
        Bs = XT[:, DT:DT + 2, CONV_PAD:]
        Cs = cut([2, TIME])
        NW = 4
        dA = cut([DT, TIME])
        w = cut([NW, TIME])
        dlt = [delta, delta2]

        cut = Cut()
        q_s = cut([BATCH, TIME])
        k_s = cut([BATCH, TIME])
        f_s = cut([BATCH, TIME])
        g_s = cut([BATCH, TIME])
        og = cut([BATCH, TIME])
        sg = cut([2, CHUNK])
        low = cut([2, CHUNK])
        sq, rms = sg, low
        kv = cut([NW, TIME])
        nrm = cut([2, CHUNK])
        head_sum = cut([HD, P])
        Wvv = cut([HD, P])

        cut = Cut()
        We = cut([NEXP, D])
        Yt = cut([ST, D])
        mCT = cut([TOKENS], BF16)
        lnz = cut([CHUNK])
        yT = cut([CHUNK])
        combine_at = cut.at
        eb = cut([ST, D])
        mxC = cut([2, TILES, PSLOT])
        ring_at = cut.at
        mCs = cut([TILES, 2 * PSLOT], BF16)
        slotX = cut([SOFT])
        slotA = cut([SOFT])
        slotB = cut([SOFT])
        cut.at = NEXP * D
        Lc = cut([RING, HW])
        xts = cut([2, P])
        xns = cut([2, P])
        assert cut.at <= combine_at
        cut.at = ring_at
        Ed = cut([RING, HW])
        Dd = cut([RING, HW])
        mD = cut([RING, NH])
        sD = cut([RING, NH])
        rD = cut([RING, NH])
        cut.at = combine_at
        Ec = cut([2, ST, CHUNK])
        flat = arena[:, 0:NEXP * D]
        t8 = flat[:, 0:4096].rearrange("p (a b) -> p a b", b=CHUNK)
        t4 = flat[:, 4096:6144].rearrange("p (a b) -> p a b", b=CHUNK)
        t2 = flat[:, 6144:7168].rearrange("p (a b) -> p a b", b=CHUNK)
        t1 = flat[:, 7168:7680]
        Rz = flat[:, 7680:8192]

        def pbank(i, n=1):
            return ps[:, i, :] if n == 1 else ps[:, i:i + n, :].rearrange("p a b -> p (a b)")

        def over(t, n):
            return t.unsqueeze(2).to_broadcast([t.shape[0], t.shape[1], n])

        def below(i, n):
            return isinstance(i, int) and i < n

        def dispatch_loop(eng, units):
            units(0)
            units(1)
            with eng.Fori(2, UNITS // RING - 1) as i:
                units(i)
            units(UNITS // RING - 1)

        def stage_end(eng, k):
            eng.drain().then_inc(sem("stage"), 1)
            eng.wait_ge(sem("stage"), ENGINES * (k + 1))

        def hold(eng, s, value):
            eng.wait_ge(s, value)
            if not isinstance(value, int):
                eng.nop(nofuse=True)

        class Chain:

            def __init__(self, eng, name):
                self.eng, self.sem, self.n = eng, sem(name), 0

            def __call__(self, ins):
                self.n += 1
                ins.then_inc(self.sem, 1)
                self.eng.wait_ge(self.sem, self.n)

        block = ctx.enter_context(nc.Block())

        @block.sync
        def _(sp_):
            for b in range(BATCH):
                sp_.dma_start(X[:, PER_BATCH * b:PER_BATCH * (b + 1), :],
                              a["L0_attn_x"][b].rearrange("(j p) d -> p j d", p=P)).then_inc(sem(f"x_in{b}"), 16)
            for dst, src in loads[0]:
                sp_.dma_start(dst, src).then_inc(sem("consts0"), 16)
            sp_.wait_ge(sem("zeroed"), 1)
            sp_.dma_start(disp.rearrange("(p a) d -> p a d", p=P), zero.unsqueeze(1).to_broadcast([P, SLOTS // P, D]))\
                .then_inc(sem("disp_zero"), 16)
            for dst, src in loads[1]:
                sp_.dma_start(dst, src).then_inc(sem("consts1"), 16)
            stage_end(sp_, 0)

            def experts(m, k):
                dsp = disp.rearrange("(e c j p) d -> p (e c) j d", c=EC, j=PER_CHUNK, p=P)

                def weights(e, b):
                    sp_.dma_start(w1s[:, b, :], a["L0_ffn_w1"][ds(e, 1), :, :].rearrange("a d h -> (a d) h"))\
                        .then_inc(sem(f"w_in{b}"), 16)
                    sp_.dma_start(w2s[:, b, :, :], a["L0_ffn_w2"][ds(e, 1), :, :].rearrange("a (k p) d -> p (a k) d", p=P))\
                        .then_inc(sem(f"w_in{b}"), 16)

                weights(0, 0)
                weights(1, 1)
                for q in range(K):
                    sp_.wait_ge(sem(f"put{q}"), 16 * TILES * (m + 1))

                def pair(i, first, last=False):
                    for p in range(2):
                        for c in range(EC):
                            if not (first and p == 0):
                                sp_.wait_ge(sem("d_T"), 16 * m + 4 * i + 2 * p + c - 1)
                            sp_.dma_start(dtile[:, c, :, :], dsp[:, ds(4 * i + 2 * p + c, 1), :, :].rearrange("p a j d -> p (a j) d"))\
                                .then_inc(sem(f"d_in{c}"), 16)
                        if not (first and p == 0) and not (last and p == 1):
                            sp_.wait_ge(sem("l2"), 16 * m + 4 * i + 2 * p)
                            weights(2 * i + p + 1, 1 - p)

                pair(0, True)
                with sp_.Fori(1, E // 2 - 1) as i:
                    pair(i, False)
                pair(E // 2 - 1, False, True)
                stage_end(sp_, k + 1)

            experts(0, 0)
            stage_end(sp_, 2)
            experts(1, 2)

            def soft(k):
                sp_.dma_start(We, a["L1_ffn_expert_w"].rearrange("n d h -> d n h")).then_inc(sem("we"), 16)
                ebs = a["L1_ffn_expert_b"].rearrange("(s j) h -> j s h", j=EPT)
                for j in range(EPT):
                    sp_.dma_start(eb[PSLOT * j:PSLOT * (j + 1), :, :], ebs[j].partition_broadcast(PSLOT))\
                        .then_inc(sem("we"), 16)
                stage_end(sp_, k + 1)
                stage_end(sp_, k + 2)

            soft(3)
            sp_.dma_start(head_sum, a["k_head_sum"]).then_inc(sem("head_sum"), 16)
            stage_end(sp_, 6)
            soft(6)
            sp_.dma_start(out.rearrange("b (j p) d -> p (b j) d", p=P), X[:, :, :]).then_inc(sem("x_out"), 16)
            sp_.wait_ge(sem("x_out"), 16)

        @block.gpsimd
        def _(pool):
            pool.memset(onesb[:, :], 1.0).then_inc(sem("ones"), 1)
            pool.memset(mean_w[:, :], 1.0 / P).then_inc(sem("ones"), 1)
            pool.memset(ones64[:, :], 1.0).then_inc(sem("ones"), 1)
            pool.memset(eps[:, :], EPS).then_inc(sem("ones"), 1)
            stage_end(pool, 0)

            def experts(m, k):
                hold(pool, sem("slots"), m + 1)
                if m == 0:
                    pool.wait_ge(sem("disp_zero"), 16)
                for q in range(K):
                    for t in range(TILES):
                        pool.indirect_dma_start(
                            disp, bass.IndirectOffsetOnAxis(ap=put_at[:, q * TILES + t:q * TILES + t + 1], axis=0),
                            XN[:, t, :], None, bounds_check=SLOTS - 1, oob_is_err=False)\
                            .then_inc(sem(f"put{q}"), 16)
                yv = yexp.rearrange("(e j p) d -> p e j d", j=PER_CHUNK, p=P)

                def store(i, first):
                    for c in range(EC):
                        hold(pool, sem("y_out"), 16 * m + EC * i + c + 1)
                        pool.dma_start(yv[:, ds(EC * i + c, 1), :, :].rearrange("p a j d -> p (a j) d"), yo[:, c, :, :])\
                            .then_inc(sem(f"y_st{c}"), 16)

                repeat(pool, E, store)
                for c in range(EC):
                    hold(pool, sem(f"y_st{c}"), 16 * E * (m + 1))
                for t in range(TILES):
                    for q in range(K):
                        pool.indirect_dma_start(
                            yg[:, t, q, :], None, yexp,
                            bass.IndirectOffsetOnAxis(ap=get_at[:, q * TILES + t:q * TILES + t + 1], axis=0))\
                            .then_inc(sem(f"got{t // GROUP}"), 16)
                stage_end(pool, k + 1)

            experts(0, 0)

            def mamba(b, first):
                for n in range(DS):
                    for d in range(DT):
                        u = DT * n + d
                        if n == 0 and d == 0:
                            hold(pool, sem("dtu"), b + 1)
                        hold(pool, sem("Bs"), DS * b + n + 1)
                        if not (first and u < NW):
                            hold(pool, sem("ysum"), 32 * b + u + 1 - NW)
                        pool.tensor_tensor(w[:, u % NW, :], dtu[:, d, :], Bs[:, n % 2, :], ALU.mult)\
                            .then_inc(sem("dBu"), 1)

            repeat(pool, BATCH, mamba)
            stage_end(pool, 2)
            experts(1, 2)

            def soft(s, k):
                base = UNITS * s

                def normalise(u, r):
                    hold(pool, sem("rD"), u + 1)
                    if not below(u, RING):
                        hold(pool, sem("slotX"), u + 1 - RING)
                    pool.tensor_tensor(Dd[:, r, :].rearrange("p (n q) -> p n q", q=PSLOT),
                                       Ed[:, r, :].rearrange("p (n q) -> p n q", q=PSLOT),
                                       over(rD[:, r, :], PSLOT), ALU.mult).then_inc(sem("Dd"), 1)

                def shift(u, r):
                    hold(pool, sem("mD"), u + 1)
                    if not below(u, RING):
                        hold(pool, sem("Dd"), u + 1 - RING)
                    pool.tensor_tensor(Ed[:, r, :].rearrange("p (n q) -> p n q", q=PSLOT),
                                       Lc[:, r, :].rearrange("p (n q) -> p n q", q=PSLOT),
                                       over(mD[:, r, :], PSLOT), ALU.subtract).then_inc(sem("Es"), 1)

                def units(i):
                    for r in range(RING):
                        u = base + RING * i + r
                        shift(u, r)
                        if not below(RING * i + r, 2):
                            normalise(u - 2, (r - 2) % RING)

                dispatch_loop(pool, units)
                for r in (2, 3):
                    normalise(base + UNITS - RING + r, r)
                stage_end(pool, k + 1)
                stage_end(pool, k + 2)

            soft(0, 3)

            def gla(b, first):
                for v in range(HD):
                    hold(pool, sem("kv_scan"), HD * b + v + 1)
                    pool.tensor_tensor(kv[:, v % NW, :], q_s[:, ds(b, 1), :].rearrange("p a t -> p (a t)"), kv[:, v % NW, :],
                                       ALU.mult).then_inc(sem("qS"), 1)

            repeat(pool, BATCH, gla)
            stage_end(pool, 6)
            soft(1, 6)

        @block.scalar
        def _(act):
            chain = Chain(act, "act_chain")
            act.preload_act_table_set("natural_log_exp_and_others")

            def ln_scale(n, c):
                hold(act, sem("ln_var"), 8 * n + c + 1)
                act.activation(ln_s[:, 6, ds(4 * c, 4)], ln_s[:, 5, ds(4 * c, 4)], ACT.Ln).then_inc(sem("ln_ln"), 1)
                hold(act, sem("ln_ln"), 8 * n + c + 1)
                act.activation(ln_s[:, 7, ds(4 * c, 4)], ln_s[:, 6, ds(4 * c, 4)], ACT.Exp, scale=-0.5)\
                    .then_inc(sem("ln_rstd"), 1)

            def ln_copies(n, b, h, bank):
                c = 2 * b + h
                if n in KEPT:
                    hold(act, sem("ln_x"), 8 * n + c + 1)
                    act.activation(XN[:, ds(4 * c, 4), :], stage[:, h, :].rearrange("p (j d) -> p j d", d=D),
                                   ACT.Copy).then_inc(sem("ln_keep"), 1)
                hold(act, sem("ln_T"), 8 * n + c + 1)
                act.activation(XT[:, ds(b, 1), CONV_PAD + CHUNK * h:CONV_PAD + CHUNK * (h + 1)].rearrange("p a t -> p (a t)"),
                               pbank(bank), ACT.Copy).then_inc(sem("ln_XT"), 1)

            for c in range(CHUNKS):
                ln_scale(0, c)
                if c:
                    ln_copies(0, (c - 1) // 2, (c - 1) % 2, 0)
            ln_copies(0, BATCH - 1, 1, 0)
            stage_end(act, 0)

            def experts(m, k):
                hold(act, sem("g_diff"), m + 1)
                act.activation(g1[5], g1[4], ACT.Exp).then_inc(sem("g_exp"), 1)
                if m == 0:
                    act.wait_ge(sem("consts1"), 16 * len(loads[1]))
                    chain(act.activation(A_neg[:, :, :], A_log[:, :, :], ACT.Exp))
                    chain(act.activation(A_neg[:, :, :], A_neg[:, :, :], ACT.Copy, scale=-1.0))

                def evac_T(v, c):
                    hold(act, sem("d_T"), v + 1)
                    act.activation(dT[:, c, :], pbank(c), ACT.Copy).then_inc(sem("dT"), 1)

                base = 16 * m
                evac_T(base, 0)

                def chunks(i, first, last=False):
                    for p in range(2):
                        for c in range(EC):
                            v = base + 4 * i + 2 * p + c
                            for hb in (0, 2):
                                hold(act, sem(f"l1_{hb}"), v + 1)
                                act.activation(hT[:, c, hb, :], pbank(2 + hb), ACT.Relu,
                                               bias=b1[:, ds(2 * i + p, 1), hb:hb + 1].rearrange("p a b -> p (a b)"))\
                                    .then_inc(sem("hT_act"), 1)
                            if not (last and p == 1 and c == EC - 1):
                                evac_T(v + 1, 1 - c)

                chunks(0, True)
                with act.Fori(1, E // 2 - 1) as i:
                    chunks(i, False)
                chunks(E // 2 - 1, False, True)
                n = 2 * m + 1
                for c in range(CHUNKS):
                    ln_scale(n, c)
                    ln_copies(n, c // 2, c % 2, 0)
                stage_end(act, k + 1)

            experts(0, 0)

            act.preload_act_table(ACT.Silu)

            def project(b, first):
                for h in range(HALVES):
                    v = 2 * b + h
                    for d in range(DT):
                        hold(act, sem("u_ps"), DT * v + d + 1)
                        if h == 0 and not first:
                            hold(act, sem("conv"), DT * v)
                        act.activation(u_pad[:, d, CONV_PAD + CHUNK * h:CONV_PAD + CHUNK * (h + 1)], pbank(d), ACT.Copy)\
                            .then_inc(sem("u_sb"), 1)
                    for d in range(DT):
                        hold(act, sem("z_ps"), DT * v + d + 1)
                        act.activation(zs[:, d, ds(b, 1), CHUNK * h:CHUNK * (h + 1)].rearrange("p a t -> p (a t)"),
                                       pbank(2 + d), ACT.Silu).then_inc(sem("zs"), 1)
                    for d in range(DT):
                        hold(act, sem("conv"), DT * v + d + 1)
                        act.activation(uc[:, d, ds(b, 1), CHUNK * h:CHUNK * (h + 1)].rearrange("p a t -> p (a t)"), cacc[:, d, :],
                                       ACT.Silu, bias=conv_b[:, d:d + 1]).then_inc(sem("uc"), 1)
                    hold(act, sem("bc_done"), v + 1)
                    act.activation(dts[0:RANK, ds(b, 1), CHUNK * h:CHUNK * (h + 1)].rearrange("p a t -> p (a t)"),
                                   pbank(6)[96:96 + RANK, :], ACT.Copy).then_inc(sem("dts"), 1)

            repeat(act, BATCH, project)
            act.preload_act_table_set("natural_log_exp_and_others")

            def softplus(b, first):
                for h in range(HALVES):
                    v = 2 * b + h
                    for d in range(DT):
                        n = DT * v + d
                        if not (first and h == 0):
                            hold(act, sem("delta"), n - 1)
                        hold(act, sem("x_ps"), n + 1)
                        act.activation(sp[d], pbank(4 + d), ACT.Abs, bias=b_dt[:, d:d + 1]).then_inc(sem("sp1"), 1)
                    for d in range(DT):
                        n = DT * v + d
                        hold(act, sem("sp1"), n + 1)
                        act.activation(sp[d], sp[d], ACT.Exp, scale=-1.0).then_inc(sem("sp2"), 1)
                    for d in range(DT):
                        n = DT * v + d
                        hold(act, sem("sp2"), n + 1)
                        act.activation(sp[d], sp[d], ACT.Ln, bias=1.0).then_inc(sem("sp3"), 1)

            repeat(act, BATCH, softplus)
            hold(act, sem("pre_all"), 1)

            def scan_in(b, first):
                for n in range(DS):
                    v = DS * b + n
                    hold(act, sem("bc"), v + 1)
                    if not (first and n < 2):
                        hold(act, sem("dBu"), DT * (v - 1))
                    act.activation(Bs[:, n % 2, :], pbank(0, 2), ACT.Copy).then_inc(sem("Bs"), 1)
                    if not (first and n < 2):
                        hold(act, sem("hC"), DT * (v - 1))
                    act.activation(Cs[:, n % 2, :], pbank(2, 2), ACT.Copy).then_inc(sem("Cs"), 1)
                    for d in range(DT):
                        if not (first and n == 0):
                            hold(act, sem("scan"), DT * (v - 1) + d + 1)
                        act.activation(dA[:, d, :], dlt[d][:, ds(b * TIME, TIME)], ACT.Exp, scale=A_neg[:, d, n:n + 1])\
                            .then_inc(sem("dA"), 1)

            repeat(act, BATCH, scan_in)
            for c in range(CHUNKS):
                ln_scale(2, c)
                ln_copies(2, c // 2, c % 2, 7)
            stage_end(act, 2)

            experts(1, 2)

            def soft(s, k):
                base = UNITS * s

                def copy_xt(t, r):
                    if not below(t, 2):
                        hold(act, sem("L"), base + 2 * t - 2)
                    act.activation(xts[:, r, :], XT[:, ds(t // PER_BATCH, 1), ds(CONV_PAD + (P * t) % TIME, P)]
                                   .rearrange("p a t -> p (a t)"), ACT.Copy).then_inc(sem("xts"), 1)

                def copy_xn(t, r):
                    if not below(t, 2):
                        hold(act, sem("slotX"), base + 2 * t - 2)
                    act.activation(xns[:, r, :], XN[:, ds(t, 1), :].rearrange("p a d -> p (a d)"),
                                   ACT.Copy).then_inc(sem("xns"), 1)

                def copy_L(u, r):
                    hold(act, sem("L"), base + u + 1)
                    if not below(u, RING):
                        hold(act, sem("Es"), base + u + 1 - RING)
                        hold(act, sem("mxC"), base + u + 1 - RING)
                    act.activation(Lc[:, r, :], pbank(2 * (r % 2), 2), ACT.Copy).then_inc(sem("Lc"), 1)

                def units(i):
                    last = isinstance(i, int) and i == UNITS // RING - 1
                    for r in range(RING):
                        u = RING * i + r
                        if not (last and r == RING - 1):
                            copy_L(u + 1, (r + 1) % RING)
                        if r % 2 == 0:
                            if not last:
                                copy_xt(2 * i + 2 + r // 2, r // 2)
                            if not below(u, 1):
                                copy_xn(2 * i - 1 + r // 2, 1 - r // 2)
                        hold(act, sem("Es"), base + u + 1)
                        act.activation(Ed[:, r, :], Ed[:, r, :], ACT.Exp).then_inc(sem("Ed"), 1)

                copy_xt(0, 0)
                copy_xt(1, 1)
                copy_L(0, 0)
                dispatch_loop(act, units)
                copy_xn(TILES - 1, 1)
                for g in range(4):
                    hold(act, sem("mCT_ps"), 4 * s + g + 1)
                    act.activation(mCT[0:64, 1024 * g:1024 * (g + 1)], pbank(g % 2).bitcast(BF16)[0:64, :], ACT.Copy)\
                        .then_inc(sem("mCT"), 1)
                for h in range(2):
                    hold(act, sem("slot_c"), 2 * s + h + 1)
                    act.activation(slotB[:, 1024 * h:1024 * (h + 1)], slotA[:, 1024 * h:1024 * (h + 1)], ACT.Square)\
                        .then_inc(sem("slot_sq"), 1)
                for h in range(2):
                    hold(act, sem("slot_v"), 2 * s + h + 1)
                    chain(act.activation(slotB[:, 1024 * h:1024 * (h + 1)], pbank(4 + 2 * h, 2), ACT.Ln, bias=eps[:, :]))
                    act.activation(slotB[:, 1024 * h:1024 * (h + 1)], slotB[:, 1024 * h:1024 * (h + 1)], ACT.Exp,
                                   scale=-0.5).then_inc(sem("slot_r"), 1)
                for h in range(2):
                    hold(act, sem("slot_n"), 2 * s + h + 1)
                    act.activation(slotA[:, 1024 * h:1024 * (h + 1)], slotA[:, 1024 * h:1024 * (h + 1)], ACT.Tanh)\
                        .then_inc(sem("slot_t"), 1)
                stage_end(act, k + 1)
                act.preload_act_table_set("natural_log_exp_and_others")

                def exp_T(v, c, first, before=None):
                    for t in range(ST):
                        if before and t == ST // 2:
                            ln_scale(4, 2 * before[0] + before[1])
                        hold(act, sem("LT"), ST * v + t + 1)
                        if t == 0 and not first:
                            hold(act, sem("yT_ps"), v - 1)
                        act.activation(Ec[:, c, t, :], pbank(t % 4), ACT.Exp, bias=phi_bc[:, t:t + 1])\
                            .then_inc(sem("Ec"), 1)

                def finish(v):
                    hold(act, sem("Z"), v + 1)
                    act.activation(lnz, pbank(4), ACT.Ln).then_inc(sem("lnz"), 1)
                    hold(act, sem("lnz"), v + 1)
                    act.activation(Rz, lnz, ACT.Exp, scale=-1.0).then_inc(sem("Rz"), 1)

                def copy_y(v):
                    hold(act, sem("yT_ps"), v + 1)
                    act.activation(yT, pbank(5), ACT.Copy).then_inc(sem("yT"), 1)

                base = CHUNKS * s
                exp_T(base, 0, True)
                finish(base)
                exp_T(base + 1, 1, True)
                copy_y(base)
                finish(base + 1)

                with act.Fori(1, CHUNKS // 2) as i:
                    for c in range(2):
                        v = base + 2 * i + c
                        exp_T(v, c, False, (i - 1, c) if s == 0 else None)
                        if s == 0:
                            ln_copies(4, i - 1, c, 7)
                        copy_y(v - 1)
                        finish(v)
                copy_y(base + CHUNKS - 1)
                if s == 0:
                    for c in range(2):
                        ln_scale(4, CHUNKS - 2 + c)
                        ln_copies(4, BATCH - 1, c, 7)
                stage_end(act, k + 2)

            soft(0, 3)

            act.preload_act_table(ACT.Sigmoid)

            def gla_in(b, first):
                for h in range(HALVES):
                    v = 2 * b + h
                    hold(act, sem("low_ps"), v + 1)
                    act.activation(low[0:HD, 0, :], pbank(2)[0:HD, :], ACT.Copy).then_inc(sem("low"), 1)
                    act.activation(low[0:HD, 1, :], pbank(3)[0:HD, :], ACT.Copy).then_inc(sem("low"), 1)
                    for j in range(2):
                        hold(act, sem("qk_ps"), 2 * v + j + 1)
                        if not (first and h == 0):
                            hold(act, sem("qk"), 2 * v + j - 1)
                        act.activation(sg[:, j, :], pbank(j), ACT.Sigmoid).then_inc(sem("qk_sig"), 1)
                    for j, t in enumerate((f_s, g_s)):
                        hold(act, sem("fg_ps"), 2 * v + j + 1)
                        act.activation(t[:, ds(b, 1), CHUNK * h:CHUNK * (h + 1)].rearrange("p a t -> p (a t)"), pbank(4 + j),
                                       ACT.Sigmoid).then_inc(sem("fg"), 1)

            repeat(act, BATCH, gla_in)
            act.preload_act_table_set("natural_log_exp_and_others")

            def square(v, b, h, early):
                if not early:
                    hold(act, sem("ms"), v - 1)
                act.activation(sq[:, h, :], og[:, ds(b, 1), CHUNK * h:CHUNK * (h + 1)].rearrange("p a t -> p (a t)"), ACT.Square)\
                    .then_inc(sem("sq"), 1)

            def head_norm(b, first, last=False):
                for h in range(HALVES):
                    v = 2 * b + h
                    hold(act, sem("ms"), v + 1)
                    act.activation(rms[:, 0, :], pbank(h), ACT.Ln, bias=eps[:, :]).then_inc(sem("rms0"), 1)
                    hold(act, sem("rms0"), v + 1)
                    if not (first and h == 0):
                        hold(act, sem("nrm"), v)
                    act.activation(rms[:, 1, :], rms[:, 0, :], ACT.Exp, scale=-0.5).then_inc(sem("rms"), 1)
                    if not (last and h == 1):
                        square(v + 1, b + h, 1 - h, first and h == 0)
                    if not (first and h == 0):
                        ln_scale(5, v - 1)
                        ln_copies(5, b if h else b - 1, 1 - h, 7)

            hold(act, sem("og"), BATCH)
            square(0, 0, 0, True)
            head_norm(0, True)
            with act.Fori(1, BATCH - 1) as i:
                head_norm(i, False)
            head_norm(BATCH - 1, False, True)
            ln_scale(5, CHUNKS - 1)
            ln_copies(5, BATCH - 1, 1, 7)
            stage_end(act, 6)
            soft(1, 6)

        @block.vector
        def _(dve):
            chain = Chain(dve, "dve_chain")
            dve.memset(zero, 0.0).then_inc(sem("zeroed"), 1)
            chain(dve.memset(XT[:, :, 0:CONV_PAD], 0.0))

            def ln_statistics(n, c):
                v = 8 * n + c
                for j in range(PER_CHUNK):
                    ins = dve.bn_stats(stats[:, ds(4 * c + j, 1), :].rearrange("p a b -> p (a b)"),
                                       X[:, ds(4 * c + j, 1), :].rearrange("p a b -> p (a b)"))
                ins.then_inc(sem("ln_bn"), 1)
                dve.wait_ge(sem("ln_bn"), v + 1)
                even, odd = (lambda j: stats[:, ds(4 * c, 4), j]), (lambda j: stats[:, ds(4 * c, 4), 3 + j])
                two_mean, gap, m2, gap2, var0, var, _, _, mean = (ln_s[:, j, ds(4 * c, 4)] for j in range(9))
                dve.tensor_tensor(two_mean, even(1), odd(1), ALU.add)
                dve.tensor_tensor(gap, even(1), odd(1), ALU.subtract)
                dve.tensor_tensor(m2, even(2), odd(2), ALU.add).then_inc(sem("ln_a"), 1)
                dve.wait_ge(sem("ln_a"), v + 1)
                dve.scalar_tensor_tensor(gap2, gap, 0.25, gap, ALU.mult, ALU.mult)
                dve.tensor_scalar(mean, two_mean, 0.5, None, ALU.mult)
                dve.tensor_scalar(var0, m2, 1.0 / D, EPS, ALU.mult, ALU.add).then_inc(sem("ln_b"), 1)
                dve.wait_ge(sem("ln_b"), v + 1)
                dve.tensor_tensor(var, var0, gap2, ALU.add).then_inc(sem("ln_var"), 1)

            def ln_apply(n, c, h):
                v = 8 * n + c
                dve.wait_ge(sem("ln_rstd"), v + 1)
                if not (isinstance(v, int) and v < 2):
                    dve.wait_ge(sem("ln_T"), v - 1)
                    if n in KEPT and not (isinstance(c, int) and c < 2):
                        dve.wait_ge(sem("ln_keep"), 8 * KEPT.index(n) + c - 1)
                for j in range(PER_CHUNK):
                    t = 4 * c + j
                    ins = dve.tensor_scalar(stage[:, h, D * j:D * (j + 1)], X[:, ds(t, 1), :].rearrange("p a d -> p (a d)"),
                                            ln_s[:, 8, ds(t, 1)], ln_s[:, 7, ds(t, 1)], ALU.subtract, ALU.mult)
                ins.then_inc(sem("ln_x"), 1)

            for c in range(CHUNKS):
                if c % 2 == 0:
                    dve.wait_ge(sem(f"x_in{c // 2}"), 16)
                ln_statistics(0, c)
                if c:
                    ln_apply(0, c - 1, (c - 1) % 2)
            ln_apply(0, CHUNKS - 1, 1)
            dve.wait_ge(sem("consts0"), 16 * len(loads[0]))
            chain(dve.tensor_copy(tri[:, :], tri_f))

            def derive():
                dve.wait_ge(sem("consts1"), 16 * len(loads[1]))
                dve.tensor_copy(W_bc3[:, :, 96:96 + RANK], W_x[:, :, 0:RANK])
                for j in range(3):
                    dve.tensor_copy(W_bc3[:, :, 32 * j:32 * (j + 1)], W_x[:, :, RANK:RANK + 32])
                for dst, src in ((identb, ident[:, :]), (row32, row32_f)):
                    chain(dve.tensor_copy(dst[:, :], src))
                for j in range(EPT):
                    chain(dve.tensor_copy(row128[:, 32 * j:32 * (j + 1)], row32[0:64, :]))
                chain(dve.tensor_copy(rest, phi_b3f))
                for j in range(3):
                    chain(dve.tensor_copy(part, rest))
                    if j == 0:
                        chain(dve.tensor_scalar(acc, part, ident[0:3, 0:1], None, ALU.mult))
                    else:
                        chain(dve.scalar_tensor_tensor(acc, part, ident[0:3, j:j + 1], acc, ALU.mult, ALU.add))
                    if j < 2:
                        chain(dve.tensor_tensor(row, rest, part, ALU.subtract))
                        chain(dve.tensor_copy(rest, row))
                chain(dve.tensor_copy(phi_b3[:, :], acc))

            stage_end(dve, 0)

            def experts(m, k):
                dve.wait_ge(sem("logits"), m + 1)
                lg = pbank(7)[:, 0:TILES * E].rearrange("p (t e) -> p t e", e=E)
                revb = rev[:, :].unsqueeze(1).to_broadcast([P, TILES, E])
                m1, m2, d21, e2, den, gt1, gt2 = g1[0], g1[1], g1[4], g1[5], g1[6], g1[7], g1[8]
                for q, top in enumerate((m1, m2)):
                    src = lg if q == 0 else g8[2]
                    chain(dve.tensor_reduce(top, src, AX, ALU.max))
                    chain(dve.tensor_tensor(g8[0], src, over(top, E), ALU.is_equal))
                    chain(dve.tensor_tensor(g8[1], g8[0], revb, ALU.mult))
                    chain(dve.tensor_reduce(rank[:, q, :], g8[1], AX, ALU.max))
                    chain(dve.tensor_tensor(mask[:, q, :].rearrange("p (t e) -> p t e", e=E), g8[1],
                                            over(rank[:, q, :], E), ALU.is_equal))
                    if q == 0:
                        chain(dve.scalar_tensor_tensor(g8[2], mask[:, 0, :].rearrange("p (t e) -> p t e", e=E), LOWEST, lg,
                                                       ALU.mult, ALU.add))
                dve.nop().then_inc(sem("masks"), 1)
                dve.tensor_tensor(d21, m2, m1, ALU.subtract).then_inc(sem("g_diff"), 1)
                dve.wait_ge(sem("g_exp"), m + 1)
                chain(dve.tensor_scalar(den, e2, 1.0, None, ALU.add))
                chain(dve.reciprocal(gt1, den))
                chain(dve.tensor_tensor(gt2, e2, gt1, ALU.mult))
                dve.wait_ge(sem("counts"), m + 1)
                inside = pbank(5)
                total = pbank(6)
                incl, loc, tmp = run
                tv = total.rearrange("p (t e) -> p t e", e=E)
                iv = incl.rearrange("p (t e) -> p t e", e=E)
                for e in range(E):
                    ins = dve.tensor_tensor_scan(iv[:, :, e], ones64[:, :], tv[:, :, e], 0.0, ALU.mult, ALU.add)
                chain(ins)
                chain(dve.tensor_tensor(tmp, incl, total, ALU.subtract))
                chain(dve.tensor_tensor(loc, tmp, inside, ALU.add))
                chain(dve.tensor_tensor(tmp, loc, mask.rearrange("p a b -> p (a b)"), ALU.mult))
                place, ok, lc, base, slot, far = g64[0:6]
                chain(dve.tensor_reduce(place, tmp.rearrange("p (t e) -> p t e", e=E), AX, ALU.add))
                chain(dve.tensor_scalar(ok, place, CAP + 0.5, None, ALU.is_lt))
                okv = ok.rearrange("p (a b) -> p a b", b=TILES)
                for q, g in enumerate((gt1, gt2)):
                    chain(dve.scalar_tensor_tensor(gate[:, q, :], g, 0.5, okv[:, q, :], ALU.mult, ALU.mult))
                chain(dve.tensor_scalar(lc, place, float(CAP), -1.0, ALU.min, ALU.add))
                chain(dve.tensor_scalar(base, rank.rearrange("p a b -> p (a b)"), -float(CAP), float(SLOTS), ALU.mult, ALU.add))
                chain(dve.tensor_tensor(slot, base, lc, ALU.add))
                chain(dve.tensor_copy(get_at, slot))
                chain(dve.tensor_scalar(far, ok, -FAR, FAR, ALU.mult, ALU.add))
                dve.tensor_tensor(put_at, far, slot, ALU.add).then_inc(sem("slots"), 1)
                if m == 0:
                    derive()

                sbase = 16 * m

                def chunks(i, first):
                    for p in range(2):
                        for c in range(EC):
                            r = 4 * i + 2 * p + c
                            v = sbase + r
                            for hb in (1, 3):
                                dve.wait_ge(sem(f"l1_{hb}"), v + 1)
                                dve.tensor_scalar(hT[:, c, hb, :], pbank(2 + hb),
                                                  b1[:, ds(2 * i + p, 1), hb:hb + 1].rearrange("p a b -> p (a b)"), 0.0,
                                                  ALU.add, ALU.max).then_inc(sem("hT_dve"), 1)
                            if not (first and p == 0 and c == 0):
                                e = 2 * i + p if c == 1 else 2 * i + p - 1
                                add_bias(v - 1, 1 - c, e, 8 * m + 2 * i + p if c == 1 else 8 * m + 2 * i + p - 1)

                def add_bias(v, c, e, stored):
                    dve.wait_ge(sem("l2"), v + 1)
                    if not (isinstance(stored, int) and stored == 0):
                        dve.wait_ge(sem(f"y_st{c}"), 16 * stored)
                    dve.tensor_tensor(yo[:, c, :, :], pbank(6 + c).rearrange("p (j d) -> p j d", d=D),
                                      b2[:, ds(e, 1), :].to_broadcast([P, PER_CHUNK, D]), ALU.add).then_inc(sem("y_out"), 1)

                repeat(dve, E // 2, chunks)
                add_bias(sbase + 15, 1, E - 1, 8 * m + 7)
                for grp in range(TILES // GROUP):
                    dve.wait_ge(sem(f"got{grp}"), 16 * K * GROUP * (m + 1))
                    for q in range(K):
                        for t in range(GROUP * grp, GROUP * (grp + 1)):
                            ins = dve.scalar_tensor_tensor(X[:, t, :], yg[:, t, q, :], gate[:, q, t:t + 1], X[:, t, :],
                                                           ALU.mult, ALU.add)
                        chain(ins)
                    ln_statistics(2 * m + 1, grp)
                    ln_apply(2 * m + 1, grp, grp % 2)
                stage_end(dve, k + 1)

            experts(0, 0)


            chain(dve.memset(u_pad[:, :, 0:CONV_PAD], 0.0))

            def split_bc(b, first):
                for h in range(HALVES):
                    v = 2 * b + h
                    for d in range(DT):
                        dve.wait_ge(sem("u_sb"), DT * v + d + 1)
                        if not (first and h == 0):
                            dve.wait_ge(sem("uc"), DT * (v - 1) + d + 1)
                        tap = lambda j: u_pad[:, d, CHUNK * h + j:CHUNK * (h + 1) + j]
                        dve.tensor_scalar(cacc[:, d, :], tap(0), conv_w[:, d, 0:1], None, ALU.mult).then_inc(sem("tap"), 1)
                        for j in range(1, DCONV):
                            dve.wait_ge(sem("tap"), 3 * (DT * v + d) + j)
                            dve.scalar_tensor_tensor(cacc[:, d, :], tap(j), conv_w[:, d, j:j + 1], cacc[:, d, :], ALU.mult, ALU.add)\
                                .then_inc(sem("conv" if j == DCONV - 1 else "tap"), 1)
                    dve.wait_ge(sem("bc_ps"), v + 1)
                    S = BCs[:, ds(b * TIME + CHUNK * h, CHUNK)]
                    dve.tensor_copy(bch[0:96, :], pbank(6)[0:96, :]).then_inc(sem("bc1"), 1)
                    dve.wait_ge(sem("bc1"), v + 1)
                    dve.tensor_tensor(bcf[0][0:96, :], pbank(6)[0:96, :], bch[0:96, :], ALU.subtract).then_inc(sem("bc2"), 1)
                    dve.tensor_copy(S[0:32, :], bch[0:32, :]).then_inc(sem("bc2"), 1)
                    dve.wait_ge(sem("bc2"), 2 * v + 2)
                    dve.nop().then_inc(sem("bc_done"), 1)
                    dve.tensor_copy(bcm[0:96, :], bcf[0][0:96, :]).then_inc(sem("bc3"), 1)
                    dve.wait_ge(sem("bc3"), v + 1)
                    dve.tensor_tensor(bcf[1][64:96, :], bcf[0][64:96, :], bcm[64:96, :], ALU.subtract).then_inc(sem("bc4"), 1)
                    dve.tensor_copy(S[32:64, :], bcm[32:64, :]).then_inc(sem("bc4"), 1)
                    dve.wait_ge(sem("bc4"), 2 * v + 2)
                    dve.tensor_copy(S[64:96, :], bcf[1][64:96, :]).then_inc(sem("BCs"), 1)

            repeat(dve, BATCH, split_bc)

            def deltas(b, first):
                for h in range(HALVES):
                    v = 2 * b + h
                    for d in range(DT):
                        n = DT * v + d
                        dve.wait_ge(sem("sp1"), n + 1)
                        dve.tensor_scalar(sp[2 + d], pbank(4 + d), b_dt[:, d:d + 1], 0.0, ALU.add, ALU.max)\
                            .then_inc(sem("sp_relu"), 1)
                        dve.wait_ge(sem("sp_relu"), n + 1)
                        dve.wait_ge(sem("sp3"), n + 1)
                        dve.tensor_tensor(dlt[d][:, ds(b * TIME + CHUNK * h, CHUNK)], sp[2 + d], sp[d], ALU.add)\
                            .then_inc(sem("delta"), 1)

            with dve.Fori(0, BATCH) as i:
                deltas(i, False)
            dve.wait_ge(sem("delta"), DT * CHUNKS)
            dve.wait_ge(sem("BCs"), CHUNKS)
            dve.wait_ge(sem("uc"), DT * CHUNKS)
            dve.wait_ge(sem("x_ps"), DT * CHUNKS)
            dve.nop().then_inc(sem("pre_all"), 1)

            def steps_times_u(b):
                for d in range(DT):
                    ins = dve.tensor_tensor(dtu[:, d, :], dlt[d][:, ds(b * TIME, TIME)],
                                            uc[:, d, ds(b, 1), :].rearrange("p a t -> p (a t)"), ALU.mult)
                ins.then_inc(sem("dtu"), 1)

            def scans(b, first, last=False):
                ub = lambda d: uc[:, d, ds(b, 1), :].rearrange("p a t -> p (a t)")
                zb = lambda d: zs[:, d, ds(b, 1), :].rearrange("p a t -> p (a t)")
                if first:
                    steps_times_u(0)

                def scale(u):
                    n = u // DT
                    dve.wait_ge(sem("scan"), 32 * b + u + 1)
                    dve.wait_ge(sem("Cs"), DS * b + n + 1)
                    dve.tensor_tensor(w[:, u % NW, :], w[:, u % NW, :], Cs[:, n % 2, :], ALU.mult).then_inc(sem("hC"), 1)

                for u in range(DT * DS):
                    n, d = u // DT, u % DT
                    dve.wait_ge(sem("dA"), 32 * b + u + 1)
                    dve.wait_ge(sem("dBu"), 32 * b + u + 1)
                    dve.tensor_tensor_scan(w[:, u % NW, :], dA[:, d, :], w[:, u % NW, :], 0.0, ALU.mult, ALU.add)\
                        .then_inc(sem("scan"), 1)
                    scale(u)
                if not last:
                    dve.wait_ge(sem("dBu"), 32 * (b + 1))
                    steps_times_u(b + 1)
                dve.wait_ge(sem("ysum"), 32 * (b + 1))
                for d in range(DT):
                    ins = dve.scalar_tensor_tensor(ub(d), ub(d), D_skip[:, d:d + 1], pbank(4 + 2 * d, 2), ALU.mult, ALU.add)
                ins.then_inc(sem("yD"), 1)
                dve.wait_ge(sem("yD"), b + 1)
                for d in range(DT):
                    ins = dve.tensor_tensor(ub(d), ub(d), zb(d), ALU.mult)
                ins.then_inc(sem("yz"), 1)

            dve.wait_ge(sem("zs"), DT * CHUNKS)
            scans(0, True)
            with dve.Fori(1, BATCH - 1) as i:
                scans(i, False)
            scans(BATCH - 1, False, True)
            for c in range(CHUNKS):
                dve.wait_ge(sem("m_out"), c + 1)
                xb = X[:, 4 * c:4 * (c + 1), :]
                chain(dve.tensor_tensor(xb, xb, pbank(c % 4).rearrange("p (j d) -> p j d", d=D), ALU.add))
                dve.nop().then_inc(sem("m_add"), 1)
                ln_statistics(2, c)
                ln_apply(2, c, c % 2)
            stage_end(dve, 2)

            experts(1, 2)

            def soft(s, k):
                base = UNITS * s

                def maxima(u, t, r):
                    dve.wait_ge(sem("Lc"), u + 1)
                    if not below(u, RING):
                        dve.wait_ge(sem("Es"), u + 1 - RING)
                    dve.tensor_reduce(mD[:, r, :], Lc[:, r, :].rearrange("p (n q) -> p n q", q=PSLOT), AX, ALU.max)\
                        .then_inc(sem("mD"), 1)
                    dve.tensor_reduce(mxC[:, r % 2, ds(t, 1), :].rearrange("p a q -> p (a q)"),
                                      Lc[:, r, :].rearrange("p (n q) -> p q n", q=PSLOT), AX, ALU.max).then_inc(sem("mxC"), 1)

                def sums(u, r):
                    dve.wait_ge(sem("Ed"), u + 1)
                    dve.tensor_reduce(sD[:, r, :], Ed[:, r, :].rearrange("p (n q) -> p n q", q=PSLOT), AX, ALU.add)\
                        .then_inc(sem("sD"), 1)
                    dve.wait_ge(sem("sD"), u + 1)
                    dve.reciprocal(rD[:, r, :], sD[:, r, :]).then_inc(sem("rD"), 1)

                def units(i):
                    for r in range(RING):
                        u = base + RING * i + r
                        maxima(u, 2 * i + r // 2, r)
                        if not below(RING * i + r, 1):
                            sums(u - 1, (r - 1) % RING)

                dispatch_loop(dve, units)
                sums(base + UNITS - 1, RING - 1)
                dve.wait_ge(sem("slotX"), UNITS * (s + 1))
                for h in range(2):
                    dve.tensor_scalar(slotX[:, HW * h:HW * (h + 1)], pbank(4 + 2 * h, 2), -33000.0, 65000.0,
                                      ALU.max, ALU.min).then_inc(sem("clipped"), 1)
                dve.wait_ge(sem("mxC"), UNITS * (s + 1))
                chain(dve.tensor_tensor(mxC[:, 0, :, :], mxC[:, 0, :, :], mxC[:, 1, :, :], ALU.max))
                chain(dve.tensor_scalar(mCs[:, :, 0:PSLOT], mxC[:, 0, :, :], -1.0, None, ALU.mult))
                dve.scalar_tensor_tensor(mCs[:, :, PSLOT:2 * PSLOT], mxC[:, 0, :, :], -1.0, mCs[:, :, 0:PSLOT],
                                         ALU.mult, ALU.subtract).then_inc(sem("mCs"), 1)
                for h in range(2):
                    dve.wait_ge(sem("slot_m"), 2 * s + h + 1)
                    dve.tensor_tensor(slotA[:, 1024 * h:1024 * (h + 1)], slotX[:, 1024 * h:1024 * (h + 1)], pbank(2 * h, 2),
                                      ALU.subtract).then_inc(sem("slot_c"), 1)
                for h in range(2):
                    dve.wait_ge(sem("slot_r"), 2 * s + h + 1)
                    dve.tensor_tensor(slotA[:, 1024 * h:1024 * (h + 1)], slotA[:, 1024 * h:1024 * (h + 1)],
                                      slotB[:, 1024 * h:1024 * (h + 1)], ALU.mult).then_inc(sem("slot_n"), 1)
                for g in range(4):
                    dve.wait_ge(sem("Yt_ps"), 4 * s + g + 1)
                    if g == 0:
                        dve.wait_ge(sem("we"), 16 * (1 + EPT) * (s + 1))
                    dve.tensor_tensor(Yt[:, 4 * g:4 * (g + 1), :], pbank(4 + g).rearrange("p (s h) -> p s h", h=D),
                                      eb[:, 4 * g:4 * (g + 1), :], ALU.add).then_inc(sem("Yt"), 1)
                stage_end(dve, k + 1)
                base = CHUNKS * s

                def normalise(v, c):
                    dve.wait_ge(sem("Ec"), ST * (v + 1))
                    ec = Ec[:, c, :, :]
                    for j, (dst, lo, hi) in enumerate(((t8, ec[:, 0:8, :], ec[:, 8:16, :]), (t4, t8[:, 0:4, :], t8[:, 4:8, :]),
                                                       (t2, t4[:, 0:2, :], t4[:, 2:4, :]), (t1, t2[:, 0, :], t2[:, 1, :]))):
                        if j:
                            dve.wait_ge(sem(f"tree{j - 1}"), v + 1)
                        dve.tensor_tensor(dst, lo, hi, ALU.add).then_inc(sem(f"tree{j}"), 1)
                    dve.wait_ge(sem("Rz"), v + 1)
                    dve.tensor_tensor(ec, ec, Rz.unsqueeze(1).to_broadcast([P, ST, CHUNK]), ALU.mult).then_inc(sem("C"), 1)

                def residual(v, i2, c):
                    dve.wait_ge(sem("y_tok"), v + 1)
                    xb = X[:, ds(8 * i2 + 4 * c, 4), :]
                    dve.scalar_tensor_tensor(xb, pbank(6).rearrange("p (j d) -> p j d", d=D), 0.5, xb, ALU.mult, ALU.add)\
                        .then_inc(sem("s_add"), 1)
                    if s == 0:
                        dve.wait_ge(sem("s_add"), v + 1)
                        ln_statistics(4, 2 * i2 + c)

                normalise(base, 0)
                normalise(base + 1, 1)
                residual(base, 0, 0)

                with dve.Fori(1, CHUNKS // 2) as i:
                    if s == 0:
                        ln_apply(4, 2 * i - 2, 0)
                    normalise(base + 2 * i, 0)
                    residual(base + 2 * i - 1, i - 1, 1)
                    if s == 0:
                        ln_apply(4, 2 * i - 1, 1)
                    normalise(base + 2 * i + 1, 1)
                    residual(base + 2 * i, i, 0)
                residual(base + CHUNKS - 1, CHUNKS // 2 - 1, 1)
                if s == 0:
                    ln_apply(4, CHUNKS - 2, 0)
                    ln_apply(4, CHUNKS - 1, 1)
                stage_end(dve, k + 2)

            soft(0, 3)

            for v in range(HD):
                ins = dve.tensor_copy(Wvv[:, v, :].rearrange("p (h k) -> p h k", k=HD),
                                      Wv[:, :].rearrange("p (h v) -> p h v", v=HD)[:, :, v:v + 1].to_broadcast([P, HEADS, HD]))
            ins.then_inc(sem("Wvv"), 1)

            def gla_in(b, first):
                for h in range(HALVES):
                    v = 2 * b + h
                    for j, (t, c) in enumerate(((q_s, float(HD) ** -0.5), (k_s, 1.0))):
                        dve.wait_ge(sem("qk_sig"), 2 * v + j + 1)
                        dve.scalar_tensor_tensor(t[:, ds(b, 1), CHUNK * h:CHUNK * (h + 1)].rearrange("p a t -> p (a t)"),
                                                 pbank(j), c, sg[:, j, :], ALU.mult, ALU.mult).then_inc(sem("qk"), 1)

            with dve.Fori(0, BATCH) as i:
                gla_in(i, False)
            dve.wait_ge(sem("fg"), 2 * CHUNKS)
            dve.wait_ge(sem("qk"), 2 * CHUNKS)

            def gla(b, first):
                kb = k_s[:, ds(b, 1), :].rearrange("p a t -> p (a t)")
                fb = f_s[:, ds(b, 1), :].rearrange("p a t -> p (a t)")

                def outer(v):
                    n = HD * b + v
                    dve.wait_ge(sem("vb"), n + 1)
                    if not (first and v < NW):
                        dve.wait_ge(sem("osum"), n + 1 - NW)
                    dve.tensor_tensor(kv[:, v % NW, :], kb, pbank(2 * (v % 2), 2), ALU.mult).then_inc(sem("kv"), 1)

                outer(0)
                for v in range(HD):
                    if v + 1 < HD:
                        outer(v + 1)
                    dve.wait_ge(sem("kv"), HD * b + v + 1)
                    dve.tensor_tensor_scan(kv[:, v % NW, :], fb, kv[:, v % NW, :], 0.0, ALU.mult, ALU.add)\
                        .then_inc(sem("kv_scan"), 1)
                dve.wait_ge(sem("osum"), HD * (b + 1))
                dve.tensor_tensor(og[:, ds(b, 1), :].rearrange("p a t -> p (a t)"), g_s[:, ds(b, 1), :].rearrange("p a t -> p (a t)"),
                                  pbank(4, 2), ALU.mult).then_inc(sem("og"), 1)

            repeat(dve, BATCH, gla)
            dve.wait_ge(sem("og"), BATCH)

            def attended(v, h):
                dve.wait_ge(sem("a_out"), v + 1)
                xb = X[:, ds(4 * v, 4), :]
                dve.tensor_tensor(xb, xb, pbank(2 + h).rearrange("p (j d) -> p j d", d=D), ALU.add).then_inc(sem("a_add"), 1)
                dve.wait_ge(sem("a_add"), v + 1)
                ln_statistics(5, v)
                ln_apply(5, v, h)

            def head_norm(b, first):
                for h in range(HALVES):
                    v = 2 * b + h
                    dve.wait_ge(sem("rms"), v + 1)
                    if not (first and v < 2):
                        dve.wait_ge(sem("a_out"), v - 1)
                    dve.scalar_tensor_tensor(nrm[:, h, :], og[:, ds(b, 1), CHUNK * h:CHUNK * (h + 1)].rearrange("p a t -> p (a t)"),
                                             norm_w[:, 0:1], rms[:, 1, :], ALU.mult, ALU.mult).then_inc(sem("nrm"), 1)
                    if not (first and h == 0):
                        attended(v - 1, 1 - h)

            repeat(dve, BATCH, head_norm)
            attended(CHUNKS - 1, 1)
            stage_end(dve, 6)
            soft(1, 6)

        @block.tensor
        def _(pe):
            pe.wait_ge(sem("ones"), 4)
            pe.wait_ge(sem("consts0"), 16 * len(loads[0]))

            def ln_turn(n, c, h, bank):
                v = 8 * n + c
                pe.wait_ge(sem("ln_x"), v + 1)
                if not (isinstance(v, int) and v == 0):
                    pe.wait_ge(sem("ln_XT"), v)
                for j in range(PER_CHUNK):
                    ins = pe.transpose(pbank(bank)[:, P * j:P * (j + 1)], stage[:, h, P * j:P * (j + 1)], ident[:, :])
                ins.then_inc(sem("ln_T"), 1)

            for c in range(CHUNKS):
                ln_turn(0, c, c % 2, 0)
            stage_end(pe, 0)

            def xt(b, h, shift=0):
                return XT[:, ds(b, 1), CONV_PAD + CHUNK * h - shift:CONV_PAD + CHUNK * (h + 1) - shift].rearrange("p a t -> p (a t)")

            def experts(m, k):
                for t in range(TILES):
                    b, j = t // PER_BATCH, t % PER_BATCH
                    ins = pe.matmul(pbank(7)[:, E * t:E * (t + 1)], XT[:, b, CONV_PAD + P * j:CONV_PAD + P * (j + 1)], wg[:, :],
                                    start=True, stop=True)
                ins.then_inc(sem("logits"), 1)
                pe.wait_ge(sem("masks"), m + 1)
                mk = mask.rearrange("p a b -> p (a b)")
                pe.matmul(pbank(5), tri[:, :], mk, start=True, stop=True)
                pe.matmul(pbank(6), onesb[:, :], mk, start=True, stop=True).then_inc(sem("counts"), 1)
                base = 16 * m

                def turn(v, c, loaded):
                    pe.wait_ge(sem(f"d_in{c}"), 16 * loaded)
                    if not (isinstance(v, int) and v < 2):
                        pe.wait_ge(sem("dT"), v - 1)
                    for j in range(PER_CHUNK):
                        ins = pe.transpose(pbank(c)[:, P * j:P * (j + 1)], dtile[:, c, j, :], ident[:, :])
                    ins.then_inc(sem("d_T"), 1)

                def layer1(v, c, p):
                    pe.wait_ge(sem("dT"), v + 1)
                    for hb in range(HB):
                        if not (isinstance(v, int) and v == 0):
                            pe.wait_ge(sem("hT_act" if hb % 2 == 0 else "hT_dve"), 2 * v - 1 + hb // 2)
                        pe.matmul(pbank(2 + hb), w1s[:, p, P * hb:P * (hb + 1)], dT[:, c, :], start=True, stop=True)\
                            .then_inc(sem(f"l1_{hb}"), 1)

                def layer2(v, c, p):
                    pe.wait_ge(sem("hT_act"), 2 * (v + 1))
                    pe.wait_ge(sem("hT_dve"), 2 * (v + 1))
                    if not (isinstance(v, int) and v < 2):
                        pe.wait_ge(sem("y_out"), v - 1)
                    for j in range(PER_CHUNK):
                        for hb in range(HB):
                            ins = pe.matmul(pbank(6 + c)[:, P * j:P * (j + 1)], hT[:, c, hb, P * j:P * (j + 1)], w2s[:, p, hb, :],
                                            start=(hb == 0), stop=(hb == HB - 1))
                    ins.then_inc(sem("l2"), 1)

                pe.wait_ge(sem("slots"), m + 1)
                turn(base, 0, 8 * m + 1)

                def chunks(i, first, last=False):
                    for p in range(2):
                        for c in range(EC):
                            v = base + 4 * i + 2 * p + c
                            if c == 0:
                                pe.wait_ge(sem(f"w_in{p}"), 32 * (4 * m + i + 1))
                            layer1(v, c, p)
                            if not (last and p == 1 and c == 1):
                                turn(v + 1, 1 - c, 8 * m + 2 * i + p + 1 + c)
                            if not (first and p == 0 and c == 0):
                                layer2(v - 1, 1 - c, p if c == 1 else 1 - p)

                chunks(0, True)
                with pe.Fori(1, E // 2 - 1) as i:
                    chunks(i, False)
                chunks(E // 2 - 1, False, True)
                layer2(base + 15, 1, 1)
                for c in range(CHUNKS):
                    ln_turn(2 * m + 1, c, c % 2, 0)
                stage_end(pe, k + 1)

            experts(0, 0)


            def project(b, first):
                for h in range(HALVES):
                    v = 2 * b + h
                    for d in range(DT):
                        if not (first and h == 0):
                            pe.wait_ge(sem("u_sb"), DT * (v - 1) + d + 1)
                        pe.matmul(pbank(d), W_in[:, P * d:P * (d + 1)], xt(b, h), start=True, stop=True).then_inc(sem("u_ps"), 1)
                    for d in range(DT):
                        if not (first and h == 0):
                            pe.wait_ge(sem("zs"), DT * (v - 1) + d + 1)
                        pe.matmul(pbank(2 + d), W_in[:, DI + P * d:DI + P * (d + 1)], xt(b, h), start=True, stop=True)\
                            .then_inc(sem("z_ps"), 1)
                    if not (first and h == 0):
                        low_rank(v - 1, b if h else b - 1, 1 - h, first)

            def low_rank(v, b, h, early):
                pe.wait_ge(sem("uc"), DT * (v + 1))
                if not early:
                    pe.wait_ge(sem("dts"), v)
                for d in range(DT):
                    ins = pe.matmul(pbank(6)[0:96 + RANK, :], W_bc3[:, d, :],
                                    uc[:, d, ds(b, 1), CHUNK * h:CHUNK * (h + 1)].rearrange("p a t -> p (a t)"),
                                    start=(d == 0), stop=(d == DT - 1))
                ins.then_inc(sem("bc_ps"), 1)

            repeat(pe, BATCH, project)
            low_rank(CHUNKS - 1, BATCH - 1, 1, False)

            def steps(b, first):
                for h in range(HALVES):
                    v = 2 * b + h
                    hold(pe, sem("dts"), v + 1)
                    for d in range(DT):
                        if not (first and h == 0):
                            hold(pe, sem("delta"), DT * (v - 1) + d + 1)
                        pe.matmul(pbank(4 + d), W_dt[:, P * d:P * (d + 1)],
                                  dts[0:RANK, ds(b, 1), CHUNK * h:CHUNK * (h + 1)].rearrange("p a t -> p (a t)"),
                                  start=True, stop=True).then_inc(sem("x_ps"), 1)

            repeat(pe, BATCH, steps)
            pe.wait_ge(sem("pre_all"), 1)

            def spread(v, b, n, early):
                for q, name in enumerate(("Bs", "Cs")):
                    if not early:
                        pe.wait_ge(sem(name), v)
                    for h in range(HALVES):
                        ins = pe.matmul(pbank(2 * q + h), row32[:, DS * q + n:DS * q + n + 1].to_broadcast([96, P]),
                                        BCs[0:96, ds(b * TIME + CHUNK * h, CHUNK)], start=True, stop=True)
                ins.then_inc(sem("bc"), 1)

            def scans(b, first, last=False):
                def add(u):
                    n, d = u // DT, u % DT
                    pe.wait_ge(sem("hC"), 32 * b + u + 1)
                    if u == 0 and not first:
                        pe.wait_ge(sem("yD"), b)
                    for h in range(HALVES):
                        ins = pe.matmul(pbank(4 + 2 * d + h), ident[:, :], w[:, u % NW, CHUNK * h:CHUNK * (h + 1)],
                                        start=(n == 0), stop=(n == DS - 1))
                    ins.then_inc(sem("ysum"), 1)

                for n in range(DS):
                    v = DS * b + n + 2
                    if n + 2 < DS:
                        spread(v, b, n + 2, False)
                    elif not last:
                        spread(v, b + 1, n + 2 - DS, False)
                    for d in range(DT):
                        add(DT * n + d)

            spread(0, 0, 0, True)
            spread(1, 0, 1, False)
            scans(0, True)
            with pe.Fori(1, BATCH - 1) as i:
                scans(i, False)
            scans(BATCH - 1, False, True)
            pe.wait_ge(sem("yz"), BATCH)
            for c in range(CHUNKS):
                if c >= 4:
                    pe.wait_ge(sem("m_add"), c - 3)
                for j in range(PER_CHUNK):
                    t = PER_CHUNK * c + j
                    at = P * (t % PER_BATCH)
                    for d in range(DT):
                        ins = pe.matmul(pbank(c % 4)[:, P * j:P * (j + 1)], uc[:, d, t // PER_BATCH, at:at + P], W_out[:, d, :],
                                        start=(d == 0), stop=(d == DT - 1))
                ins.then_inc(sem("m_out"), 1)
                if c:
                    ln_turn(2, c - 1, (c - 1) % 2, 7)
            ln_turn(2, CHUNKS - 1, 1, 7)
            stage_end(pe, 2)

            experts(1, 2)

            def soft(s, k):
                base = UNITS * s

                def logits(u, t, r):
                    h = r % 2
                    if h == 0:
                        pe.wait_ge(sem("xts"), TILES * s + t + 1)
                    if not below(u, 2):
                        pe.wait_ge(sem("Lc"), u - 1)
                    for c in range(2):
                        at = HW * h + CHUNK * c
                        pe.matmul(pbank(2 * h + c), xts[:, r // 2, :], phiT[:, at:at + CHUNK], start=True, stop=False)
                        ins = pe.matmul(pbank(2 * h + c), onesb[0:3, :], phi_b3[:, at:at + CHUNK], start=False, stop=True)
                    ins.then_inc(sem("L"), 1)

                def gather(u, t, r, start, stop):
                    h = r % 2
                    pe.wait_ge(sem("Dd"), u + 1)
                    if h == 0:
                        pe.wait_ge(sem("xns"), TILES * s + t + 1)
                    for c in range(2):
                        ins = pe.matmul(pbank(4 + 2 * h + c), xns[:, r // 2, :], Dd[:, r, CHUNK * c:CHUNK * (c + 1)],
                                        start=start, stop=stop, skip_group_check=True)
                    ins.then_inc(sem("slotX"), 1)

                def units(i):
                    for r in range(RING):
                        u = base + RING * i + r
                        t = 2 * i + r // 2
                        logits(u, t, r)
                        if not below(i, 1):
                            gather(u - RING, t - 2, r, below(t - 2, 1), False)

                dispatch_loop(pe, units)
                for r in range(RING):
                    gather(base + UNITS - RING + r, TILES - 2 + r // 2, r, False, r >= 2)
                pe.wait_ge(sem("mCs"), s + 1)
                for g in range(4):
                    if g > 1:
                        pe.wait_ge(sem("mCT"), 4 * s + g - 1)
                    for j in range(8):
                        ins = pe.transpose(pbank(g % 2).bitcast(BF16)[0:64, P * j:P * (j + 1)], mCs[:, 8 * g + j, :], identb[:, :])
                    ins.then_inc(sem("mCT_ps"), 1)
                pe.wait_ge(sem("mCT"), 4 * (s + 1))
                pe.wait_ge(sem("clipped"), 2 * (s + 1))
                for h in range(2):
                    for c in range(2):
                        at = 1024 * h + CHUNK * c
                        ins = pe.matmul(pbank(2 * h + c), mean_w[:, :], slotX[:, at:at + CHUNK], start=True, stop=True)
                    ins.then_inc(sem("slot_m"), 1)
                for h in range(2):
                    pe.wait_ge(sem("slot_sq"), 2 * s + h + 1)
                    for c in range(2):
                        at = 1024 * h + CHUNK * c
                        ins = pe.matmul(pbank(4 + 2 * h + c), mean_w[:, :], slotB[:, at:at + CHUNK], start=True, stop=True)
                    ins.then_inc(sem("slot_v"), 1)
                pe.wait_ge(sem("slot_r"), 2 * (s + 1))
                pe.wait_ge(sem("we"), 16 * (1 + EPT) * (s + 1))
                for g in range(4):
                    pe.wait_ge(sem("slot_t"), 2 * s + g // 2 + 1)
                    for t in range(4):
                        for j in range(EPT):
                            n = EPT * (4 * g + t) + j
                            ins = pe.matmul(pbank(4 + g)[PSLOT * j:PSLOT * (j + 1), P * t:P * (t + 1)],
                                            slotA[:, PSLOT * n:PSLOT * (n + 1)], We[:, n, :], start=True, stop=True,
                                            skip_group_check=True)
                    ins.then_inc(sem("Yt_ps"), 1)
                stage_end(pe, k + 1)
                base = CHUNKS * s

                def logits_T(v, b, c, early):
                    for t in range(ST):
                        if not (early and t < 4):
                            pe.wait_ge(sem("Ec"), ST * v + t - 3)
                        pe.matmul(pbank(t % 4), phiT[:, P * t:P * (t + 1)], xt(b, c), start=True, stop=False)
                        pe.matmul(pbank(t % 4), row128[:, :],
                                  mCT[0:64, ds(b * TIME + CHUNK * c, CHUNK)], start=False, stop=True).then_inc(sem("LT"), 1)

                def total(v):
                    pe.wait_ge(sem("tree3"), v + 1)
                    pe.matmul(pbank(4), same_p[:, :], t1, start=True, stop=True).then_inc(sem("Z"), 1)

                def combine(v, c, early):
                    pe.wait_ge(sem("C"), v + 1)
                    if not early:
                        pe.wait_ge(sem("yT"), v)
                    for t in range(ST):
                        ins = pe.matmul(pbank(5), Yt[:, t, :], Ec[:, c, t, :], start=(t == 0), stop=(t == ST - 1))
                    ins.then_inc(sem("yT_ps"), 1)

                def turn_y(v, early):
                    pe.wait_ge(sem("yT"), v + 1)
                    if not early:
                        pe.wait_ge(sem("s_add"), v)
                    for j in range(PER_CHUNK):
                        ins = pe.transpose(pbank(6)[:, P * j:P * (j + 1)], yT[:, P * j:P * (j + 1)], ident[:, :])
                    ins.then_inc(sem("y_tok"), 1)

                e0 = s == 0
                logits_T(base, 0, 0, True)
                total(base)
                logits_T(base + 1, 0, 1, False)
                combine(base, 0, e0)
                total(base + 1)
                turn_y(base, e0)

                with pe.Fori(1, CHUNKS // 2) as i:
                    for c in range(2):
                        v = base + 2 * i + c
                        logits_T(v, i, c, False)
                        if s == 0:
                            ln_turn(4, 2 * (i - 1) + c, c, 7)
                        combine(v - 1, 1 - c, False)
                        total(v)
                        turn_y(v - 1, False)
                combine(base + CHUNKS - 1, 1, False)
                turn_y(base + CHUNKS - 1, False)
                if s == 0:
                    for c in range(2):
                        ln_turn(4, CHUNKS - 2 + c, c, 7)
                stage_end(pe, k + 2)

            soft(0, 3)

            def gla_in(b, first):
                for h in range(HALVES):
                    v = 2 * b + h
                    if not (first and h == 0):
                        pe.wait_ge(sem("low"), 2 * v)
                    pe.matmul(pbank(2)[0:HD, :], Wf1[:, :], xt(b, h), start=True, stop=True)
                    pe.matmul(pbank(3)[0:HD, :], Wg1[:, :], xt(b, h), start=True, stop=True).then_inc(sem("low_ps"), 1)
                    for j, W in enumerate((Wq, Wk)):
                        if not (first and h == 0):
                            pe.wait_ge(sem("qk"), 2 * (v - 1) + j + 1)
                        pe.matmul(pbank(j), W[:, :], xt(b, h), start=True, stop=True).then_inc(sem("qk_ps"), 1)
                    pe.wait_ge(sem("low"), 2 * (v + 1))
                    for j, W in enumerate((Wf2, Wg2)):
                        if not (first and h == 0):
                            pe.wait_ge(sem("fg"), 2 * (v - 1) + j + 1)
                        pe.matmul(pbank(4 + j), W[:, :], low[0:HD, j, :], start=True, stop=True).then_inc(sem("fg_ps"), 1)

            repeat(pe, BATCH, gla_in)
            pe.wait_ge(sem("fg"), 2 * CHUNKS)
            pe.wait_ge(sem("qk"), 2 * CHUNKS)

            def gla(b, first):
                def values(v):
                    n = HD * b + v
                    if not (first and v < 2):
                        pe.wait_ge(sem("kv"), n - 1)
                    if v == 0 and first:
                        pe.wait_ge(sem("Wvv"), 1)
                    for h in range(HALVES):
                        ins = pe.matmul(pbank(2 * (v % 2) + h), Wvv[:, v, :], xt(b, h), start=True, stop=True)
                    ins.then_inc(sem("vb"), 1)

                def add(v):
                    if v == 0 and first:
                        pe.wait_ge(sem("head_sum"), 16)
                    pe.wait_ge(sem("qS"), HD * b + v + 1)
                    if v == 0 and not first:
                        pe.wait_ge(sem("og"), b)
                    for h in range(HALVES):
                        ins = pe.matmul(pbank(4 + h), head_sum[:, v, :], kv[:, v % NW, CHUNK * h:CHUNK * (h + 1)],
                                        start=(v == 0), stop=(v == HD - 1))
                    ins.then_inc(sem("osum"), 1)

                values(0)
                values(1)
                for v in range(HD):
                    if v + 2 < HD:
                        values(v + 2)
                    add(v)

            repeat(pe, BATCH, gla)

            def mean_square(v, h, early):
                pe.wait_ge(sem("sq"), v + 1)
                if not early:
                    pe.wait_ge(sem("rms0"), v - 1)
                pe.matmul(pbank(h), head_mean[:, :], sq[:, h, :], start=True, stop=True).then_inc(sem("ms"), 1)

            def head_norm(b, first, last=False):
                for h in range(HALVES):
                    v = 2 * b + h
                    if not (last and h == 1):
                        mean_square(v + 1, 1 - h, first and h == 0)
                    pe.wait_ge(sem("nrm"), v + 1)
                    if not first:
                        pe.wait_ge(sem("a_add"), v - 1)
                    for j in range(PER_CHUNK):
                        ins = pe.matmul(pbank(2 + h)[:, P * j:P * (j + 1)], nrm[:, h, P * j:P * (j + 1)], Wo[:, :],
                                        start=True, stop=True)
                    ins.then_inc(sem("a_out"), 1)
                    if not (first and h == 0):
                        ln_turn(5, v - 1, 1 - h, 7)

            mean_square(0, 0, True)
            head_norm(0, True)
            with pe.Fori(1, BATCH - 1) as i:
                head_norm(i, False)
            head_norm(BATCH - 1, False, True)
            ln_turn(5, CHUNKS - 1, 1, 7)
            stage_end(pe, 6)
            soft(1, 6)


def constants():
    i = np.arange(P)
    f = np.float32
    hs = np.zeros((P, HD, P), f)
    for v in range(HD):
        for h in range(HEADS):
            hs[h * HD:(h + 1) * HD, v, h * HD + v] = 1.0
    return {
        "k_ident": np.eye(P, dtype=f),
        "k_tri": (i[:, None] <= i[None, :]).astype(f),
        "k_rev": np.broadcast_to(np.arange(E, 0, -1).astype(f), (P, E)).copy(),
        "k_row32": (np.arange(96)[:, None] % 32 == np.arange(32)[None, :]).astype(f),
        "k_same_p": (i[:, None] % PSLOT == i[None, :] % PSLOT).astype(f),
        "k_head_mean": (i[:, None] // HD == i[None, :] // HD).astype(f) / HD,
        "k_head_sum": hs,
    }


def kernel(**inputs):
    import concourse.bacc as bacc
    from concourse.bass_utils import run_bass_kernel_spmd

    arr = {k: np.ascontiguousarray(v) for k, v in inputs.items()}
    col = lambda v: np.ascontiguousarray(v.reshape(-1, P).T)
    arrays = {k: arr[k] for k in (
        "L0_attn_x", "L0_attn_W_in", "L0_attn_conv_w", "L0_attn_W_xproj", "L0_attn_W_dt", "L0_attn_A_log", "L0_attn_W_out", "L0_ffn_wg",
        "L0_ffn_w1", "L0_ffn_w2", "L0_ffn_b2", "L1_attn_Wq", "L1_attn_Wk", "L1_attn_Wv", "L1_attn_Wo", "L1_attn_Wf1",
        "L1_attn_Wf2", "L1_attn_Wg1", "L1_attn_Wg2", "L1_ffn_phi_b", "L1_ffn_expert_w", "L1_ffn_expert_b")}
    arrays["h_b1"] = np.ascontiguousarray(arr["L0_ffn_b1"].reshape(E, HB, P).transpose(2, 0, 1))
    arrays["h_conv_b"] = col(arr["L0_attn_conv_b"])
    arrays["h_b_dt"] = col(arr["L0_attn_b_dt"])
    arrays["h_D"] = col(arr["L0_attn_D"])
    arrays["h_phi_wT"] = np.ascontiguousarray(arr["L1_ffn_phi_w"].T)
    arrays["h_phi_b"] = col(arr["L1_ffn_phi_b"])
    arrays["h_norm_w"] = col(arr["L1_attn_norm_weight"])
    arrays.update(constants())

    nc = bacc.Bacc("TRN2", target_bir_lowering=False, num_devices=1)
    a, named = {}, {}
    for name, v in arrays.items():
        named["in_" + name] = v
        a[name] = nc.dram_tensor("in_" + name, v.shape, mybir.dt.from_np(v.dtype), kind="ExternalInput").ap()
    out = nc.dram_tensor("out_x", (BATCH, TIME, D), F32, kind="ExternalOutput").ap()
    disp = nc.dram_tensor("slot_inputs", (SLOTS, D), F32, kind="Internal").ap()
    yexp = nc.dram_tensor("slot_outputs", (SLOTS, D), F32, kind="Internal").ap()
    build(nc, a, out, disp, yexp)
    r = run_bass_kernel_spmd(nc, [named], core_ids=[0])
    return r.results[0]["out_x"]
```

```python
from contextlib import ExitStack

import numpy as np

import concourse.bass as bass
from concourse import mybir

F32 = mybir.dt.float32
BF16 = mybir.dt.bfloat16
U32 = mybir.dt.uint32
ALU = mybir.AluOpType
ACT = mybir.ActivationFunctionType
AX = mybir.AxisListType.X

P = 128
CHUNK = 512
EPS = 1e-5
LOWEST = -3.0e38

BATCH, TIME, D = 4, 1024, 128
TOKENS = BATCH * TIME
TILES = TOKENS // P
PER_BATCH = TIME // P
HALVES = TIME // CHUNK
CHUNKS = TOKENS // CHUNK
PER_CHUNK = CHUNK // P
E, K, H = 8, 2, 512
HB = H // P
CAP = K * (TOKENS // E)
SLOTS = E * CAP
ROW = D + 1
EC = CAP // CHUNK
FAR = float(1 << 20)
DI, DS, DCONV, RANK = 256, 16, 4, 8
DT = DI // P
CONV_PAD = DCONV - 1
HEADS, HD = 16, 8
NEXP, PSLOT = 64, 32
SOFT = NEXP * PSLOT
ST = SOFT // P
EPT = P // PSLOT
NH = NEXP // 2
UNITS = 2 * TILES
RING = 4
HW = SOFT // 2
GROUP = 4
PUT = 8
ENGINES = 5
KEPT = (0, 2, 3, 5)


def build(nc, a, out, disp, ytok):
    with ExitStack() as ctx:
        def sb(name, shape, dt=F32):
            return ctx.enter_context(nc.sbuf_tensor(name, shape, dt))

        sems = {}

        def sem(name):
            if name not in sems:
                sems[name] = ctx.enter_context(nc.semaphore(name))
            return sems[name]

        def ds(start, size):
            return bass.ds(start, size)

        def repeat(eng, n, body):
            body(0, True)
            with eng.Fori(1, n) as i:
                body(i, False)

        X = sb("X", [P, TILES, D])
        XN = sb("XN", [P, TILES, ROW])
        XT = sb("XT", [P, BATCH, CONV_PAD + TIME])
        ps = ctx.enter_context(nc.psum_tensor("ps", [P, 8, CHUNK], F32))

        loads = [[], []]

        def resident(name, shape, src, dt=F32):
            t = sb("c_" + name, shape, dt)
            full = t[tuple(slice(None) for _ in shape)]
            loads[name not in ("ident", "rev", "wg", "row_id")].append((full, src))
            return t

        ident = resident("ident", [P, P], a["k_ident"])
        rev = resident("rev", [P, E], a["k_rev"])
        row_id = resident("row_id", [P, TILES], a["k_row_id"])
        wg = resident("wg", [P, E], a["L0_ffn_wg"])
        b1 = resident("b1", [P, E, HB], a["h_b1"])
        b2 = resident("b2", [P, E, D], a["L0_ffn_b2"].partition_broadcast(P))
        W_in = resident("W_in", [P, 2 * DI], a["L0_attn_W_in"])
        conv_w = resident("conv_w", [P, DT, DCONV], a["L0_attn_conv_w"].rearrange("(k p) n -> p k n", p=P))
        conv_b = resident("conv_b", [P, DT], a["h_conv_b"])
        W_x = resident("W_x", [P, DT, RANK + 2 * DS], a["L0_attn_W_xproj"].rearrange("(k p) n -> p k n", p=P))
        W_dt = resident("W_dt", [RANK, DI], a["L0_attn_W_dt"])
        b_dt = resident("b_dt", [P, DT], a["h_b_dt"])
        A_log = resident("A_log", [P, DT, DS], a["L0_attn_A_log"].rearrange("(k p) n -> p k n", p=P))
        D_skip = resident("D_skip", [P, DT], a["h_D"])
        W_out = resident("W_out", [P, DT, D], a["L0_attn_W_out"].rearrange("(k p) n -> p k n", p=P))
        phiT = resident("phiT", [P, SOFT], a["h_phi_wT"])
        phi_bc = resident("phi_bc", [P, ST], a["h_phi_b"])
        same_p = resident("same_p", [P, P], a["k_same_p"])
        Wq = resident("Wq", [P, D], a["L1_attn_Wq"])
        Wk = resident("Wk", [P, D], a["L1_attn_Wk"])
        Wv = resident("Wv", [P, D], a["L1_attn_Wv"])
        Wo = resident("Wo", [P, D], a["L1_attn_Wo"])
        Wf1 = resident("Wf1", [P, HD], a["L1_attn_Wf1"])
        Wg1 = resident("Wg1", [P, HD], a["L1_attn_Wg1"])
        Wf2 = resident("Wf2", [HD, D], a["L1_attn_Wf2"])
        Wg2 = resident("Wg2", [HD, D], a["L1_attn_Wg2"])
        norm_w = resident("norm_w", [P, 1], a["h_norm_w"])
        head_mean = resident("head_mean", [P, P], a["k_head_mean"])

        tri = sb("tri", [P, P], BF16)
        identb = sb("identb", [P, P], BF16)
        row32 = sb("row32", [96, 32], BF16)
        onesb = sb("onesb", [P, P], BF16)
        mean_w = sb("mean_w", [P, P])
        ones64 = sb("ones64", [P, K * TILES])
        eps = sb("eps", [P, 1])
        zero = sb("zero", [P, ROW])
        W_bc3 = sb("W_bc3", [P, DT, 96 + RANK])
        A_neg = sb("A_neg", [P, DT, DS])
        phi_b3 = sb("phi_b3", [3, SOFT], BF16)
        row128 = sb("row128", [64, P], BF16)

        stats = sb("stats", [P, TILES, 6])
        ln_s = sb("ln_s", [P, 9, TILES])
        stage = sb("stage", [P, HALVES, CHUNK])

        ARENA = 120 * 256
        arena = sb("arena", [P, ARENA])

        class Cut:
            def __init__(self):
                self.at = 0

            def __call__(self, shape, dt=F32):
                n = int(np.prod(shape))
                words = n if dt != BF16 else (n + 1) // 2
                words = (words + 7) // 8 * 8
                assert self.at + words <= ARENA, (self.at + words, ARENA)
                t = arena[:, self.at:self.at + words]
                self.at += words
                if dt != F32:
                    t = t.bitcast(dt)
                t = t[:, 0:n]
                if len(shape) == 2:
                    t = t.rearrange("p (a b) -> p a b", b=shape[1])
                if len(shape) == 3:
                    t = t.rearrange("p (a b c) -> p a b c", b=shape[1], c=shape[2])
                return t

        cut = Cut()
        cut.at = ARENA - 9 * SOFT // 2 - 2 * D
        setup_at = cut.at
        phi_b3f, row, rest, acc = (cut([SOFT])[0:3, :] for _ in range(4))
        part = cut([SOFT], BF16)[0:3, :]
        tri_f = cut([P])
        row32_f = cut([32])[0:96, :]
        loads[0].append((tri_f, a["k_tri"]))
        loads[1].append((row32_f, a["k_row32"]))
        loads[1].append((phi_b3f, a["L1_ffn_phi_b"].partition_broadcast(3)))

        cut = Cut()
        w1s = cut([2, H])
        w2s = cut([2, HB, D])
        dtile = cut([EC, PER_CHUNK, ROW])
        dT = cut([EC, CHUNK])
        hT = cut([EC, HB, CHUNK])
        yo = cut([EC, PER_CHUNK, D])
        yg = cut([TILES, K, D])
        g8 = [cut([TILES, E]) for _ in range(3)]
        g1 = [cut([TILES]) for _ in range(10)]
        mask = cut([K, TILES * E], BF16)
        run = [cut([K * TILES * E]) for _ in range(3)]
        g64 = [cut([K * TILES]) for _ in range(8)]
        gate = cut([K, TILES])
        rank = cut([K, TILES])
        put_at = cut([K * TILES], U32)
        empty = cut([PER_CHUNK])
        y_at = cut([EC * PER_CHUNK], U32)
        assert cut.at <= setup_at, (cut.at, setup_at)

        cut = Cut()
        uc = cut([DT, BATCH, TIME])
        zs = cut([DT, BATCH, TIME])
        delta = XN[:, :, :].rearrange("p a b -> p (a b)")[:, 0:BATCH * TIME]
        delta2 = cut([BATCH * TIME])
        BCs = cut([TOKENS], BF16)
        pre = cut.at
        sp_ln = cut([2, DT, CHUNK])
        sp_relu = cut([2, DT, CHUNK])
        dts = cut([BATCH, TIME])
        cut.at = pre
        bcf = cut([CHUNK])
        bcm = cut([CHUNK], BF16)
        u_pad = delta[:, 0:DT * (CONV_PAD + TIME)].rearrange("p (d t) -> p d t", d=DT)
        cacc = delta[:, 2560:2560 + DT * CHUNK].rearrange("p (d t) -> p d t", d=DT)
        cut.at = pre
        dtu = XT[:, 0:DT, CONV_PAD:]
        Bs = XT[:, DT:DT + 2, CONV_PAD:]
        Cs = cut([2, TIME])
        NW = 4
        dA = cut([DT, TIME])
        w = cut([NW, TIME])
        dlt = [delta, delta2]

        cut = Cut()
        q_s = cut([BATCH, TIME])
        k_s = cut([BATCH, TIME])
        f_s = cut([BATCH, TIME])
        g_s = cut([BATCH, TIME])
        og = cut([BATCH, TIME])
        sg = cut([2, CHUNK])
        low = cut([2, CHUNK])
        sq, rms = sg, low
        kv = cut([NW, TIME])
        nrm = cut([2, CHUNK])
        head_sum = cut([HD, P])
        Wvv = cut([HD, P])

        cut = Cut()
        We = cut([NEXP, D])
        Yt = cut([ST, D])
        mCT = cut([TOKENS], BF16)
        lnz = cut([CHUNK])
        yT = cut([CHUNK])
        combine_at = cut.at
        eb = cut([ST, D])
        mxC = cut([2, TILES, PSLOT])
        ring_at = cut.at
        mCs = cut([TILES, 2 * PSLOT], BF16)
        slotX = cut([SOFT])
        slotA = cut([SOFT])
        slotB = cut([SOFT])
        cut.at = NEXP * D
        Lc = cut([RING, HW])
        xts = cut([2, P])
        xns = cut([2, P])
        assert cut.at <= combine_at
        cut.at = ring_at
        Ed = cut([RING, HW])
        Dd = cut([RING, HW])
        mD = cut([RING, NH])
        sD = cut([RING, NH])
        rD = cut([RING, NH])
        cut.at = combine_at
        Ec = cut([2, ST, CHUNK])
        flat = arena[:, 0:NEXP * D]
        t8 = flat[:, 0:4096].rearrange("p (a b) -> p a b", b=CHUNK)
        t4 = flat[:, 4096:6144].rearrange("p (a b) -> p a b", b=CHUNK)
        t2 = flat[:, 6144:7168].rearrange("p (a b) -> p a b", b=CHUNK)
        t1 = flat[:, 7168:7680]
        Rz = flat[:, 7680:8192]

        def pbank(i, n=1):
            return ps[:, i, :] if n == 1 else ps[:, i:i + n, :].rearrange("p a b -> p (a b)")

        def over(t, n):
            return t.unsqueeze(2).to_broadcast([t.shape[0], t.shape[1], n])

        def below(i, n):
            return isinstance(i, int) and i < n

        def dispatch_loop(eng, units):
            units(0)
            units(1)
            with eng.Fori(2, UNITS // RING - 1) as i:
                units(i)
            units(UNITS // RING - 1)

        def stage_end(eng, k):
            eng.drain().then_inc(sem("stage"), 1)
            eng.wait_ge(sem("stage"), ENGINES * (k + 1))

        def hold(eng, s, value):
            eng.wait_ge(s, value)
            if not isinstance(value, int):
                eng.nop(nofuse=True)

        def tap(d, h, j):
            return u_pad[:, d, CHUNK * h + j:CHUNK * (h + 1) + j]

        class Chain:

            def __init__(self, eng, name):
                self.eng, self.sem, self.n = eng, sem(name), 0

            def __call__(self, ins):
                self.n += 1
                ins.then_inc(self.sem, 1)
                self.eng.wait_ge(self.sem, self.n)

        block = ctx.enter_context(nc.Block())

        @block.sync
        def _(sp_):
            for b in range(BATCH):
                sp_.dma_start(X[:, PER_BATCH * b:PER_BATCH * (b + 1), :],
                              a["L0_attn_x"][b].rearrange("(j p) d -> p j d", p=P)).then_inc(sem(f"x_in{b}"), 16)
            for dst, src in loads[0]:
                sp_.dma_start(dst, src).then_inc(sem("consts0"), 16)

            def clear(m):
                for t, name in ((disp[m], "disp_zero"), (ytok[m], "ytok_zero")):
                    width = t.shape[1]
                    sp_.dma_start(t.rearrange("(p a) d -> p a d", p=P),
                                  zero[:, 0:width].unsqueeze(1).to_broadcast([P, SLOTS // P, width])).then_inc(sem(name), 16)

            sp_.wait_ge(sem("zeroed"), 1)
            clear(0)
            for dst, src in loads[1]:
                sp_.dma_start(dst, src).then_inc(sem("consts1"), 16)
            stage_end(sp_, 0)

            def experts(m, k):
                dsp = disp[m].rearrange("(e c j p) d -> p (e c) j d", c=EC, j=PER_CHUNK, p=P)

                def weights(e, b):
                    sp_.dma_start(w1s[:, b, :], a["L0_ffn_w1"][ds(e, 1), :, :].rearrange("a d h -> (a d) h"))\
                        .then_inc(sem(f"w_in{b}"), 16)
                    sp_.dma_start(w2s[:, b, :, :], a["L0_ffn_w2"][ds(e, 1), :, :].rearrange("a (k p) d -> p (a k) d", p=P))\
                        .then_inc(sem(f"w_in{b}"), 16)

                weights(0, 0)
                weights(1, 1)
                for g in range(TILES // PUT):
                    sp_.wait_ge(sem(f"put{g}"), 16 * K * PUT * (m + 1))

                def pair(i, first, last=False):
                    for p in range(2):
                        for c in range(EC):
                            if not (first and p == 0):
                                sp_.wait_ge(sem("d_T"), 16 * m + 4 * i + 2 * p + c - 1)
                                sp_.wait_ge(sem("y_at"), 16 * m + 4 * i + 2 * p + c - 1)
                            sp_.dma_start(dtile[:, c, :, :], dsp[:, ds(4 * i + 2 * p + c, 1), :, :].rearrange("p a j d -> p (a j) d"))\
                                .then_inc(sem(f"d_in{c}"), 16)
                        if not (first and p == 0) and not (last and p == 1):
                            sp_.wait_ge(sem("l2"), 16 * m + 4 * i + 2 * p)
                            weights(2 * i + p + 1, 1 - p)

                pair(0, True)
                with sp_.Fori(1, E // 2 - 1) as i:
                    pair(i, False)
                pair(E // 2 - 1, False, True)
                for c in range(EC):
                    sp_.wait_ge(sem(f"y_put{c}"), 16 * PER_CHUNK * E * (m + 1))
                yv = ytok[m].rearrange("(t p q) d -> p t q d", p=P, q=K)
                for g in range(TILES // GROUP):
                    sp_.dma_start(yg[:, GROUP * g:GROUP * (g + 1), :, :], yv[:, GROUP * g:GROUP * (g + 1), :, :])\
                        .then_inc(sem(f"got{g}"), 16)
                stage_end(sp_, k + 1)

            experts(0, 0)
            clear(1)
            stage_end(sp_, 2)
            experts(1, 2)

            def soft(k):
                sp_.dma_start(We, a["L1_ffn_expert_w"].rearrange("n d h -> d n h")).then_inc(sem("we"), 16)
                ebs = a["L1_ffn_expert_b"].rearrange("(s j) h -> j s h", j=EPT)
                for j in range(EPT):
                    sp_.dma_start(eb[PSLOT * j:PSLOT * (j + 1), :, :], ebs[j].partition_broadcast(PSLOT))\
                        .then_inc(sem("we"), 16)
                stage_end(sp_, k + 1)
                stage_end(sp_, k + 2)

            soft(3)
            sp_.dma_start(head_sum, a["k_head_sum"]).then_inc(sem("head_sum"), 16)
            stage_end(sp_, 6)
            soft(6)
            sp_.dma_start(out.rearrange("b (j p) d -> p (b j) d", p=P), X[:, :, :]).then_inc(sem("x_out"), 16)
            sp_.wait_ge(sem("x_out"), 16)

        @block.gpsimd
        def _(pool):
            pool.memset(onesb[:, :], 1.0).then_inc(sem("ones"), 1)
            pool.memset(mean_w[:, :], 1.0 / P).then_inc(sem("ones"), 1)
            pool.memset(ones64[:, :], 1.0).then_inc(sem("ones"), 1)
            pool.memset(eps[:, :], EPS).then_inc(sem("ones"), 1)
            stage_end(pool, 0)

            def experts(m, k):
                hold(pool, sem("slots"), m + 1)
                pool.wait_ge(sem("disp_zero"), 16 * (m + 1))
                for q in range(K):
                    for t in range(TILES):
                        if q and t % PUT == 0:
                            hold(pool, sem("second"), TILES // PUT * m + t // PUT + 1)
                        pool.indirect_dma_start(
                            disp[m], bass.IndirectOffsetOnAxis(ap=put_at[:, q * TILES + t:q * TILES + t + 1], axis=0),
                            XN[:, t, :], None, bounds_check=SLOTS - 1, oob_is_err=False)\
                            .then_inc(sem(f"put{t // PUT}"), 16)
                pool.wait_ge(sem("ytok_zero"), 16 * (m + 1))

                def store(i, first):
                    for c in range(EC):
                        hold(pool, sem("y_out"), 16 * m + EC * i + c + 1)
                        for j in range(PER_CHUNK):
                            pool.indirect_dma_start(
                                ytok[m], bass.IndirectOffsetOnAxis(ap=y_at[:, PER_CHUNK * c + j:PER_CHUNK * c + j + 1], axis=0),
                                yo[:, c, j, :], None, bounds_check=K * TOKENS - 1, oob_is_err=False)\
                                .then_inc(sem(f"y_put{c}"), 16)

                repeat(pool, E, store)
                stage_end(pool, k + 1)

            experts(0, 0)

            def mamba(b, first):
                for n in range(DS):
                    for d in range(DT):
                        u = DT * n + d
                        if n == 0 and d == 0:
                            hold(pool, sem("dtu"), b + 1)
                        hold(pool, sem("Bs"), DS * b + n + 1)
                        if not (first and u < NW):
                            hold(pool, sem("ysum"), 32 * b + u + 1 - NW)
                        pool.tensor_tensor(w[:, u % NW, :], dtu[:, d, :], Bs[:, n % 2, :], ALU.mult)\
                            .then_inc(sem("dBu"), 1)

            repeat(pool, BATCH, mamba)
            stage_end(pool, 2)
            experts(1, 2)

            def soft(s, k):
                base = UNITS * s

                def normalise(u, r):
                    hold(pool, sem("rD"), u + 1)
                    if not below(u, RING):
                        hold(pool, sem("slotX"), u + 1 - RING)
                    pool.tensor_tensor(Dd[:, r, :].rearrange("p (n q) -> p n q", q=PSLOT),
                                       Ed[:, r, :].rearrange("p (n q) -> p n q", q=PSLOT),
                                       over(rD[:, r, :], PSLOT), ALU.mult).then_inc(sem("Dd"), 1)

                def shift(u, r):
                    hold(pool, sem("mD"), u + 1)
                    if not below(u, RING):
                        hold(pool, sem("Dd"), u + 1 - RING)
                    pool.tensor_tensor(Ed[:, r, :].rearrange("p (n q) -> p n q", q=PSLOT),
                                       Lc[:, r, :].rearrange("p (n q) -> p n q", q=PSLOT),
                                       over(mD[:, r, :], PSLOT), ALU.subtract).then_inc(sem("Es"), 1)

                def units(i):
                    for r in range(RING):
                        u = base + RING * i + r
                        shift(u, r)
                        if not below(RING * i + r, 2):
                            normalise(u - 2, (r - 2) % RING)

                dispatch_loop(pool, units)
                for r in (2, 3):
                    normalise(base + UNITS - RING + r, r)
                stage_end(pool, k + 1)
                stage_end(pool, k + 2)

            soft(0, 3)

            def gla(b, first):
                for v in range(HD):
                    hold(pool, sem("kv_scan"), HD * b + v + 1)
                    pool.tensor_tensor(kv[:, v % NW, :], q_s[:, ds(b, 1), :].rearrange("p a t -> p (a t)"), kv[:, v % NW, :],
                                       ALU.mult).then_inc(sem("qS"), 1)

            repeat(pool, BATCH, gla)
            stage_end(pool, 6)
            soft(1, 6)

        @block.scalar
        def _(act):
            chain = Chain(act, "act_chain")
            act.preload_act_table_set("natural_log_exp_and_others")

            def ln_scale(n, c):
                hold(act, sem("ln_var"), 8 * n + c + 1)
                act.activation(ln_s[:, 6, ds(4 * c, 4)], ln_s[:, 5, ds(4 * c, 4)], ACT.Ln).then_inc(sem("ln_ln"), 1)
                hold(act, sem("ln_ln"), 8 * n + c + 1)
                act.activation(ln_s[:, 7, ds(4 * c, 4)], ln_s[:, 6, ds(4 * c, 4)], ACT.Exp, scale=-0.5)\
                    .then_inc(sem("ln_rstd"), 1)

            def ln_copies(n, b, h, bank):
                c = 2 * b + h
                if n in KEPT:
                    hold(act, sem("ln_x"), 8 * n + c + 1)
                    act.activation(XN[:, ds(4 * c, 4), 0:D], stage[:, h, :].rearrange("p (j d) -> p j d", d=D),
                                   ACT.Copy).then_inc(sem("ln_keep"), 1)
                hold(act, sem("ln_T"), 8 * n + c + 1)
                act.activation(XT[:, ds(b, 1), CONV_PAD + CHUNK * h:CONV_PAD + CHUNK * (h + 1)].rearrange("p a t -> p (a t)"),
                               pbank(bank), ACT.Copy).then_inc(sem("ln_XT"), 1)

            for c in range(CHUNKS):
                ln_scale(0, c)
                if c:
                    ln_copies(0, (c - 1) // 2, (c - 1) % 2, 0)
            ln_copies(0, BATCH - 1, 1, 0)
            stage_end(act, 0)

            def experts(m, k):
                hold(act, sem("g_diff"), m + 1)
                act.activation(g1[5], g1[4], ACT.Exp).then_inc(sem("g_exp"), 1)
                if m == 0:
                    act.wait_ge(sem("consts1"), 16 * len(loads[1]))
                    chain(act.activation(A_neg[:, :, :], A_log[:, :, :], ACT.Exp))
                    chain(act.activation(A_neg[:, :, :], A_neg[:, :, :], ACT.Copy, scale=-1.0))

                def evac_T(v, c):
                    hold(act, sem("d_T"), v + 1)
                    act.activation(dT[:, c, :], pbank(c), ACT.Copy).then_inc(sem("dT"), 1)

                base = 16 * m
                evac_T(base, 0)

                def chunks(i, first, last=False):
                    for p in range(2):
                        for c in range(EC):
                            v = base + 4 * i + 2 * p + c
                            for hb in (0, 2):
                                hold(act, sem("l1"), HB * v + hb + 1)
                                act.activation(hT[:, c, hb, :], pbank(2 + hb), ACT.Relu,
                                               bias=b1[:, ds(2 * i + p, 1), hb:hb + 1].rearrange("p a b -> p (a b)"))\
                                    .then_inc(sem("hT_act"), 1)
                            if not (last and p == 1 and c == EC - 1):
                                evac_T(v + 1, 1 - c)

                chunks(0, True)
                with act.Fori(1, E // 2 - 1) as i:
                    chunks(i, False)
                chunks(E // 2 - 1, False, True)
                n = 2 * m + 1
                for c in range(CHUNKS):
                    ln_scale(n, c)
                    if c:
                        ln_copies(n, (c - 1) // 2, (c - 1) % 2, 0)
                ln_copies(n, BATCH - 1, 1, 0)
                stage_end(act, k + 1)

            experts(0, 0)

            act.preload_act_table(ACT.Silu)

            def project(b, first):
                for h in range(HALVES):
                    v = 2 * b + h
                    for d in range(DT):
                        hold(act, sem("u_ps"), DT * v + d + 1)
                        if h == 0 and not first:
                            hold(act, sem(f"conv{d}"), v)
                        act.activation(u_pad[:, d, CONV_PAD + CHUNK * h:CONV_PAD + CHUNK * (h + 1)], pbank(d), ACT.Copy)\
                            .then_inc(sem("u_sb"), 1)
                    for d in range(DT):
                        hold(act, sem("u_sb"), DT * v + d + 1)
                        if not below(v, 1):
                            hold(act, sem("uc"), DT * (v - 1) + d + 1)
                        act.activation(cacc[:, d, :], tap(d, h, 0), ACT.Copy, scale=conv_w[:, d, 0:1]).then_inc(sem(f"tap{d}"), 1)
                    for d in range(DT):
                        hold(act, sem("z_ps"), DT * v + d + 1)
                        act.activation(zs[:, d, ds(b, 1), CHUNK * h:CHUNK * (h + 1)].rearrange("p a t -> p (a t)"),
                                       pbank(2 + d), ACT.Silu).then_inc(sem("zs"), 1)
                    if not (first and h == 0):
                        low_rank(v - 1, b if h else b - 1, 1 - h)
                    for d in range(DT):
                        hold(act, sem(f"conv{d}"), v + 1)
                        act.activation(uc[:, d, ds(b, 1), CHUNK * h:CHUNK * (h + 1)].rearrange("p a t -> p (a t)"), cacc[:, d, :],
                                       ACT.Silu, bias=conv_b[:, d:d + 1]).then_inc(sem("uc"), 1)

            def low_rank(v, b, h):
                hold(act, sem("bc_ps"), v + 1)
                act.activation(BCs[0:96, ds(b * TIME + CHUNK * h, CHUNK)], pbank(6 + h)[0:96, :], ACT.Copy).then_inc(sem("dts"), 1)
                act.activation(dts[0:RANK, ds(b, 1), CHUNK * h:CHUNK * (h + 1)].rearrange("p a t -> p (a t)"),
                               pbank(6 + h)[96:96 + RANK, :], ACT.Copy).then_inc(sem("dts"), 1)

            act.wait_ge(sem("u_padded"), 1)
            repeat(act, BATCH, project)
            low_rank(CHUNKS - 1, BATCH - 1, 1)
            act.preload_act_table_set("natural_log_exp_and_others")

            def magnitude(v, h, d):
                hold(act, sem("x_ps"), DT * v + d + 1)
                act.activation(sp_ln[:, h, d, :], pbank(DT * h + d), ACT.Abs, bias=b_dt[:, d:d + 1]).then_inc(sem("sp1"), 1)

            def softplus(b, first, last=False):
                for h in range(HALVES):
                    v = 2 * b + h
                    more = not (last and h == 1)
                    if more:
                        if not (first and h == 0):
                            hold(act, sem("delta"), DT * v)
                        magnitude(v + 1, 1 - h, 0)
                    hold(act, sem("sp1"), DT * v + 2)
                    act.activation(sp_ln[:, h, :, :], sp_ln[:, h, :, :], ACT.Exp, scale=-1.0).then_inc(sem("sp2"), 1)
                    if more:
                        magnitude(v + 1, 1 - h, 1)
                    hold(act, sem("sp2"), v + 1)
                    act.activation(sp_ln[:, h, :, :], sp_ln[:, h, :, :], ACT.Ln, bias=1.0).then_inc(sem("sp3"), 1)

            hold(act, sem("BCs"), CHUNKS)
            for d in range(DT):
                magnitude(0, 0, d)
            softplus(0, True)
            with act.Fori(1, BATCH - 1) as i:
                softplus(i, False)
            softplus(BATCH - 1, False, True)
            hold(act, sem("pre_all"), 1)

            def scan_in(b, first):
                for n in range(DS):
                    v = DS * b + n
                    hold(act, sem("bc"), v + 1)
                    if not (first and n < 2):
                        hold(act, sem("dBu"), DT * (v - 1))
                    act.activation(Bs[:, n % 2, :], pbank(0, 2), ACT.Copy).then_inc(sem("Bs"), 1)
                    if not (first and n < 2):
                        hold(act, sem("hC"), DT * (v - 1))
                    act.activation(Cs[:, n % 2, :], pbank(2, 2), ACT.Copy).then_inc(sem("Cs"), 1)
                    for d in range(DT):
                        if not (first and n == 0):
                            hold(act, sem("scan"), DT * (v - 1) + d + 1)
                        act.activation(dA[:, d, :], dlt[d][:, ds(b * TIME, TIME)], ACT.Exp, scale=A_neg[:, d, n:n + 1])\
                            .then_inc(sem("dA"), 1)

            repeat(act, BATCH, scan_in)
            for c in range(CHUNKS):
                ln_scale(2, c)
                if c:
                    ln_copies(2, (c - 1) // 2, (c - 1) % 2, 6)
            ln_copies(2, BATCH - 1, 1, 6)
            stage_end(act, 2)

            experts(1, 2)

            def soft(s, k):
                base = UNITS * s

                def copy_xt(t, r):
                    if not below(t, 2):
                        hold(act, sem("L"), base + 2 * t - 2)
                    act.activation(xts[:, r, :], XT[:, ds(t // PER_BATCH, 1), ds(CONV_PAD + (P * t) % TIME, P)]
                                   .rearrange("p a t -> p (a t)"), ACT.Copy).then_inc(sem("xts"), 1)

                def copy_xn(t, r):
                    if not below(t, 2):
                        hold(act, sem("slotX"), base + 2 * t - 2)
                    act.activation(xns[:, r, :], XN[:, ds(t, 1), 0:D].rearrange("p a d -> p (a d)"),
                                   ACT.Copy).then_inc(sem("xns"), 1)

                def copy_L(u, r):
                    hold(act, sem("L"), base + u + 1)
                    if not below(u, RING):
                        hold(act, sem("Es"), base + u + 1 - RING)
                        hold(act, sem("mxC"), base + u + 1 - RING)
                    act.activation(Lc[:, r, :], pbank(2 * (r % 2), 2), ACT.Copy).then_inc(sem("Lc"), 1)

                def units(i):
                    last = isinstance(i, int) and i == UNITS // RING - 1
                    for r in range(RING):
                        u = RING * i + r
                        if not (last and r == RING - 1):
                            copy_L(u + 1, (r + 1) % RING)
                        if r % 2 == 0:
                            if not last:
                                copy_xt(2 * i + 2 + r // 2, r // 2)
                            if not below(u, 1):
                                copy_xn(2 * i - 1 + r // 2, 1 - r // 2)
                        hold(act, sem("Es"), base + u + 1)
                        act.activation(Ed[:, r, :], Ed[:, r, :], ACT.Exp).then_inc(sem("Ed"), 1)

                copy_xt(0, 0)
                copy_xt(1, 1)
                copy_L(0, 0)
                dispatch_loop(act, units)
                copy_xn(TILES - 1, 1)
                for g in range(4):
                    hold(act, sem("mCT_ps"), 4 * s + g + 1)
                    act.activation(mCT[0:64, 1024 * g:1024 * (g + 1)], pbank(g % 2).bitcast(BF16)[0:64, :], ACT.Copy)\
                        .then_inc(sem("mCT"), 1)
                for h in range(2):
                    hold(act, sem("slot_c"), 2 * s + h + 1)
                    act.activation(slotB[:, 1024 * h:1024 * (h + 1)], slotA[:, 1024 * h:1024 * (h + 1)], ACT.Square)\
                        .then_inc(sem("slot_sq"), 1)
                for h in range(2):
                    hold(act, sem("slot_v"), 2 * s + h + 1)
                    chain(act.activation(slotB[:, 1024 * h:1024 * (h + 1)], pbank(4 + 2 * h, 2), ACT.Ln, bias=eps[:, :]))
                    act.activation(slotB[:, 1024 * h:1024 * (h + 1)], slotB[:, 1024 * h:1024 * (h + 1)], ACT.Exp,
                                   scale=-0.5).then_inc(sem("slot_r"), 1)
                for h in range(2):
                    hold(act, sem("slot_n"), 2 * s + h + 1)
                    act.activation(slotA[:, 1024 * h:1024 * (h + 1)], slotA[:, 1024 * h:1024 * (h + 1)], ACT.Tanh)\
                        .then_inc(sem("slot_t"), 1)
                stage_end(act, k + 1)
                act.preload_act_table_set("natural_log_exp_and_others")

                def exp_T(v, c, first, before=None):
                    for t in range(ST):
                        if before and t == ST // 2:
                            ln_scale(4, 2 * before[0] + before[1])
                        hold(act, sem("LT"), ST * v + t + 1)
                        if t == 0 and not first:
                            hold(act, sem("yT_ps"), v - 1)
                        act.activation(Ec[:, c, t, :], pbank(t % 4), ACT.Exp, bias=phi_bc[:, t:t + 1])\
                            .then_inc(sem("Ec"), 1)

                def finish(v):
                    hold(act, sem("Z"), v + 1)
                    act.activation(lnz, pbank(4), ACT.Ln).then_inc(sem("lnz"), 1)
                    hold(act, sem("lnz"), v + 1)
                    act.activation(Rz, lnz, ACT.Exp, scale=-1.0).then_inc(sem("Rz"), 1)

                def copy_y(v):
                    hold(act, sem("yT_ps"), v + 1)
                    act.activation(yT, pbank(5), ACT.Copy).then_inc(sem("yT"), 1)

                base = CHUNKS * s
                exp_T(base, 0, True)
                finish(base)
                exp_T(base + 1, 1, True)
                copy_y(base)
                finish(base + 1)

                with act.Fori(1, CHUNKS // 2) as i:
                    for c in range(2):
                        v = base + 2 * i + c
                        exp_T(v, c, False, (i - 1, c) if s == 0 else None)
                        if s == 0:
                            ln_copies(4, i - 1, c, 7)
                        copy_y(v - 1)
                        finish(v)
                copy_y(base + CHUNKS - 1)
                if s == 0:
                    for c in range(2):
                        ln_scale(4, CHUNKS - 2 + c)
                        ln_copies(4, BATCH - 1, c, 7)
                stage_end(act, k + 2)

            soft(0, 3)

            act.preload_act_table(ACT.Sigmoid)

            def gla_in(b, first):
                for h in range(HALVES):
                    v = 2 * b + h
                    hold(act, sem("low_ps"), v + 1)
                    act.activation(low[0:HD, 0, :], pbank(2)[0:HD, :], ACT.Copy).then_inc(sem("low"), 1)
                    act.activation(low[0:HD, 1, :], pbank(3)[0:HD, :], ACT.Copy).then_inc(sem("low"), 1)
                    for j in range(2):
                        hold(act, sem("qk_ps"), 2 * v + j + 1)
                        if not (first and h == 0):
                            hold(act, sem("qk"), 2 * v + j - 1)
                        act.activation(sg[:, j, :], pbank(j), ACT.Sigmoid).then_inc(sem("qk_sig"), 1)
                    for j, t in enumerate((f_s, g_s)):
                        hold(act, sem("fg_ps"), 2 * v + j + 1)
                        act.activation(t[:, ds(b, 1), CHUNK * h:CHUNK * (h + 1)].rearrange("p a t -> p (a t)"), pbank(4 + j),
                                       ACT.Sigmoid).then_inc(sem("fg"), 1)

            repeat(act, BATCH, gla_in)
            act.preload_act_table_set("natural_log_exp_and_others")

            def square(v, b, h, early):
                if not early:
                    hold(act, sem("ms"), v - 1)
                act.activation(sq[:, h, :], og[:, ds(b, 1), CHUNK * h:CHUNK * (h + 1)].rearrange("p a t -> p (a t)"), ACT.Square)\
                    .then_inc(sem("sq"), 1)

            def head_norm(b, first, last=False):
                for h in range(HALVES):
                    v = 2 * b + h
                    hold(act, sem("ms"), v + 1)
                    act.activation(rms[:, 0, :], pbank(h), ACT.Ln, bias=eps[:, :]).then_inc(sem("rms0"), 1)
                    hold(act, sem("rms0"), v + 1)
                    if not (first and h == 0):
                        hold(act, sem("nrm"), v)
                    act.activation(rms[:, 1, :], rms[:, 0, :], ACT.Exp, scale=-0.5).then_inc(sem("rms"), 1)
                    if not (last and h == 1):
                        square(v + 1, b + h, 1 - h, first and h == 0)
                    if not (first and h == 0):
                        ln_scale(5, v - 1)
                        ln_copies(5, b if h else b - 1, 1 - h, 7)

            hold(act, sem("og"), BATCH)
            square(0, 0, 0, True)
            head_norm(0, True)
            with act.Fori(1, BATCH - 1) as i:
                head_norm(i, False)
            head_norm(BATCH - 1, False, True)
            ln_scale(5, CHUNKS - 1)
            ln_copies(5, BATCH - 1, 1, 7)
            stage_end(act, 6)
            soft(1, 6)

        @block.vector
        def _(dve):
            chain = Chain(dve, "dve_chain")
            dve.memset(zero[:, :], 0.0).then_inc(sem("zeroed"), 1)
            chain(dve.memset(XT[:, :, 0:CONV_PAD], 0.0))

            def ln_statistics(n, c):
                v = 8 * n + c
                for j in range(PER_CHUNK):
                    ins = dve.bn_stats(stats[:, ds(4 * c + j, 1), :].rearrange("p a b -> p (a b)"),
                                       X[:, ds(4 * c + j, 1), :].rearrange("p a b -> p (a b)"))
                ins.then_inc(sem("ln_step"), 1)
                dve.wait_ge(sem("ln_step"), 3 * v + 1)
                even, odd = (lambda j: stats[:, ds(4 * c, 4), j]), (lambda j: stats[:, ds(4 * c, 4), 3 + j])
                two_mean, gap, m2, gap2, var0, var, _, _, mean = (ln_s[:, j, ds(4 * c, 4)] for j in range(9))
                dve.tensor_tensor(two_mean, even(1), odd(1), ALU.add)
                dve.tensor_tensor(gap, even(1), odd(1), ALU.subtract)
                dve.tensor_tensor(m2, even(2), odd(2), ALU.add).then_inc(sem("ln_step"), 1)
                dve.wait_ge(sem("ln_step"), 3 * v + 2)
                dve.scalar_tensor_tensor(gap2, gap, 0.25, gap, ALU.mult, ALU.mult)
                dve.tensor_scalar(mean, two_mean, 0.5, None, ALU.mult)
                dve.tensor_scalar(var0, m2, 1.0 / D, EPS, ALU.mult, ALU.add).then_inc(sem("ln_step"), 1)
                dve.wait_ge(sem("ln_step"), 3 * v + 3)
                dve.tensor_tensor(var, var0, gap2, ALU.add).then_inc(sem("ln_var"), 1)

            def ln_apply(n, c, h):
                v = 8 * n + c
                dve.wait_ge(sem("ln_rstd"), v + 1)
                if not (isinstance(v, int) and v < 2):
                    dve.wait_ge(sem("ln_T"), v - 1)
                    if n in KEPT and not (isinstance(c, int) and c < 2):
                        dve.wait_ge(sem("ln_keep"), 8 * KEPT.index(n) + c - 1)
                for j in range(PER_CHUNK):
                    t = 4 * c + j
                    ins = dve.tensor_scalar(stage[:, h, D * j:D * (j + 1)], X[:, ds(t, 1), :].rearrange("p a d -> p (a d)"),
                                            ln_s[:, 8, ds(t, 1)], ln_s[:, 7, ds(t, 1)], ALU.subtract, ALU.mult)
                ins.then_inc(sem("ln_x"), 1)

            for c in range(CHUNKS):
                if c % 2 == 0:
                    dve.wait_ge(sem(f"x_in{c // 2}"), 16)
                ln_statistics(0, c)
                if c:
                    ln_apply(0, c - 1, (c - 1) % 2)
            ln_apply(0, CHUNKS - 1, 1)
            dve.wait_ge(sem("consts0"), 16 * len(loads[0]))
            chain(dve.tensor_copy(tri[:, :], tri_f))

            def derive():
                dve.wait_ge(sem("consts1"), 16 * len(loads[1]))
                dve.tensor_copy(W_bc3[:, :, 96:96 + RANK], W_x[:, :, 0:RANK])
                for j in range(3):
                    dve.tensor_copy(W_bc3[:, :, 32 * j:32 * (j + 1)], W_x[:, :, RANK:RANK + 32])
                for dst, src in ((identb, ident[:, :]), (row32, row32_f)):
                    chain(dve.tensor_copy(dst[:, :], src))
                for j in range(EPT):
                    chain(dve.tensor_copy(row128[:, 32 * j:32 * (j + 1)], row32[0:64, :]))
                chain(dve.tensor_copy(rest, phi_b3f))
                for j in range(3):
                    chain(dve.tensor_copy(part, rest))
                    if j == 0:
                        chain(dve.tensor_scalar(acc, part, ident[0:3, 0:1], None, ALU.mult))
                    else:
                        chain(dve.scalar_tensor_tensor(acc, part, ident[0:3, j:j + 1], acc, ALU.mult, ALU.add))
                    if j < 2:
                        chain(dve.tensor_tensor(row, rest, part, ALU.subtract))
                        chain(dve.tensor_copy(rest, row))
                chain(dve.tensor_copy(phi_b3[:, :], acc))

            stage_end(dve, 0)

            def experts(m, k):
                dve.wait_ge(sem("logits"), m + 1)
                lg = pbank(7)[:, 0:TILES * E].rearrange("p (t e) -> p t e", e=E)
                revb = rev[:, :].unsqueeze(1).to_broadcast([P, TILES, E])
                m1, m2, d21, e2, den, gt1, gt2 = g1[0], g1[1], g1[4], g1[5], g1[6], g1[7], g1[8]
                for q, top in enumerate((m1, m2)):
                    src = lg if q == 0 else g8[2]
                    chain(dve.tensor_reduce(top, src, AX, ALU.max))
                    chain(dve.tensor_tensor(g8[0], src, over(top, E), ALU.is_equal))
                    chain(dve.tensor_tensor(g8[1], g8[0], revb, ALU.mult))
                    chain(dve.tensor_reduce(rank[:, q, :], g8[1], AX, ALU.max))
                    chain(dve.tensor_tensor(mask[:, q, :].rearrange("p (t e) -> p t e", e=E), g8[1],
                                            over(rank[:, q, :], E), ALU.is_equal))
                    if q == 0:
                        chain(dve.scalar_tensor_tensor(g8[2], mask[:, 0, :].rearrange("p (t e) -> p t e", e=E), LOWEST, lg,
                                                       ALU.mult, ALU.add))
                dve.nop().then_inc(sem("masks"), 1)
                dve.tensor_tensor(d21, m2, m1, ALU.subtract).then_inc(sem("g_diff"), 1)
                dve.wait_ge(sem("g_exp"), m + 1)
                chain(dve.tensor_scalar(den, e2, 1.0, None, ALU.add))
                chain(dve.reciprocal(gt1, den))
                chain(dve.tensor_tensor(gt2, e2, gt1, ALU.mult))
                dve.wait_ge(sem("counts"), m + 1)
                inside = pbank(5)
                total = pbank(6)
                incl, loc, tmp = run
                tv = total.rearrange("p (t e) -> p t e", e=E)
                iv = incl.rearrange("p (t e) -> p t e", e=E)
                for e in range(E):
                    ins = dve.tensor_tensor_scan(iv[:, :, e], ones64[:, :], tv[:, :, e], 0.0, ALU.mult, ALU.add)
                chain(ins)
                chain(dve.tensor_tensor(tmp, incl, total, ALU.subtract))
                chain(dve.tensor_tensor(loc, tmp, inside, ALU.add))
                chain(dve.tensor_tensor(tmp, loc, mask.rearrange("p a b -> p (a b)"), ALU.mult))
                place, ok, lc, base, slot, far = g64[0:6]
                chain(dve.tensor_reduce(place, tmp.rearrange("p (t e) -> p t e", e=E), AX, ALU.add))
                chain(dve.tensor_scalar(ok, place, CAP + 0.5, None, ALU.is_lt))
                okv = ok.rearrange("p (a b) -> p a b", b=TILES)
                for q, g in enumerate((gt1, gt2)):
                    chain(dve.scalar_tensor_tensor(gate[:, q, :], g, 0.5, okv[:, q, :], ALU.mult, ALU.mult))
                chain(dve.tensor_scalar(lc, place, float(CAP), -1.0, ALU.min, ALU.add))
                chain(dve.tensor_scalar(base, rank.rearrange("p a b -> p (a b)"), -float(CAP), float(SLOTS), ALU.mult, ALU.add))
                chain(dve.tensor_tensor(slot, base, lc, ALU.add))
                chain(dve.tensor_scalar(far, ok, -FAR, FAR, ALU.mult, ALU.add))
                chain(dve.tensor_copy(XN[:, :, D], row_id[:, :]))
                dve.tensor_tensor(put_at, far, slot, ALU.add).then_inc(sem("slots"), 1)
                if m == 0:
                    derive()
                for g in range(TILES // PUT):
                    dve.wait_ge(sem(f"put{g}"), 16 * PUT * (K * m + 1))
                    ids = XN[:, PUT * g:PUT * (g + 1), D]
                    dve.tensor_scalar(ids, ids, 1.0, None, ALU.add).then_inc(sem("second"), 1)

                sbase = 16 * m

                def places(v, c, loaded, used):
                    rows = dtile[:, c, :, D]
                    dve.wait_ge(sem(f"d_in{c}"), 16 * loaded)
                    if not below(v, 1):
                        dve.wait_ge(sem("y_at"), v)
                    if not below(used, 1):
                        dve.wait_ge(sem(f"y_put{c}"), 16 * PER_CHUNK * used)
                    dve.tensor_scalar(empty, rows, 0.5, FAR, ALU.is_lt, ALU.mult).then_inc(sem("empty"), 1)
                    dve.wait_ge(sem("empty"), v + 1)
                    dve.scalar_tensor_tensor(y_at[:, PER_CHUNK * c:PER_CHUNK * (c + 1)], rows, -1.0, empty, ALU.add, ALU.add)\
                        .then_inc(sem("y_at"), 1)

                def chunks(i, first):
                    for p in range(2):
                        for c in range(EC):
                            r = 4 * i + 2 * p + c
                            v = sbase + r
                            for hb in (1, 3):
                                dve.wait_ge(sem("l1"), HB * v + hb + 1)
                                dve.tensor_scalar(hT[:, c, hb, :], pbank(2 + hb),
                                                  b1[:, ds(2 * i + p, 1), hb:hb + 1].rearrange("p a b -> p (a b)"), 0.0,
                                                  ALU.add, ALU.max).then_inc(sem("hT_dve"), 1)
                            places(v, c, 8 * m + 2 * i + p + 1, 8 * m + 2 * i + p)
                            if not (first and p == 0 and c == 0):
                                e = 2 * i + p if c == 1 else 2 * i + p - 1
                                add_bias(v - 1, 1 - c, e, 8 * m + 2 * i + p if c == 1 else 8 * m + 2 * i + p - 1)

                def add_bias(v, c, e, stored):
                    dve.wait_ge(sem("l2"), v + 1)
                    if not below(stored, 1):
                        dve.wait_ge(sem(f"y_put{c}"), 16 * PER_CHUNK * stored)
                    dve.tensor_tensor(yo[:, c, :, :], pbank(6 + c).rearrange("p (j d) -> p j d", d=D),
                                      b2[:, ds(e, 1), :].to_broadcast([P, PER_CHUNK, D]), ALU.add).then_inc(sem("y_out"), 1)

                repeat(dve, E // 2, chunks)
                add_bias(sbase + 15, 1, E - 1, 8 * m + 7)
                for grp in range(TILES // GROUP):
                    dve.wait_ge(sem(f"got{grp}"), 16 * (m + 1))
                    for q in range(K):
                        for t in range(GROUP * grp, GROUP * (grp + 1)):
                            ins = dve.scalar_tensor_tensor(X[:, t, :], yg[:, t, q, :], gate[:, q, t:t + 1], X[:, t, :],
                                                           ALU.mult, ALU.add)
                        chain(ins)
                    ln_statistics(2 * m + 1, grp)
                    if grp:
                        ln_apply(2 * m + 1, grp - 1, (grp - 1) % 2)
                ln_apply(2 * m + 1, CHUNKS - 1, 1)
                stage_end(dve, k + 1)

            experts(0, 0)


            chain(dve.memset(u_pad[:, :, 0:CONV_PAD], 0.0))
            dve.nop().then_inc(sem("u_padded"), 1)

            def split_bc(v, b, h):
                S = BCs[:, ds(b * TIME + CHUNK * h, CHUNK)]
                dve.wait_ge(sem("dts"), 2 * (v + 1))
                if not below(v, 1):
                    dve.wait_ge(sem("BCs"), v)
                dve.tensor_tensor(bcf[0:96, :], pbank(6 + h)[0:96, :], S[0:96, :], ALU.subtract).then_inc(sem("bc_rest"), 1)
                dve.wait_ge(sem("bc_rest"), v + 1)
                dve.tensor_copy(bcm[64:96, :], bcf[64:96, :]).then_inc(sem("bc_mid"), 1)
                dve.tensor_copy(S[32:64, :], bcf[32:64, :])
                dve.wait_ge(sem("bc_mid"), v + 1)
                dve.tensor_tensor(S[64:96, :], bcf[64:96, :], bcm[64:96, :], ALU.subtract).then_inc(sem("BCs"), 1)

            def project(b, first):
                for h in range(HALVES):
                    v = 2 * b + h
                    for j in range(1, DCONV):
                        for d in range(DT):
                            dve.wait_ge(sem(f"tap{d}"), 3 * v + j)
                            dve.scalar_tensor_tensor(cacc[:, d, :], tap(d, h, j), conv_w[:, d, j:j + 1], cacc[:, d, :],
                                                     ALU.mult, ALU.add).then_inc(sem(f"conv{d}" if j == DCONV - 1 else f"tap{d}"), 1)
                    if not (first and h == 0):
                        split_bc(v - 1, b if h else b - 1, 1 - h)

            repeat(dve, BATCH, project)
            split_bc(CHUNKS - 1, BATCH - 1, 1)

            def deltas(b, first):
                for h in range(HALVES):
                    v = 2 * b + h
                    for d in range(DT):
                        dve.wait_ge(sem("sp1"), DT * v + d + 1)
                        dve.tensor_scalar(sp_relu[:, h, d, :], pbank(DT * h + d), b_dt[:, d:d + 1], 0.0, ALU.add, ALU.max)\
                            .then_inc(sem("relu"), 1)
                    dve.wait_ge(sem("relu"), DT * (v + 1))
                    dve.wait_ge(sem("sp3"), v + 1)
                    for d in range(DT):
                        dve.tensor_tensor(dlt[d][:, ds(b * TIME + CHUNK * h, CHUNK)], sp_relu[:, h, d, :], sp_ln[:, h, d, :],
                                          ALU.add).then_inc(sem("delta"), 1)

            repeat(dve, BATCH, deltas)
            dve.wait_ge(sem("delta"), DT * CHUNKS)
            dve.wait_ge(sem("BCs"), CHUNKS)
            dve.wait_ge(sem("uc"), DT * CHUNKS)
            dve.wait_ge(sem("x_ps"), DT * CHUNKS)
            dve.nop().then_inc(sem("pre_all"), 1)

            def steps_times_u(b):
                for d in range(DT):
                    ins = dve.tensor_tensor(dtu[:, d, :], dlt[d][:, ds(b * TIME, TIME)],
                                            uc[:, d, ds(b, 1), :].rearrange("p a t -> p (a t)"), ALU.mult)
                ins.then_inc(sem("dtu"), 1)

            def scans(b, first, last=False):
                ub = lambda d: uc[:, d, ds(b, 1), :].rearrange("p a t -> p (a t)")
                zb = lambda d: zs[:, d, ds(b, 1), :].rearrange("p a t -> p (a t)")
                if first:
                    steps_times_u(0)

                def scale(u):
                    n = u // DT
                    dve.wait_ge(sem("scan"), 32 * b + u + 1)
                    dve.wait_ge(sem("Cs"), DS * b + n + 1)
                    dve.tensor_tensor(w[:, u % NW, :], w[:, u % NW, :], Cs[:, n % 2, :], ALU.mult).then_inc(sem("hC"), 1)

                for u in range(DT * DS):
                    n, d = u // DT, u % DT
                    dve.wait_ge(sem("dA"), 32 * b + u + 1)
                    dve.wait_ge(sem("dBu"), 32 * b + u + 1)
                    dve.tensor_tensor_scan(w[:, u % NW, :], dA[:, d, :], w[:, u % NW, :], 0.0, ALU.mult, ALU.add)\
                        .then_inc(sem("scan"), 1)
                    scale(u)
                if not last:
                    dve.wait_ge(sem("dBu"), 32 * (b + 1))
                    steps_times_u(b + 1)
                dve.wait_ge(sem("ysum"), 32 * (b + 1))
                for d in range(DT):
                    ins = dve.scalar_tensor_tensor(ub(d), ub(d), D_skip[:, d:d + 1], pbank(4 + 2 * d, 2), ALU.mult, ALU.add)
                ins.then_inc(sem("yD"), 1)
                dve.wait_ge(sem("yD"), b + 1)
                for d in range(DT):
                    ins = dve.tensor_tensor(ub(d), ub(d), zb(d), ALU.mult)
                ins.then_inc(sem("yz"), 1)

            dve.wait_ge(sem("zs"), DT * CHUNKS)
            scans(0, True)
            with dve.Fori(1, BATCH - 1) as i:
                scans(i, False)
            scans(BATCH - 1, False, True)
            for c in range(CHUNKS):
                dve.wait_ge(sem("m_out"), c + 1)
                xb = X[:, 4 * c:4 * (c + 1), :]
                chain(dve.tensor_tensor(xb, xb, pbank(c % 4).rearrange("p (j d) -> p j d", d=D), ALU.add))
                dve.nop().then_inc(sem("m_add"), 1)
                ln_statistics(2, c)
                if c:
                    ln_apply(2, c - 1, (c - 1) % 2)
            ln_apply(2, CHUNKS - 1, 1)
            stage_end(dve, 2)

            experts(1, 2)

            def soft(s, k):
                base = UNITS * s

                def maxima(u, t, r):
                    dve.wait_ge(sem("Lc"), u + 1)
                    if not below(u, RING):
                        dve.wait_ge(sem("Es"), u + 1 - RING)
                    dve.tensor_reduce(mD[:, r, :], Lc[:, r, :].rearrange("p (n q) -> p n q", q=PSLOT), AX, ALU.max)\
                        .then_inc(sem("mD"), 1)
                    dve.tensor_reduce(mxC[:, r % 2, ds(t, 1), :].rearrange("p a q -> p (a q)"),
                                      Lc[:, r, :].rearrange("p (n q) -> p q n", q=PSLOT), AX, ALU.max).then_inc(sem("mxC"), 1)

                def sums(u, r):
                    dve.wait_ge(sem("Ed"), u + 1)
                    dve.tensor_reduce(sD[:, r, :], Ed[:, r, :].rearrange("p (n q) -> p n q", q=PSLOT), AX, ALU.add)\
                        .then_inc(sem("sD"), 1)
                    dve.wait_ge(sem("sD"), u + 1)
                    dve.reciprocal(rD[:, r, :], sD[:, r, :]).then_inc(sem("rD"), 1)

                def units(i):
                    for r in range(RING):
                        u = base + RING * i + r
                        maxima(u, 2 * i + r // 2, r)
                        if not below(RING * i + r, 1):
                            sums(u - 1, (r - 1) % RING)

                dispatch_loop(dve, units)
                sums(base + UNITS - 1, RING - 1)
                dve.wait_ge(sem("slotX"), UNITS * (s + 1))
                for h in range(2):
                    dve.tensor_scalar(slotX[:, HW * h:HW * (h + 1)], pbank(4 + 2 * h, 2), -33000.0, 65000.0,
                                      ALU.max, ALU.min).then_inc(sem("clipped"), 1)
                dve.wait_ge(sem("mxC"), UNITS * (s + 1))
                chain(dve.tensor_tensor(mxC[:, 0, :, :], mxC[:, 0, :, :], mxC[:, 1, :, :], ALU.max))
                chain(dve.tensor_scalar(mCs[:, :, 0:PSLOT], mxC[:, 0, :, :], -1.0, None, ALU.mult))
                dve.scalar_tensor_tensor(mCs[:, :, PSLOT:2 * PSLOT], mxC[:, 0, :, :], -1.0, mCs[:, :, 0:PSLOT],
                                         ALU.mult, ALU.subtract).then_inc(sem("mCs"), 1)
                for h in range(2):
                    dve.wait_ge(sem("slot_m"), 2 * s + h + 1)
                    dve.tensor_tensor(slotA[:, 1024 * h:1024 * (h + 1)], slotX[:, 1024 * h:1024 * (h + 1)], pbank(2 * h, 2),
                                      ALU.subtract).then_inc(sem("slot_c"), 1)
                for h in range(2):
                    dve.wait_ge(sem("slot_r"), 2 * s + h + 1)
                    dve.tensor_tensor(slotA[:, 1024 * h:1024 * (h + 1)], slotA[:, 1024 * h:1024 * (h + 1)],
                                      slotB[:, 1024 * h:1024 * (h + 1)], ALU.mult).then_inc(sem("slot_n"), 1)
                for g in range(4):
                    dve.wait_ge(sem("Yt_ps"), 4 * s + g + 1)
                    if g == 0:
                        dve.wait_ge(sem("we"), 16 * (1 + EPT) * (s + 1))
                    dve.tensor_tensor(Yt[:, 4 * g:4 * (g + 1), :], pbank(4 + g).rearrange("p (s h) -> p s h", h=D),
                                      eb[:, 4 * g:4 * (g + 1), :], ALU.add).then_inc(sem("Yt"), 1)
                stage_end(dve, k + 1)
                base = CHUNKS * s

                def normalise(v, c):
                    dve.wait_ge(sem("Ec"), ST * (v + 1))
                    ec = Ec[:, c, :, :]
                    for j, (dst, lo, hi) in enumerate(((t8, ec[:, 0:8, :], ec[:, 8:16, :]), (t4, t8[:, 0:4, :], t8[:, 4:8, :]),
                                                       (t2, t4[:, 0:2, :], t4[:, 2:4, :]), (t1, t2[:, 0, :], t2[:, 1, :]))):
                        if j:
                            dve.wait_ge(sem("tree"), 4 * v + j)
                        dve.tensor_tensor(dst, lo, hi, ALU.add).then_inc(sem("tree"), 1)
                    dve.wait_ge(sem("Rz"), v + 1)
                    dve.tensor_tensor(ec, ec, Rz.unsqueeze(1).to_broadcast([P, ST, CHUNK]), ALU.mult).then_inc(sem("C"), 1)

                def residual(v, i2, c):
                    dve.wait_ge(sem("y_tok"), v + 1)
                    xb = X[:, ds(8 * i2 + 4 * c, 4), :]
                    dve.scalar_tensor_tensor(xb, pbank(6).rearrange("p (j d) -> p j d", d=D), 0.5, xb, ALU.mult, ALU.add)\
                        .then_inc(sem("s_add"), 1)
                    if s == 0:
                        dve.wait_ge(sem("s_add"), v + 1)
                        ln_statistics(4, 2 * i2 + c)

                normalise(base, 0)
                normalise(base + 1, 1)
                residual(base, 0, 0)

                with dve.Fori(1, CHUNKS // 2) as i:
                    if s == 0:
                        ln_apply(4, 2 * i - 2, 0)
                    normalise(base + 2 * i, 0)
                    residual(base + 2 * i - 1, i - 1, 1)
                    if s == 0:
                        ln_apply(4, 2 * i - 1, 1)
                    normalise(base + 2 * i + 1, 1)
                    residual(base + 2 * i, i, 0)
                residual(base + CHUNKS - 1, CHUNKS // 2 - 1, 1)
                if s == 0:
                    ln_apply(4, CHUNKS - 2, 0)
                    ln_apply(4, CHUNKS - 1, 1)
                stage_end(dve, k + 2)

            soft(0, 3)

            for v in range(HD):
                ins = dve.tensor_copy(Wvv[:, v, :].rearrange("p (h k) -> p h k", k=HD),
                                      Wv[:, :].rearrange("p (h v) -> p h v", v=HD)[:, :, v:v + 1].to_broadcast([P, HEADS, HD]))
            ins.then_inc(sem("Wvv"), 1)

            def gla_in(b, first):
                for h in range(HALVES):
                    v = 2 * b + h
                    for j, (t, c) in enumerate(((q_s, float(HD) ** -0.5), (k_s, 1.0))):
                        dve.wait_ge(sem("qk_sig"), 2 * v + j + 1)
                        dve.scalar_tensor_tensor(t[:, ds(b, 1), CHUNK * h:CHUNK * (h + 1)].rearrange("p a t -> p (a t)"),
                                                 pbank(j), c, sg[:, j, :], ALU.mult, ALU.mult).then_inc(sem("qk"), 1)

            with dve.Fori(0, BATCH) as i:
                gla_in(i, False)
            dve.wait_ge(sem("fg"), 2 * CHUNKS)
            dve.wait_ge(sem("qk"), 2 * CHUNKS)

            def gla(b, first):
                kb = k_s[:, ds(b, 1), :].rearrange("p a t -> p (a t)")
                fb = f_s[:, ds(b, 1), :].rearrange("p a t -> p (a t)")

                def outer(v):
                    n = HD * b + v
                    dve.wait_ge(sem("vb"), n + 1)
                    if not (first and v < NW):
                        dve.wait_ge(sem("osum"), n + 1 - NW)
                    dve.tensor_tensor(kv[:, v % NW, :], kb, pbank(2 * (v % 2), 2), ALU.mult).then_inc(sem("kv"), 1)

                outer(0)
                for v in range(HD):
                    if v + 1 < HD:
                        outer(v + 1)
                    dve.wait_ge(sem("kv"), HD * b + v + 1)
                    dve.tensor_tensor_scan(kv[:, v % NW, :], fb, kv[:, v % NW, :], 0.0, ALU.mult, ALU.add)\
                        .then_inc(sem("kv_scan"), 1)
                dve.wait_ge(sem("osum"), HD * (b + 1))
                dve.tensor_tensor(og[:, ds(b, 1), :].rearrange("p a t -> p (a t)"), g_s[:, ds(b, 1), :].rearrange("p a t -> p (a t)"),
                                  pbank(4, 2), ALU.mult).then_inc(sem("og"), 1)

            repeat(dve, BATCH, gla)
            dve.wait_ge(sem("og"), BATCH)

            def attended(v, h):
                dve.wait_ge(sem("a_out"), v + 1)
                xb = X[:, ds(4 * v, 4), :]
                dve.tensor_tensor(xb, xb, pbank(2 + h).rearrange("p (j d) -> p j d", d=D), ALU.add).then_inc(sem("a_add"), 1)
                dve.wait_ge(sem("a_add"), v + 1)
                ln_statistics(5, v)
                ln_apply(5, v, h)

            def head_norm(b, first):
                for h in range(HALVES):
                    v = 2 * b + h
                    dve.wait_ge(sem("rms"), v + 1)
                    if not (first and v < 2):
                        dve.wait_ge(sem("a_out"), v - 1)
                    dve.scalar_tensor_tensor(nrm[:, h, :], og[:, ds(b, 1), CHUNK * h:CHUNK * (h + 1)].rearrange("p a t -> p (a t)"),
                                             norm_w[:, 0:1], rms[:, 1, :], ALU.mult, ALU.mult).then_inc(sem("nrm"), 1)
                    if not (first and h == 0):
                        attended(v - 1, 1 - h)

            repeat(dve, BATCH, head_norm)
            attended(CHUNKS - 1, 1)
            stage_end(dve, 6)
            soft(1, 6)

        @block.tensor
        def _(pe):
            pe.wait_ge(sem("ones"), 4)
            pe.wait_ge(sem("consts0"), 16 * len(loads[0]))

            def ln_turn(n, c, h, bank):
                v = 8 * n + c
                pe.wait_ge(sem("ln_x"), v + 1)
                if not (isinstance(v, int) and v == 0):
                    pe.wait_ge(sem("ln_XT"), v)
                for j in range(PER_CHUNK):
                    ins = pe.transpose(pbank(bank)[:, P * j:P * (j + 1)], stage[:, h, P * j:P * (j + 1)], ident[:, :])
                ins.then_inc(sem("ln_T"), 1)

            def gates(n, c):
                pe.wait_ge(sem("ln_XT"), 8 * n + c + 1)
                for t in range(PER_CHUNK * c, PER_CHUNK * (c + 1)):
                    b, j = t // PER_BATCH, t % PER_BATCH
                    ins = pe.matmul(pbank(7)[:, E * t:E * (t + 1)], XT[:, b, CONV_PAD + P * j:CONV_PAD + P * (j + 1)], wg[:, :],
                                    start=True, stop=True)
                if c == CHUNKS - 1:
                    ins.then_inc(sem("logits"), 1)

            for c in range(CHUNKS):
                ln_turn(0, c, c % 2, 0)
                if c:
                    gates(0, c - 1)
            gates(0, CHUNKS - 1)
            stage_end(pe, 0)

            def xt(b, h, shift=0):
                return XT[:, ds(b, 1), CONV_PAD + CHUNK * h - shift:CONV_PAD + CHUNK * (h + 1) - shift].rearrange("p a t -> p (a t)")

            def experts(m, k):
                pe.wait_ge(sem("masks"), m + 1)
                mk = mask.rearrange("p a b -> p (a b)")
                pe.matmul(pbank(5), tri[:, :], mk, start=True, stop=True)
                pe.matmul(pbank(6), onesb[:, :], mk, start=True, stop=True).then_inc(sem("counts"), 1)
                base = 16 * m

                def turn(v, c, loaded):
                    pe.wait_ge(sem(f"d_in{c}"), 16 * loaded)
                    if not (isinstance(v, int) and v < 2):
                        pe.wait_ge(sem("dT"), v - 1)
                    for j in range(PER_CHUNK):
                        ins = pe.transpose(pbank(c)[:, P * j:P * (j + 1)], dtile[:, c, j, 0:D], ident[:, :])
                    ins.then_inc(sem("d_T"), 1)

                def layer1(v, c, p):
                    pe.wait_ge(sem("dT"), v + 1)
                    for hb in range(HB):
                        if not (isinstance(v, int) and v == 0):
                            pe.wait_ge(sem("hT_act" if hb % 2 == 0 else "hT_dve"), 2 * v - 1 + hb // 2)
                        pe.matmul(pbank(2 + hb), w1s[:, p, P * hb:P * (hb + 1)], dT[:, c, :], start=True, stop=True)\
                            .then_inc(sem("l1"), 1)

                def layer2(v, c, p):
                    pe.wait_ge(sem("hT_act"), 2 * (v + 1))
                    pe.wait_ge(sem("hT_dve"), 2 * (v + 1))
                    if not (isinstance(v, int) and v < 2):
                        pe.wait_ge(sem("y_out"), v - 1)
                    for j in range(PER_CHUNK):
                        for hb in range(HB):
                            ins = pe.matmul(pbank(6 + c)[:, P * j:P * (j + 1)], hT[:, c, hb, P * j:P * (j + 1)], w2s[:, p, hb, :],
                                            start=(hb == 0), stop=(hb == HB - 1))
                    ins.then_inc(sem("l2"), 1)

                pe.wait_ge(sem("slots"), m + 1)
                turn(base, 0, 8 * m + 1)

                def chunks(i, first, last=False):
                    for p in range(2):
                        for c in range(EC):
                            v = base + 4 * i + 2 * p + c
                            if c == 0:
                                pe.wait_ge(sem(f"w_in{p}"), 32 * (4 * m + i + 1))
                            layer1(v, c, p)
                            if not (last and p == 1 and c == 1):
                                turn(v + 1, 1 - c, 8 * m + 2 * i + p + 1 + c)
                            if not (first and p == 0 and c == 0):
                                layer2(v - 1, 1 - c, p if c == 1 else 1 - p)

                chunks(0, True)
                with pe.Fori(1, E // 2 - 1) as i:
                    chunks(i, False)
                chunks(E // 2 - 1, False, True)
                layer2(base + 15, 1, 1)
                for c in range(CHUNKS):
                    ln_turn(2 * m + 1, c, c % 2, 0)
                stage_end(pe, k + 1)

            experts(0, 0)


            def project(b, first):
                for h in range(HALVES):
                    v = 2 * b + h
                    for d in range(DT):
                        if not (first and h == 0):
                            pe.wait_ge(sem("u_sb"), DT * (v - 1) + d + 1)
                        pe.matmul(pbank(d), W_in[:, P * d:P * (d + 1)], xt(b, h), start=True, stop=True).then_inc(sem("u_ps"), 1)
                    for d in range(DT):
                        if not (first and h == 0):
                            pe.wait_ge(sem("zs"), DT * (v - 1) + d + 1)
                        pe.matmul(pbank(2 + d), W_in[:, DI + P * d:DI + P * (d + 1)], xt(b, h), start=True, stop=True)\
                            .then_inc(sem("z_ps"), 1)
                    if not (first and h == 0):
                        low_rank(v - 1, b if h else b - 1, 1 - h)

            def low_rank(v, b, h):
                pe.wait_ge(sem("uc"), DT * (v + 1))
                if not below(v, 2):
                    pe.wait_ge(sem("bc_rest"), v - 1)
                for d in range(DT):
                    ins = pe.matmul(pbank(6 + h)[0:96 + RANK, :], W_bc3[:, d, :],
                                    uc[:, d, ds(b, 1), CHUNK * h:CHUNK * (h + 1)].rearrange("p a t -> p (a t)"),
                                    start=(d == 0), stop=(d == DT - 1))
                ins.then_inc(sem("bc_ps"), 1)

            repeat(pe, BATCH, project)
            low_rank(CHUNKS - 1, BATCH - 1, 1)

            pe.wait_ge(sem("u_sb"), DT * CHUNKS)
            pe.wait_ge(sem("zs"), DT * CHUNKS)

            def steps(b, first):
                for h in range(HALVES):
                    v = 2 * b + h
                    hold(pe, sem("dts"), 2 * (v + 1))
                    for d in range(DT):
                        if not first:
                            hold(pe, sem("relu"), DT * (v - 2) + d + 1)
                        pe.matmul(pbank(DT * h + d), W_dt[:, P * d:P * (d + 1)],
                                  dts[0:RANK, ds(b, 1), CHUNK * h:CHUNK * (h + 1)].rearrange("p a t -> p (a t)"),
                                  start=True, stop=True).then_inc(sem("x_ps"), 1)

            repeat(pe, BATCH, steps)
            pe.wait_ge(sem("pre_all"), 1)

            def spread(v, b, n, early):
                for q, name in enumerate(("Bs", "Cs")):
                    if not early:
                        pe.wait_ge(sem(name), v)
                    for h in range(HALVES):
                        ins = pe.matmul(pbank(2 * q + h), row32[:, DS * q + n:DS * q + n + 1].to_broadcast([96, P]),
                                        BCs[0:96, ds(b * TIME + CHUNK * h, CHUNK)], start=True, stop=True)
                ins.then_inc(sem("bc"), 1)

            def scans(b, first, last=False):
                def add(u):
                    n, d = u // DT, u % DT
                    pe.wait_ge(sem("hC"), 32 * b + u + 1)
                    if u == 0 and not first:
                        pe.wait_ge(sem("yD"), b)
                    for h in range(HALVES):
                        ins = pe.matmul(pbank(4 + 2 * d + h), ident[:, :], w[:, u % NW, CHUNK * h:CHUNK * (h + 1)],
                                        start=(n == 0), stop=(n == DS - 1))
                    ins.then_inc(sem("ysum"), 1)

                for n in range(DS):
                    v = DS * b + n + 2
                    if n + 2 < DS:
                        spread(v, b, n + 2, False)
                    elif not last:
                        spread(v, b + 1, n + 2 - DS, False)
                    for d in range(DT):
                        add(DT * n + d)

            spread(0, 0, 0, True)
            spread(1, 0, 1, False)
            scans(0, True)
            with pe.Fori(1, BATCH - 1) as i:
                scans(i, False)
            scans(BATCH - 1, False, True)
            pe.wait_ge(sem("yz"), BATCH)
            for c in range(CHUNKS):
                if c >= 4:
                    pe.wait_ge(sem("m_add"), c - 3)
                for j in range(PER_CHUNK):
                    t = PER_CHUNK * c + j
                    at = P * (t % PER_BATCH)
                    for d in range(DT):
                        ins = pe.matmul(pbank(c % 4)[:, P * j:P * (j + 1)], uc[:, d, t // PER_BATCH, at:at + P], W_out[:, d, :],
                                        start=(d == 0), stop=(d == DT - 1))
                ins.then_inc(sem("m_out"), 1)
                if c > 1:
                    ln_turn(2, c - 2, c % 2, 6)
                if c > 2:
                    gates(2, c - 3)
            for c in range(CHUNKS - 3, CHUNKS):
                if c > CHUNKS - 3:
                    ln_turn(2, c, c % 2, 6)
                gates(2, c)
            stage_end(pe, 2)

            experts(1, 2)

            def soft(s, k):
                base = UNITS * s

                def logits(u, t, r):
                    h = r % 2
                    if h == 0:
                        pe.wait_ge(sem("xts"), TILES * s + t + 1)
                    if not below(u, 2):
                        pe.wait_ge(sem("Lc"), u - 1)
                    for c in range(2):
                        at = HW * h + CHUNK * c
                        pe.matmul(pbank(2 * h + c), xts[:, r // 2, :], phiT[:, at:at + CHUNK], start=True, stop=False)
                        ins = pe.matmul(pbank(2 * h + c), onesb[0:3, :], phi_b3[:, at:at + CHUNK], start=False, stop=True)
                    ins.then_inc(sem("L"), 1)

                def gather(u, t, r, start, stop):
                    h = r % 2
                    pe.wait_ge(sem("Dd"), u + 1)
                    if h == 0:
                        pe.wait_ge(sem("xns"), TILES * s + t + 1)
                    for c in range(2):
                        ins = pe.matmul(pbank(4 + 2 * h + c), xns[:, r // 2, :], Dd[:, r, CHUNK * c:CHUNK * (c + 1)],
                                        start=start, stop=stop, skip_group_check=True)
                    ins.then_inc(sem("slotX"), 1)

                def units(i):
                    for r in range(RING):
                        u = base + RING * i + r
                        t = 2 * i + r // 2
                        logits(u, t, r)
                        if not below(i, 1):
                            gather(u - RING, t - 2, r, below(t - 2, 1), False)

                dispatch_loop(pe, units)
                for r in range(RING):
                    gather(base + UNITS - RING + r, TILES - 2 + r // 2, r, False, r >= 2)
                pe.wait_ge(sem("mCs"), s + 1)
                for g in range(4):
                    if g > 1:
                        pe.wait_ge(sem("mCT"), 4 * s + g - 1)
                    for j in range(8):
                        ins = pe.transpose(pbank(g % 2).bitcast(BF16)[0:64, P * j:P * (j + 1)], mCs[:, 8 * g + j, :], identb[:, :])
                    ins.then_inc(sem("mCT_ps"), 1)
                pe.wait_ge(sem("mCT"), 4 * (s + 1))
                pe.wait_ge(sem("clipped"), 2 * (s + 1))
                for h in range(2):
                    for c in range(2):
                        at = 1024 * h + CHUNK * c
                        ins = pe.matmul(pbank(2 * h + c), mean_w[:, :], slotX[:, at:at + CHUNK], start=True, stop=True)
                    ins.then_inc(sem("slot_m"), 1)
                for h in range(2):
                    pe.wait_ge(sem("slot_sq"), 2 * s + h + 1)
                    for c in range(2):
                        at = 1024 * h + CHUNK * c
                        ins = pe.matmul(pbank(4 + 2 * h + c), mean_w[:, :], slotB[:, at:at + CHUNK], start=True, stop=True)
                    ins.then_inc(sem("slot_v"), 1)
                pe.wait_ge(sem("slot_r"), 2 * (s + 1))
                pe.wait_ge(sem("we"), 16 * (1 + EPT) * (s + 1))
                for g in range(4):
                    pe.wait_ge(sem("slot_t"), 2 * s + g // 2 + 1)
                    for t in range(4):
                        for j in range(EPT):
                            n = EPT * (4 * g + t) + j
                            ins = pe.matmul(pbank(4 + g)[PSLOT * j:PSLOT * (j + 1), P * t:P * (t + 1)],
                                            slotA[:, PSLOT * n:PSLOT * (n + 1)], We[:, n, :], start=True, stop=True,
                                            skip_group_check=True)
                    ins.then_inc(sem("Yt_ps"), 1)
                stage_end(pe, k + 1)
                base = CHUNKS * s

                def logits_T(v, b, c, early):
                    for t in range(ST):
                        if not (early and t < 4):
                            pe.wait_ge(sem("Ec"), ST * v + t - 3)
                        pe.matmul(pbank(t % 4), phiT[:, P * t:P * (t + 1)], xt(b, c), start=True, stop=False)
                        pe.matmul(pbank(t % 4), row128[:, :],
                                  mCT[0:64, ds(b * TIME + CHUNK * c, CHUNK)], start=False, stop=True).then_inc(sem("LT"), 1)

                def total(v):
                    pe.wait_ge(sem("tree"), 4 * (v + 1))
                    pe.matmul(pbank(4), same_p[:, :], t1, start=True, stop=True).then_inc(sem("Z"), 1)

                def combine(v, c, early):
                    pe.wait_ge(sem("C"), v + 1)
                    if not early:
                        pe.wait_ge(sem("yT"), v)
                    for t in range(ST):
                        ins = pe.matmul(pbank(5), Yt[:, t, :], Ec[:, c, t, :], start=(t == 0), stop=(t == ST - 1))
                    ins.then_inc(sem("yT_ps"), 1)

                def turn_y(v, early):
                    pe.wait_ge(sem("yT"), v + 1)
                    if not early:
                        pe.wait_ge(sem("s_add"), v)
                    for j in range(PER_CHUNK):
                        ins = pe.transpose(pbank(6)[:, P * j:P * (j + 1)], yT[:, P * j:P * (j + 1)], ident[:, :])
                    ins.then_inc(sem("y_tok"), 1)

                e0 = s == 0
                logits_T(base, 0, 0, True)
                total(base)
                logits_T(base + 1, 0, 1, False)
                combine(base, 0, e0)
                total(base + 1)
                turn_y(base, e0)

                with pe.Fori(1, CHUNKS // 2) as i:
                    for c in range(2):
                        v = base + 2 * i + c
                        logits_T(v, i, c, False)
                        if s == 0:
                            ln_turn(4, 2 * (i - 1) + c, c, 7)
                        combine(v - 1, 1 - c, False)
                        total(v)
                        turn_y(v - 1, False)
                combine(base + CHUNKS - 1, 1, False)
                turn_y(base + CHUNKS - 1, False)
                if s == 0:
                    for c in range(2):
                        ln_turn(4, CHUNKS - 2 + c, c, 7)
                stage_end(pe, k + 2)

            soft(0, 3)

            def gla_in(b, first):
                for h in range(HALVES):
                    v = 2 * b + h
                    if not (first and h == 0):
                        pe.wait_ge(sem("low"), 2 * v)
                    pe.matmul(pbank(2)[0:HD, :], Wf1[:, :], xt(b, h), start=True, stop=True)
                    pe.matmul(pbank(3)[0:HD, :], Wg1[:, :], xt(b, h), start=True, stop=True).then_inc(sem("low_ps"), 1)
                    for j, W in enumerate((Wq, Wk)):
                        if not (first and h == 0):
                            pe.wait_ge(sem("qk"), 2 * (v - 1) + j + 1)
                        pe.matmul(pbank(j), W[:, :], xt(b, h), start=True, stop=True).then_inc(sem("qk_ps"), 1)
                    pe.wait_ge(sem("low"), 2 * (v + 1))
                    for j, W in enumerate((Wf2, Wg2)):
                        if not (first and h == 0):
                            pe.wait_ge(sem("fg"), 2 * (v - 1) + j + 1)
                        pe.matmul(pbank(4 + j), W[:, :], low[0:HD, j, :], start=True, stop=True).then_inc(sem("fg_ps"), 1)

            repeat(pe, BATCH, gla_in)
            pe.wait_ge(sem("fg"), 2 * CHUNKS)
            pe.wait_ge(sem("qk"), 2 * CHUNKS)

            def gla(b, first):
                def values(v):
                    n = HD * b + v
                    if not (first and v < 2):
                        pe.wait_ge(sem("kv"), n - 1)
                    if v == 0 and first:
                        pe.wait_ge(sem("Wvv"), 1)
                    for h in range(HALVES):
                        ins = pe.matmul(pbank(2 * (v % 2) + h), Wvv[:, v, :], xt(b, h), start=True, stop=True)
                    ins.then_inc(sem("vb"), 1)

                def add(v):
                    if v == 0 and first:
                        pe.wait_ge(sem("head_sum"), 16)
                    pe.wait_ge(sem("qS"), HD * b + v + 1)
                    if v == 0 and not first:
                        pe.wait_ge(sem("og"), b)
                    for h in range(HALVES):
                        ins = pe.matmul(pbank(4 + h), head_sum[:, v, :], kv[:, v % NW, CHUNK * h:CHUNK * (h + 1)],
                                        start=(v == 0), stop=(v == HD - 1))
                    ins.then_inc(sem("osum"), 1)

                values(0)
                values(1)
                for v in range(HD):
                    if v + 2 < HD:
                        values(v + 2)
                    add(v)

            repeat(pe, BATCH, gla)

            def mean_square(v, h, early):
                pe.wait_ge(sem("sq"), v + 1)
                if not early:
                    pe.wait_ge(sem("rms0"), v - 1)
                pe.matmul(pbank(h), head_mean[:, :], sq[:, h, :], start=True, stop=True).then_inc(sem("ms"), 1)

            def head_norm(b, first, last=False):
                for h in range(HALVES):
                    v = 2 * b + h
                    if not (last and h == 1):
                        mean_square(v + 1, 1 - h, first and h == 0)
                    pe.wait_ge(sem("nrm"), v + 1)
                    if not first:
                        pe.wait_ge(sem("a_add"), v - 1)
                    for j in range(PER_CHUNK):
                        ins = pe.matmul(pbank(2 + h)[:, P * j:P * (j + 1)], nrm[:, h, P * j:P * (j + 1)], Wo[:, :],
                                        start=True, stop=True)
                    ins.then_inc(sem("a_out"), 1)
                    if not (first and h == 0):
                        ln_turn(5, v - 1, 1 - h, 7)

            mean_square(0, 0, True)
            head_norm(0, True)
            with pe.Fori(1, BATCH - 1) as i:
                head_norm(i, False)
            head_norm(BATCH - 1, False, True)
            ln_turn(5, CHUNKS - 1, 1, 7)
            stage_end(pe, 6)
            soft(1, 6)


def constants():
    i = np.arange(P)
    f = np.float32
    hs = np.zeros((P, HD, P), f)
    for v in range(HD):
        for h in range(HEADS):
            hs[h * HD:(h + 1) * HD, v, h * HD + v] = 1.0
    return {
        "k_ident": np.eye(P, dtype=f),
        "k_tri": (i[:, None] <= i[None, :]).astype(f),
        "k_row_id": (K * np.arange(TOKENS).reshape(TILES, P).T + 1).astype(f),
        "k_rev": np.broadcast_to(np.arange(E, 0, -1).astype(f), (P, E)).copy(),
        "k_row32": (np.arange(96)[:, None] % 32 == np.arange(32)[None, :]).astype(f),
        "k_same_p": (i[:, None] % PSLOT == i[None, :] % PSLOT).astype(f),
        "k_head_mean": (i[:, None] // HD == i[None, :] // HD).astype(f) / HD,
        "k_head_sum": hs,
    }


def kernel(**inputs):
    import concourse.bacc as bacc
    from concourse.bass_utils import run_bass_kernel_spmd

    arr = {k: np.ascontiguousarray(v) for k, v in inputs.items()}
    col = lambda v: np.ascontiguousarray(v.reshape(-1, P).T)
    arrays = {k: arr[k] for k in (
        "L0_attn_x", "L0_attn_W_in", "L0_attn_conv_w", "L0_attn_W_xproj", "L0_attn_W_dt", "L0_attn_A_log", "L0_attn_W_out", "L0_ffn_wg",
        "L0_ffn_w1", "L0_ffn_w2", "L0_ffn_b2", "L1_attn_Wq", "L1_attn_Wk", "L1_attn_Wv", "L1_attn_Wo", "L1_attn_Wf1",
        "L1_attn_Wf2", "L1_attn_Wg1", "L1_attn_Wg2", "L1_ffn_phi_b", "L1_ffn_expert_w", "L1_ffn_expert_b")}
    arrays["h_b1"] = np.ascontiguousarray(arr["L0_ffn_b1"].reshape(E, HB, P).transpose(2, 0, 1))
    arrays["h_conv_b"] = col(arr["L0_attn_conv_b"])
    arrays["h_b_dt"] = col(arr["L0_attn_b_dt"])
    arrays["h_D"] = col(arr["L0_attn_D"])
    arrays["h_phi_wT"] = np.ascontiguousarray(arr["L1_ffn_phi_w"].T)
    arrays["h_phi_b"] = col(arr["L1_ffn_phi_b"])
    arrays["h_norm_w"] = col(arr["L1_attn_norm_weight"])
    arrays.update(constants())

    nc = bacc.Bacc("TRN2", target_bir_lowering=False, num_devices=1)
    a, named = {}, {}
    for name, v in arrays.items():
        named["in_" + name] = v
        a[name] = nc.dram_tensor("in_" + name, v.shape, mybir.dt.from_np(v.dtype), kind="ExternalInput").ap()
    out = nc.dram_tensor("out_x", (BATCH, TIME, D), F32, kind="ExternalOutput").ap()
    disp = [nc.dram_tensor(f"slot_inputs{m}", (SLOTS, ROW), F32, kind="Internal").ap() for m in range(2)]
    ytok = [nc.dram_tensor(f"token_outputs{m}", (K * TOKENS, D), F32, kind="Internal").ap() for m in range(2)]
    build(nc, a, out, disp, ytok)
    r = run_bass_kernel_spmd(nc, [named], core_ids=[0])
    return r.results[0]["out_x"]
```

```python
from contextlib import ExitStack

import numpy as np

import concourse.bass as bass
from concourse import mybir

F32 = mybir.dt.float32
BF16 = mybir.dt.bfloat16
U32 = mybir.dt.uint32
ALU = mybir.AluOpType
ACT = mybir.ActivationFunctionType
AX = mybir.AxisListType.X

P = 128
CHUNK = 512
EPS = 1e-5
LOWEST = -3.0e38

BATCH, TIME, D = 4, 1024, 128
TOKENS = BATCH * TIME
TILES = TOKENS // P
PER_BATCH = TIME // P
HALVES = TIME // CHUNK
CHUNKS = TOKENS // CHUNK
PER_CHUNK = CHUNK // P
E, K, H = 8, 2, 512
HB = H // P
CAP = K * (TOKENS // E)
SLOTS = E * CAP
ROW = D + 1
EC = CAP // CHUNK
FAR = float(1 << 20)
DI, DS, DCONV, RANK = 256, 16, 4, 8
DT = DI // P
CONV_PAD = DCONV - 1
HEADS, HD = 16, 8
NEXP, PSLOT = 64, 32
SOFT = NEXP * PSLOT
ST = SOFT // P
EPT = P // PSLOT
NH = NEXP // 2
UNITS = 2 * TILES
RING = 4
HW = SOFT // 2
GROUP = 4
PUT = 8
ENGINES = 5
KEPT = (0, 2, 3, 5)


def build(nc, a, out, disp, ytok):
    with ExitStack() as ctx:
        def sb(name, shape, dt=F32):
            return ctx.enter_context(nc.sbuf_tensor(name, shape, dt))

        sems = {}

        def sem(name):
            if name not in sems:
                sems[name] = ctx.enter_context(nc.semaphore(name))
            return sems[name]

        def ds(start, size):
            return bass.ds(start, size)

        def repeat(eng, n, body):
            body(0, True)
            with eng.Fori(1, n) as i:
                body(i, False)

        X = sb("X", [P, TILES, D])
        XN = sb("XN", [P, TILES, ROW])
        XT = sb("XT", [P, BATCH, CONV_PAD + TIME])
        ps = ctx.enter_context(nc.psum_tensor("ps", [P, 8, CHUNK], F32))

        loads = [[], []]

        def resident(name, shape, src, dt=F32):
            t = sb("c_" + name, shape, dt)
            full = t[tuple(slice(None) for _ in shape)]
            loads[name not in ("ident", "rev", "wg", "row_id")].append((full, src))
            return t

        ident = resident("ident", [P, P], a["k_ident"])
        rev = resident("rev", [P, E], a["k_rev"])
        row_id = resident("row_id", [P, TILES], a["k_row_id"])
        wg = resident("wg", [P, E], a["L0_ffn_wg"])
        b1 = resident("b1", [P, E, HB], a["h_b1"])
        b2 = resident("b2", [P, E, D], a["L0_ffn_b2"].partition_broadcast(P))
        W_in = resident("W_in", [P, 2 * DI], a["L0_attn_W_in"])
        conv_w = resident("conv_w", [P, DT, DCONV], a["L0_attn_conv_w"].rearrange("(k p) n -> p k n", p=P))
        conv_b = resident("conv_b", [P, DT], a["h_conv_b"])
        W_x = resident("W_x", [P, DT, RANK + 2 * DS], a["L0_attn_W_xproj"].rearrange("(k p) n -> p k n", p=P))
        W_dt = resident("W_dt", [RANK, DI], a["L0_attn_W_dt"])
        b_dt = resident("b_dt", [P, DT], a["h_b_dt"])
        A_log = resident("A_log", [P, DT, DS], a["L0_attn_A_log"].rearrange("(k p) n -> p k n", p=P))
        D_skip = resident("D_skip", [P, DT], a["h_D"])
        W_out = resident("W_out", [P, DT, D], a["L0_attn_W_out"].rearrange("(k p) n -> p k n", p=P))
        phiT = resident("phiT", [P, SOFT], a["h_phi_wT"])
        phi_bc = resident("phi_bc", [P, ST], a["h_phi_b"])
        same_p = resident("same_p", [P, P], a["k_same_p"])
        Wq = resident("Wq", [P, D], a["L1_attn_Wq"])
        Wk = resident("Wk", [P, D], a["L1_attn_Wk"])
        Wv = resident("Wv", [P, D], a["L1_attn_Wv"])
        Wo = resident("Wo", [P, D], a["L1_attn_Wo"])
        Wf1 = resident("Wf1", [P, HD], a["L1_attn_Wf1"])
        Wg1 = resident("Wg1", [P, HD], a["L1_attn_Wg1"])
        Wf2 = resident("Wf2", [HD, D], a["L1_attn_Wf2"])
        Wg2 = resident("Wg2", [HD, D], a["L1_attn_Wg2"])
        norm_w = resident("norm_w", [P, 1], a["h_norm_w"])
        head_mean = resident("head_mean", [P, P], a["k_head_mean"])

        tri = sb("tri", [P, P], BF16)
        identb = sb("identb", [P, P], BF16)
        row32 = sb("row32", [96, 32], BF16)
        onesb = sb("onesb", [P, P], BF16)
        mean_w = sb("mean_w", [P, P])
        ones64 = sb("ones64", [P, K * TILES])
        eps = sb("eps", [P, 1])
        zero = sb("zero", [P, ROW])
        diag_D = sb("diag_D", [P, DT, P])
        W_bc3 = sb("W_bc3", [P, DT, 96 + RANK])
        A_neg = sb("A_neg", [P, DT, DS])
        phi_b3 = sb("phi_b3", [3, SOFT], BF16)
        row128 = sb("row128", [64, P], BF16)

        stats = sb("stats", [P, TILES, 6])
        ln_s = sb("ln_s", [P, 9, TILES])
        stage = sb("stage", [P, HALVES, CHUNK])

        ARENA = 120 * 256
        arena = sb("arena", [P, ARENA])

        class Cut:
            def __init__(self):
                self.at = 0

            def __call__(self, shape, dt=F32):
                n = int(np.prod(shape))
                words = n if dt != BF16 else (n + 1) // 2
                words = (words + 7) // 8 * 8
                assert self.at + words <= ARENA, (self.at + words, ARENA)
                t = arena[:, self.at:self.at + words]
                self.at += words
                if dt != F32:
                    t = t.bitcast(dt)
                t = t[:, 0:n]
                if len(shape) == 2:
                    t = t.rearrange("p (a b) -> p a b", b=shape[1])
                if len(shape) == 3:
                    t = t.rearrange("p (a b c) -> p a b c", b=shape[1], c=shape[2])
                return t

        cut = Cut()
        cut.at = ARENA - 9 * SOFT // 2 - 2 * D
        setup_at = cut.at
        phi_b3f, row, rest, acc = (cut([SOFT])[0:3, :] for _ in range(4))
        part = cut([SOFT], BF16)[0:3, :]
        tri_f = cut([P])
        row32_f = cut([32])[0:96, :]
        loads[0].append((tri_f, a["k_tri"]))
        loads[1].append((row32_f, a["k_row32"]))
        loads[1].append((phi_b3f, a["L1_ffn_phi_b"].partition_broadcast(3)))

        cut = Cut()
        w1s = cut([2, H])
        w2s = cut([2, HB, D])
        dtile = cut([EC, PER_CHUNK, ROW])
        dT = cut([EC, CHUNK])
        hT = cut([EC, HB, CHUNK])
        yo = cut([EC, PER_CHUNK, D])
        yg = cut([TILES, K, D])
        g8 = [cut([TILES, E]) for _ in range(3)]
        g1 = [cut([TILES]) for _ in range(10)]
        mask = cut([K, TILES * E], BF16)
        run = [cut([K * TILES * E]) for _ in range(3)]
        g64 = [cut([K * TILES]) for _ in range(8)]
        gate = cut([K, TILES])
        rank = cut([K, TILES])
        put_at = cut([K * TILES], U32)
        empty = cut([PER_CHUNK])
        y_at = cut([EC * PER_CHUNK], U32)
        assert cut.at <= setup_at, (cut.at, setup_at)

        cut = Cut()
        uc = cut([DT, BATCH, TIME])
        zs = cut([DT, BATCH, TIME])
        delta = XN[:, :, :].rearrange("p a b -> p (a b)")[:, 0:BATCH * TIME]
        delta2 = cut([BATCH * TIME])
        BCs = cut([TOKENS], BF16)
        pre = cut.at
        sp_ln = cut([2, DT, CHUNK])
        sp_relu = cut([2, DT, CHUNK])
        dts = cut([BATCH, TIME])
        cut.at = pre
        bcf = cut([CHUNK])
        bcm = cut([CHUNK], BF16)
        u_pad = delta[:, 0:DT * (CONV_PAD + TIME)].rearrange("p (d t) -> p d t", d=DT)
        cacc = delta[:, 2560:2560 + DT * CHUNK].rearrange("p (d t) -> p d t", d=DT)
        cut.at = pre
        dtu = XT[:, 0:DT, CONV_PAD:]
        Bs = XT[:, DT:DT + 2, CONV_PAD:]
        Cs = cut([2, TIME])
        NW = 4
        dA = cut([DT, TIME])
        w = cut([NW, TIME])
        dlt = [delta, delta2]

        cut = Cut()
        q_s = cut([BATCH, TIME])
        k_s = cut([BATCH, TIME])
        f_s = cut([BATCH, TIME])
        g_s = cut([BATCH, TIME])
        og = cut([BATCH, TIME])
        sg = cut([2, CHUNK])
        low = cut([2, CHUNK])
        sq, rms = sg, low
        kv = cut([NW, TIME])
        nrm = cut([2, CHUNK])
        head_sum = cut([HD, P])
        Wvv = cut([HD, P])

        cut = Cut()
        We = cut([NEXP, D])
        Yt = cut([ST, D])
        mCT = cut([TOKENS], BF16)
        lnz = cut([CHUNK])
        yT = cut([CHUNK])
        combine_at = cut.at
        eb = cut([ST, D])
        slots_at = cut.at
        slotX = cut([SOFT])
        slotA = cut([SOFT])
        slotB = cut([SOFT])
        assert cut.at - combine_at == ST * CHUNK
        cut.at = combine_at
        Ec_odd = cut([ST, CHUNK])
        Ec = [cut([ST, CHUNK]), Ec_odd]
        cut.at = NEXP * D
        Lc = cut([RING, HW])
        xts = cut([2, P])
        xns = cut([2, P])
        assert cut.at <= combine_at
        cut.at = slots_at
        Ed = cut([RING, HW])
        Dd = cut([RING, HW])
        mD = cut([RING, NH])
        sD = cut([RING, NH])
        rD = cut([RING, NH])
        mxC = cut([2, TILES, PSLOT])
        mCs = cut([TILES, 2 * PSLOT], BF16)
        flat = arena[:, 0:NEXP * D]
        t8 = flat[:, 0:4096].rearrange("p (a b) -> p a b", b=CHUNK)
        t4 = flat[:, 4096:6144].rearrange("p (a b) -> p a b", b=CHUNK)
        t2 = flat[:, 6144:7168].rearrange("p (a b) -> p a b", b=CHUNK)
        t1 = flat[:, 7168:7680]
        Rz = flat[:, 7680:8192]

        def pbank(i, n=1):
            return ps[:, i, :] if n == 1 else ps[:, i:i + n, :].rearrange("p a b -> p (a b)")

        def over(t, n):
            return t.unsqueeze(2).to_broadcast([t.shape[0], t.shape[1], n])

        def below(i, n):
            return isinstance(i, int) and i < n

        def dispatch_loop(eng, units):
            units(0)
            units(1)
            with eng.Fori(2, UNITS // RING - 1) as i:
                units(i)
            units(UNITS // RING - 1)

        def stage_end(eng, k):
            eng.drain().then_inc(sem("stage"), 1)
            eng.wait_ge(sem("stage"), ENGINES * (k + 1))

        def hold(eng, s, value):
            eng.wait_ge(s, value)
            if not isinstance(value, int):
                eng.nop(nofuse=True)

        def tap(d, h, j):
            return u_pad[:, d, CHUNK * h + j:CHUNK * (h + 1) + j]

        class Chain:

            def __init__(self, eng, name):
                self.eng, self.sem, self.n = eng, sem(name), 0

            def __call__(self, ins):
                self.n += 1
                ins.then_inc(self.sem, 1)
                self.eng.wait_ge(self.sem, self.n)

        block = ctx.enter_context(nc.Block())

        @block.sync
        def _(sp_):
            for b in range(BATCH):
                sp_.dma_start(X[:, PER_BATCH * b:PER_BATCH * (b + 1), :],
                              a["L0_attn_x"][b].rearrange("(j p) d -> p j d", p=P)).then_inc(sem(f"x_in{b}"), 16)
            for dst, src in loads[0]:
                sp_.dma_start(dst, src).then_inc(sem("consts0"), 16)

            def clear(m):
                for t, name in ((disp[m], "disp_zero"), (ytok[m], "ytok_zero")):
                    width = t.shape[1]
                    sp_.dma_start(t.rearrange("(p a) d -> p a d", p=P),
                                  zero[:, 0:width].unsqueeze(1).to_broadcast([P, SLOTS // P, width])).then_inc(sem(name), 16)

            sp_.wait_ge(sem("zeroed"), 1)
            clear(0)
            for dst, src in loads[1]:
                sp_.dma_start(dst, src).then_inc(sem("consts1"), 16)
            stage_end(sp_, 0)

            def experts(m, k):
                dsp = disp[m].rearrange("(e c j p) d -> p (e c) j d", c=EC, j=PER_CHUNK, p=P)

                def weights(e, b):
                    sp_.dma_start(w1s[:, b, :], a["L0_ffn_w1"][ds(e, 1), :, :].rearrange("a d h -> (a d) h"))\
                        .then_inc(sem(f"w_in{b}"), 16)
                    sp_.dma_start(w2s[:, b, :, :], a["L0_ffn_w2"][ds(e, 1), :, :].rearrange("a (k p) d -> p (a k) d", p=P))\
                        .then_inc(sem(f"w_in{b}"), 16)

                weights(0, 0)
                weights(1, 1)
                for g in range(TILES // PUT):
                    sp_.wait_ge(sem(f"put{g}"), 16 * K * PUT * (m + 1))

                def pair(i, first, last=False):
                    for p in range(2):
                        for c in range(EC):
                            if not (first and p == 0):
                                sp_.wait_ge(sem("d_T"), 16 * m + 4 * i + 2 * p + c - 1)
                                sp_.wait_ge(sem("y_at"), 16 * m + 4 * i + 2 * p + c - 1)
                            sp_.dma_start(dtile[:, c, :, :], dsp[:, ds(4 * i + 2 * p + c, 1), :, :].rearrange("p a j d -> p (a j) d"))\
                                .then_inc(sem(f"d_in{c}"), 16)
                        if not (first and p == 0) and not (last and p == 1):
                            sp_.wait_ge(sem("l2"), 16 * m + 4 * i + 2 * p)
                            weights(2 * i + p + 1, 1 - p)

                pair(0, True)
                with sp_.Fori(1, E // 2 - 1) as i:
                    pair(i, False)
                pair(E // 2 - 1, False, True)
                for c in range(EC):
                    sp_.wait_ge(sem(f"y_put{c}"), 16 * PER_CHUNK * E * (m + 1))
                yv = ytok[m].rearrange("(t p q) d -> p t q d", p=P, q=K)
                for g in range(TILES // GROUP):
                    sp_.dma_start(yg[:, GROUP * g:GROUP * (g + 1), :, :], yv[:, GROUP * g:GROUP * (g + 1), :, :])\
                        .then_inc(sem(f"got{g}"), 16)
                stage_end(sp_, k + 1)

            experts(0, 0)
            clear(1)
            stage_end(sp_, 2)
            experts(1, 2)

            def soft(k, last=False):
                sp_.dma_start(We, a["L1_ffn_expert_w"].rearrange("n d h -> d n h")).then_inc(sem("we"), 16)
                ebs = a["L1_ffn_expert_b"].rearrange("(s j) h -> j s h", j=EPT)
                for j in range(EPT):
                    sp_.dma_start(eb[PSLOT * j:PSLOT * (j + 1), :, :], ebs[j].partition_broadcast(PSLOT))\
                        .then_inc(sem("we"), 16)
                if not last:
                    stage_end(sp_, k + 1)

            soft(3)
            sp_.dma_start(head_sum, a["k_head_sum"]).then_inc(sem("head_sum"), 16)
            stage_end(sp_, 5)
            soft(5, True)
            for c in range(CHUNKS):
                sp_.wait_ge(sem("s_add"), CHUNKS + c + 1)
                sp_.dma_start(out.rearrange("b (j p) d -> p (b j) d", p=P)[:, 4 * c:4 * (c + 1), :], X[:, 4 * c:4 * (c + 1), :])\
                    .then_inc(sem("x_out"), 16)
            sp_.wait_ge(sem("x_out"), 16 * CHUNKS)

        @block.gpsimd
        def _(pool):
            pool.memset(onesb[:, :], 1.0).then_inc(sem("ones"), 1)
            pool.memset(mean_w[:, :], 1.0 / P).then_inc(sem("ones"), 1)
            pool.memset(ones64[:, :], 1.0).then_inc(sem("ones"), 1)
            pool.memset(eps[:, :], EPS).then_inc(sem("ones"), 1)
            stage_end(pool, 0)

            def experts(m, k):
                pool.wait_ge(sem("disp_zero"), 16 * (m + 1))
                for q in range(K):
                    hold(pool, sem("slots"), K * m + q + 1)
                    for t in range(TILES):
                        if q and t % PUT == 0:
                            hold(pool, sem("second"), TILES // PUT * m + t // PUT + 1)
                        pool.indirect_dma_start(
                            disp[m], bass.IndirectOffsetOnAxis(ap=put_at[:, q * TILES + t:q * TILES + t + 1], axis=0),
                            XN[:, t, :], None, bounds_check=SLOTS - 1, oob_is_err=False)\
                            .then_inc(sem(f"put{t // PUT}"), 16)
                pool.wait_ge(sem("ytok_zero"), 16 * (m + 1))

                def store(i, first):
                    for c in range(EC):
                        hold(pool, sem("y_out"), 16 * m + EC * i + c + 1)
                        for j in range(PER_CHUNK):
                            pool.indirect_dma_start(
                                ytok[m], bass.IndirectOffsetOnAxis(ap=y_at[:, PER_CHUNK * c + j:PER_CHUNK * c + j + 1], axis=0),
                                yo[:, c, j, :], None, bounds_check=K * TOKENS - 1, oob_is_err=False)\
                                .then_inc(sem(f"y_put{c}"), 16)

                repeat(pool, E, store)
                pool.wait_ge(sem("gates"), m + 1)
                for g in range(TILES // GROUP):
                    hold(pool, sem(f"got{g}"), 16 * (m + 1))
                    group = slice(GROUP * g, GROUP * (g + 1))
                    pool.tensor_tensor(yg[:, group, :, :], yg[:, group, :, :],
                                       gate[:, :, group].rearrange("p q t -> p t q").unsqueeze(3).to_broadcast([P, GROUP, K, D]),
                                       ALU.mult).then_inc(sem("gated"), 1)
                    hold(pool, sem("gated"), 8 * m + g + 1)
                    pool.tensor_tensor(yg[:, group, 0, :], yg[:, group, 0, :], yg[:, group, 1, :], ALU.add)\
                        .then_inc(sem("y_sum"), 1)
                stage_end(pool, k + 1)

            experts(0, 0)

            def mamba(b, first):
                for n in range(DS):
                    for d in range(DT):
                        u = DT * n + d
                        if n == 0 and d == 0:
                            hold(pool, sem("dtu"), b + 1)
                        hold(pool, sem("Bs"), DS * b + n + 1)
                        if not (first and u < NW):
                            hold(pool, sem("ysum"), 32 * b + u + 1 - NW)
                        pool.tensor_tensor(w[:, u % NW, :], dtu[:, d, :], Bs[:, n % 2, :], ALU.mult)\
                            .then_inc(sem("dBu"), 1)

            repeat(pool, BATCH, mamba)
            stage_end(pool, 2)
            experts(1, 2)

            def soft(s, k):
                base = UNITS * s

                def normalise(u, r):
                    hold(pool, sem("rD"), u + 1)
                    if not below(u, RING):
                        hold(pool, sem("slotX"), u + 1 - RING)
                    pool.tensor_tensor(Dd[:, r, :].rearrange("p (n q) -> p n q", q=PSLOT),
                                       Ed[:, r, :].rearrange("p (n q) -> p n q", q=PSLOT),
                                       over(rD[:, r, :], PSLOT), ALU.mult).then_inc(sem("Dd"), 1)

                def shift(u, r):
                    hold(pool, sem("mD"), u + 1)
                    if not below(u, RING):
                        hold(pool, sem("Dd"), u + 1 - RING)
                    pool.tensor_tensor(Ed[:, r, :].rearrange("p (n q) -> p n q", q=PSLOT),
                                       Lc[:, r, :].rearrange("p (n q) -> p n q", q=PSLOT),
                                       over(mD[:, r, :], PSLOT), ALU.subtract).then_inc(sem("Es"), 1)

                def units(i):
                    for r in range(RING):
                        u = base + RING * i + r
                        shift(u, r)
                        if not below(RING * i + r, 2):
                            normalise(u - 2, (r - 2) % RING)

                dispatch_loop(pool, units)
                for r in (2, 3):
                    normalise(base + UNITS - RING + r, r)
                if s == 0:
                    stage_end(pool, k + 1)

            soft(0, 3)

            def gla(b, first):
                for v in range(HD):
                    hold(pool, sem("kv_scan"), HD * b + v + 1)
                    pool.tensor_tensor(kv[:, v % NW, :], q_s[:, ds(b, 1), :].rearrange("p a t -> p (a t)"), kv[:, v % NW, :],
                                       ALU.mult).then_inc(sem("qS"), 1)

            repeat(pool, BATCH, gla)
            stage_end(pool, 5)
            soft(1, 5)

        @block.scalar
        def _(act):
            chain = Chain(act, "act_chain")
            act.preload_act_table_set("natural_log_exp_and_others")

            def ln_scale(n, c):
                hold(act, sem("ln_var"), 8 * n + c + 1)
                act.activation(ln_s[:, 6, ds(4 * c, 4)], ln_s[:, 5, ds(4 * c, 4)], ACT.Ln).then_inc(sem("ln_ln"), 1)
                hold(act, sem("ln_ln"), 8 * n + c + 1)
                act.activation(ln_s[:, 7, ds(4 * c, 4)], ln_s[:, 6, ds(4 * c, 4)], ACT.Exp, scale=-0.5)\
                    .then_inc(sem("ln_rstd"), 1)

            def ln_copies(n, b, h, bank):
                c = 2 * b + h
                if n in KEPT:
                    hold(act, sem("ln_x"), 8 * n + c + 1)
                    act.activation(XN[:, ds(4 * c, 4), 0:D], stage[:, h, :].rearrange("p (j d) -> p j d", d=D),
                                   ACT.Copy).then_inc(sem("ln_keep"), 1)
                hold(act, sem("ln_T"), 8 * n + c + 1)
                act.activation(XT[:, ds(b, 1), CONV_PAD + CHUNK * h:CONV_PAD + CHUNK * (h + 1)].rearrange("p a t -> p (a t)"),
                               pbank(bank), ACT.Copy).then_inc(sem("ln_XT"), 1)

            for c in range(CHUNKS):
                ln_scale(0, c)
                if c:
                    ln_copies(0, (c - 1) // 2, (c - 1) % 2, 0)
            ln_copies(0, BATCH - 1, 1, 0)
            stage_end(act, 0)

            def experts(m, k):
                hold(act, sem("g_diff"), m + 1)
                act.activation(g1[5], g1[4], ACT.Exp).then_inc(sem("g_exp"), 1)
                if m == 0:
                    act.wait_ge(sem("consts1"), 16 * len(loads[1]))
                    chain(act.activation(A_neg[:, :, :], A_log[:, :, :], ACT.Exp))
                    chain(act.activation(A_neg[:, :, :], A_neg[:, :, :], ACT.Copy, scale=-1.0))

                def evac_T(v, c):
                    hold(act, sem("d_T"), v + 1)
                    act.activation(dT[:, c, :], pbank(c), ACT.Copy).then_inc(sem("dT"), 1)

                base = 16 * m
                evac_T(base, 0)

                def chunks(i, first, last=False):
                    for p in range(2):
                        for c in range(EC):
                            v = base + 4 * i + 2 * p + c
                            for hb in (0, 2):
                                hold(act, sem("l1"), HB * v + hb + 1)
                                act.activation(hT[:, c, hb, :], pbank(2 + hb), ACT.Relu,
                                               bias=b1[:, ds(2 * i + p, 1), hb:hb + 1].rearrange("p a b -> p (a b)"))\
                                    .then_inc(sem("hT_act"), 1)
                            if not (last and p == 1 and c == EC - 1):
                                evac_T(v + 1, 1 - c)

                chunks(0, True)
                with act.Fori(1, E // 2 - 1) as i:
                    chunks(i, False)
                chunks(E // 2 - 1, False, True)
                n = 2 * m + 1
                for c in range(CHUNKS):
                    ln_scale(n, c)
                    if c:
                        ln_copies(n, (c - 1) // 2, (c - 1) % 2, 0)
                ln_copies(n, BATCH - 1, 1, 0)
                stage_end(act, k + 1)

            experts(0, 0)

            act.preload_act_table(ACT.Silu)

            def project(b, first):
                for h in range(HALVES):
                    v = 2 * b + h
                    for d in range(DT):
                        hold(act, sem("u_ps"), DT * v + d + 1)
                        if h == 0 and not first:
                            hold(act, sem(f"conv{d}"), v)
                        act.activation(u_pad[:, d, CONV_PAD + CHUNK * h:CONV_PAD + CHUNK * (h + 1)], pbank(d), ACT.Copy)\
                            .then_inc(sem("u_sb"), 1)
                    for d in range(DT):
                        hold(act, sem("u_sb"), DT * v + d + 1)
                        if not below(v, 1):
                            hold(act, sem("uc"), DT * (v - 1) + d + 1)
                        act.activation(cacc[:, d, :], tap(d, h, 0), ACT.Copy, scale=conv_w[:, d, 0:1]).then_inc(sem(f"tap{d}"), 1)
                    for d in range(DT):
                        hold(act, sem("z_ps"), DT * v + d + 1)
                        act.activation(zs[:, d, ds(b, 1), CHUNK * h:CHUNK * (h + 1)].rearrange("p a t -> p (a t)"),
                                       pbank(2 + d), ACT.Silu).then_inc(sem("zs"), 1)
                    if not (first and h == 0):
                        low_rank(v - 1, b if h else b - 1, 1 - h)
                    for d in range(DT):
                        hold(act, sem(f"conv{d}"), v + 1)
                        act.activation(uc[:, d, ds(b, 1), CHUNK * h:CHUNK * (h + 1)].rearrange("p a t -> p (a t)"), cacc[:, d, :],
                                       ACT.Silu, bias=conv_b[:, d:d + 1]).then_inc(sem("uc"), 1)

            def low_rank(v, b, h):
                hold(act, sem("bc_ps"), v + 1)
                act.activation(BCs[0:96, ds(b * TIME + CHUNK * h, CHUNK)], pbank(6 + h)[0:96, :], ACT.Copy).then_inc(sem("dts"), 1)
                act.activation(dts[0:RANK, ds(b, 1), CHUNK * h:CHUNK * (h + 1)].rearrange("p a t -> p (a t)"),
                               pbank(6 + h)[96:96 + RANK, :], ACT.Copy).then_inc(sem("dts"), 1)

            act.wait_ge(sem("u_padded"), 1)
            repeat(act, BATCH, project)
            low_rank(CHUNKS - 1, BATCH - 1, 1)
            act.preload_act_table_set("natural_log_exp_and_others")

            def magnitude(v, h, d):
                hold(act, sem("x_ps"), DT * v + d + 1)
                act.activation(sp_ln[:, h, d, :], pbank(DT * h + d), ACT.Abs, bias=b_dt[:, d:d + 1]).then_inc(sem("sp1"), 1)

            def softplus(b, first, last=False):
                for h in range(HALVES):
                    v = 2 * b + h
                    hold(act, sem("sp1"), DT * v + 2)
                    act.activation(sp_ln[:, h, :, :], sp_ln[:, h, :, :], ACT.Exp, scale=-1.0).then_inc(sem("sp2"), 1)
                    if not (last and h == 1):
                        if not (first and h == 0):
                            hold(act, sem("delta"), DT * v)
                        for d in range(DT):
                            magnitude(v + 1, 1 - h, d)
                    hold(act, sem("sp2"), v + 1)
                    act.activation(sp_ln[:, h, :, :], sp_ln[:, h, :, :], ACT.Ln, bias=1.0).then_inc(sem("sp3"), 1)

            hold(act, sem("BCs"), CHUNKS)
            for d in range(DT):
                magnitude(0, 0, d)
            softplus(0, True)
            with act.Fori(1, BATCH - 1) as i:
                softplus(i, False)
            softplus(BATCH - 1, False, True)
            hold(act, sem("pre_all"), 1)

            def scan_in(b, first):
                for n in range(DS):
                    v = DS * b + n
                    hold(act, sem("bc"), v + 1)
                    if not (first and n < 2):
                        hold(act, sem("dBu"), DT * (v - 1))
                    act.activation(Bs[:, n % 2, :], pbank(0, 2), ACT.Copy).then_inc(sem("Bs"), 1)
                    if not (first and n < 2):
                        hold(act, sem("hC"), DT * (v - 1))
                    act.activation(Cs[:, n % 2, :], pbank(2, 2), ACT.Copy).then_inc(sem("Cs"), 1)
                    for d in range(DT):
                        if not (first and n == 0):
                            hold(act, sem("scan"), DT * (v - 1) + d + 1)
                        act.activation(dA[:, d, :], dlt[d][:, ds(b * TIME, TIME)], ACT.Exp, scale=A_neg[:, d, n:n + 1])\
                            .then_inc(sem("dA"), 1)

            repeat(act, BATCH, scan_in)
            for c in range(CHUNKS):
                ln_scale(2, c)
                if c:
                    ln_copies(2, (c - 1) // 2, (c - 1) % 2, 6)
            ln_copies(2, BATCH - 1, 1, 6)
            stage_end(act, 2)

            experts(1, 2)

            def soft(s, k):
                base = UNITS * s

                def copy_xt(t, r):
                    if not below(t, 2):
                        hold(act, sem("L"), base + 2 * t - 2)
                    act.activation(xts[:, r, :], XT[:, ds(t // PER_BATCH, 1), ds(CONV_PAD + (P * t) % TIME, P)]
                                   .rearrange("p a t -> p (a t)"), ACT.Copy).then_inc(sem("xts"), 1)

                def copy_xn(t, r):
                    if not below(t, 2):
                        hold(act, sem("slotX"), base + 2 * t - 2)
                    act.activation(xns[:, r, :], XN[:, ds(t, 1), 0:D].rearrange("p a d -> p (a d)"),
                                   ACT.Copy).then_inc(sem("xns"), 1)

                def copy_L(u, r):
                    hold(act, sem("L"), base + u + 1)
                    if not below(u, RING):
                        hold(act, sem("Es"), base + u + 1 - RING)
                        hold(act, sem("mxC"), base + u + 1 - RING)
                    act.activation(Lc[:, r, :], pbank(2 * (r % 2), 2), ACT.Copy).then_inc(sem("Lc"), 1)

                def units(i):
                    last = isinstance(i, int) and i == UNITS // RING - 1
                    for r in range(RING):
                        u = RING * i + r
                        if not (last and r == RING - 1):
                            copy_L(u + 1, (r + 1) % RING)
                        if r % 2 == 0:
                            if not last:
                                copy_xt(2 * i + 2 + r // 2, r // 2)
                            if not below(u, 1):
                                copy_xn(2 * i - 1 + r // 2, 1 - r // 2)
                        hold(act, sem("Es"), base + u + 1)
                        act.activation(Ed[:, r, :], Ed[:, r, :], ACT.Exp).then_inc(sem("Ed"), 1)

                copy_xt(0, 0)
                copy_xt(1, 1)
                copy_L(0, 0)
                dispatch_loop(act, units)
                copy_xn(TILES - 1, 1)
                for g in range(4):
                    hold(act, sem("mCT_ps"), 4 * s + g + 1)
                    act.activation(mCT[0:64, 1024 * g:1024 * (g + 1)], pbank(4 + g).bitcast(BF16)[0:64, :], ACT.Copy)\
                        .then_inc(sem("mCT"), 1)
                    if g % 2 == 1:
                        h = g // 2
                        hold(act, sem("slot_c"), 2 * s + h + 1)
                        act.activation(slotB[:, 1024 * h:1024 * (h + 1)], slotA[:, 1024 * h:1024 * (h + 1)], ACT.Square)\
                            .then_inc(sem("slot_sq"), 1)
                for h in range(2):
                    hold(act, sem("slot_v"), 2 * s + h + 1)
                    chain(act.activation(slotB[:, 1024 * h:1024 * (h + 1)], pbank(4 + 2 * h, 2), ACT.Ln, bias=eps[:, :]))
                    act.activation(slotB[:, 1024 * h:1024 * (h + 1)], slotB[:, 1024 * h:1024 * (h + 1)], ACT.Exp,
                                   scale=-0.5).then_inc(sem("slot_r"), 1)

                def slots_tanh():
                    for h in range(2):
                        hold(act, sem("slot_n"), 2 * s + h + 1)
                        act.activation(slotA[:, 1024 * h:1024 * (h + 1)], slotA[:, 1024 * h:1024 * (h + 1)], ACT.Tanh)\
                            .then_inc(sem("slot_t"), 1)
                    act.preload_act_table_set("natural_log_exp_and_others")

                def exp_T(v, c, first, before=None, beside=None, at=0):
                    for t in range(ST):
                        if beside and t == at:
                            beside()
                        if before and t == ST - 4:
                            ln_scale(4, 2 * before[0] + before[1])
                        hold(act, sem("LT"), ST * v + t + 1)
                        if t == 0 and not first:
                            hold(act, sem("yT_ps"), v - 1)
                        act.activation(Ec[c][:, t, :], pbank(t % 4), ACT.Exp, bias=phi_bc[:, t:t + 1])\
                            .then_inc(sem("Ec"), 1)

                def finish(v):
                    hold(act, sem("Z"), v + 1)
                    act.activation(lnz, pbank(4), ACT.Ln).then_inc(sem("lnz"), 1)
                    hold(act, sem("lnz"), v + 1)
                    act.activation(Rz, lnz, ACT.Exp, scale=-1.0).then_inc(sem("Rz"), 1)

                def copy_y(v):
                    hold(act, sem("yT_ps"), v + 1)
                    act.activation(yT, pbank(5), ACT.Copy).then_inc(sem("yT"), 1)

                base = CHUNKS * s
                exp_T(base, 0, True, beside=slots_tanh, at=12)
                hold(act, sem("Yt"), 4 * (s + 1))
                exp_T(base + 1, 1, True, beside=lambda: finish(base), at=9)
                copy_y(base)
                finish(base + 1)

                with act.Fori(1, CHUNKS // 2) as i:
                    for c in range(2):
                        v = base + 2 * i + c
                        exp_T(v, c, False, (i - 1, c) if s == 0 else None)
                        copy_y(v - 1)
                        if s == 0:
                            ln_copies(4, i - 1, c, 7)
                        finish(v)
                if s == 0:
                    ln_scale(4, CHUNKS - 2)
                copy_y(base + CHUNKS - 1)
                if s == 0:
                    ln_copies(4, BATCH - 1, 0, 7)
                    ln_scale(4, CHUNKS - 1)
                    ln_copies(4, BATCH - 1, 1, 7)
                if s == 0:
                    stage_end(act, k + 1)

            soft(0, 3)

            act.preload_act_table(ACT.Sigmoid)

            def gla_in(b, first):
                for h in range(HALVES):
                    v = 2 * b + h
                    hold(act, sem("low_ps"), v + 1)
                    act.activation(low[0:HD, 0, :], pbank(2)[0:HD, :], ACT.Copy).then_inc(sem("low"), 1)
                    act.activation(low[0:HD, 1, :], pbank(3)[0:HD, :], ACT.Copy).then_inc(sem("low"), 1)
                    for j in range(2):
                        hold(act, sem("qk_ps"), 2 * v + j + 1)
                        if not (first and h == 0):
                            hold(act, sem("qk"), 2 * v + j - 1)
                        act.activation(sg[:, j, :], pbank(j), ACT.Sigmoid).then_inc(sem("qk_sig"), 1)
                    for j, t in enumerate((f_s, g_s)):
                        hold(act, sem("fg_ps"), 2 * v + j + 1)
                        act.activation(t[:, ds(b, 1), CHUNK * h:CHUNK * (h + 1)].rearrange("p a t -> p (a t)"), pbank(4 + j),
                                       ACT.Sigmoid).then_inc(sem("fg"), 1)

            repeat(act, BATCH, gla_in)
            act.preload_act_table_set("natural_log_exp_and_others")

            for b in range(BATCH):
                act.wait_ge(sem("og"), b + 1)
                for h in range(HALVES):
                    act.activation(sq[:, h, :], og[:, b, CHUNK * h:CHUNK * (h + 1)], ACT.Square).then_inc(sem("sq"), 1)
                for h in range(HALVES):
                    v = 2 * b + h
                    act.wait_ge(sem("ms"), v + 1)
                    if v:
                        act.wait_ge(sem("rms"), v)
                    act.activation(rms[:, 0, :], pbank(6), ACT.Ln, bias=eps[:, :]).then_inc(sem("rms0"), 1)
                    act.wait_ge(sem("rms0"), v + 1)
                    if v:
                        act.wait_ge(sem("nrm"), v)
                    act.activation(rms[:, 1, :], rms[:, 0, :], ACT.Exp, scale=-0.5).then_inc(sem("rms"), 1)
                for h in range(HALVES):
                    ln_scale(5, 2 * b + h)
                    ln_copies(5, b, h, 6)
            stage_end(act, 5)
            soft(1, 5)

        @block.vector
        def _(dve):
            chain = Chain(dve, "dve_chain")
            dve.memset(zero[:, :], 0.0).then_inc(sem("zeroed"), 1)
            chain(dve.memset(XT[:, :, 0:CONV_PAD], 0.0))

            def ln_statistics(n, c):
                v = 8 * n + c
                for j in range(PER_CHUNK):
                    ins = dve.bn_stats(stats[:, ds(4 * c + j, 1), :].rearrange("p a b -> p (a b)"),
                                       X[:, ds(4 * c + j, 1), :].rearrange("p a b -> p (a b)"))
                ins.then_inc(sem("ln_step"), 1)
                dve.wait_ge(sem("ln_step"), 3 * v + 1)
                even, odd = (lambda j: stats[:, ds(4 * c, 4), j]), (lambda j: stats[:, ds(4 * c, 4), 3 + j])
                two_mean, gap, m2, gap2, var0, var, _, _, mean = (ln_s[:, j, ds(4 * c, 4)] for j in range(9))
                dve.tensor_tensor(two_mean, even(1), odd(1), ALU.add)
                dve.tensor_tensor(gap, even(1), odd(1), ALU.subtract)
                dve.tensor_tensor(m2, even(2), odd(2), ALU.add).then_inc(sem("ln_step"), 1)
                dve.wait_ge(sem("ln_step"), 3 * v + 2)
                dve.scalar_tensor_tensor(gap2, gap, 0.25, gap, ALU.mult, ALU.mult)
                dve.tensor_scalar(mean, two_mean, 0.5, None, ALU.mult)
                dve.tensor_scalar(var0, m2, 1.0 / D, EPS, ALU.mult, ALU.add).then_inc(sem("ln_step"), 1)
                dve.wait_ge(sem("ln_step"), 3 * v + 3)
                dve.tensor_tensor(var, var0, gap2, ALU.add).then_inc(sem("ln_var"), 1)

            def ln_apply(n, c, h):
                v = 8 * n + c
                dve.wait_ge(sem("ln_rstd"), v + 1)
                if not (isinstance(v, int) and v < 2):
                    dve.wait_ge(sem("ln_T"), v - 1)
                    if n in KEPT and not (isinstance(c, int) and c < 2):
                        dve.wait_ge(sem("ln_keep"), 8 * KEPT.index(n) + c - 1)
                for j in range(PER_CHUNK):
                    t = 4 * c + j
                    ins = dve.tensor_scalar(stage[:, h, D * j:D * (j + 1)], X[:, ds(t, 1), :].rearrange("p a d -> p (a d)"),
                                            ln_s[:, 8, ds(t, 1)], ln_s[:, 7, ds(t, 1)], ALU.subtract, ALU.mult)
                ins.then_inc(sem("ln_x"), 1)

            for c in range(CHUNKS):
                if c % 2 == 0:
                    dve.wait_ge(sem(f"x_in{c // 2}"), 16)
                ln_statistics(0, c)
                if c:
                    ln_apply(0, c - 1, (c - 1) % 2)
            ln_apply(0, CHUNKS - 1, 1)
            dve.wait_ge(sem("consts0"), 16 * len(loads[0]))
            chain(dve.tensor_copy(tri[:, :], tri_f))

            def derive():
                dve.wait_ge(sem("consts1"), 16 * len(loads[1]))
                for d in range(DT):
                    dve.tensor_scalar(diag_D[:, d, :], ident[:, :], D_skip[:, d:d + 1], None, ALU.mult)
                dve.tensor_copy(W_bc3[:, :, 96:96 + RANK], W_x[:, :, 0:RANK])
                for j in range(3):
                    dve.tensor_copy(W_bc3[:, :, 32 * j:32 * (j + 1)], W_x[:, :, RANK:RANK + 32])
                for dst, src in ((identb, ident[:, :]), (row32, row32_f)):
                    chain(dve.tensor_copy(dst[:, :], src))
                for j in range(EPT):
                    chain(dve.tensor_copy(row128[:, 32 * j:32 * (j + 1)], row32[0:64, :]))
                chain(dve.tensor_copy(rest, phi_b3f))
                for j in range(3):
                    chain(dve.tensor_copy(part, rest))
                    if j == 0:
                        chain(dve.tensor_scalar(acc, part, ident[0:3, 0:1], None, ALU.mult))
                    else:
                        chain(dve.scalar_tensor_tensor(acc, part, ident[0:3, j:j + 1], acc, ALU.mult, ALU.add))
                    if j < 2:
                        chain(dve.tensor_tensor(row, rest, part, ALU.subtract))
                        chain(dve.tensor_copy(rest, row))
                chain(dve.tensor_copy(phi_b3[:, :], acc))

            stage_end(dve, 0)

            def experts(m, k):
                dve.wait_ge(sem("logits"), m + 1)
                lg = pbank(7)[:, 0:TILES * E].rearrange("p (t e) -> p t e", e=E)
                revb = rev[:, :].unsqueeze(1).to_broadcast([P, TILES, E])
                m1, m2, d21, e2, den, gt1, gt2 = g1[0], g1[1], g1[4], g1[5], g1[6], g1[7], g1[8]
                incl, loc, tmp = run
                place, ok, lc, base, slot, far = (g.rearrange("p (a b) -> p a b", b=TILES) for g in g64[0:6])
                wide = TILES * E
                chain(dve.tensor_copy(XN[:, :, D], row_id[:, :]))
                for q, top in enumerate((m1, m2)):
                    src = lg if q == 0 else g8[2]
                    mq = mask[:, q, :].rearrange("p (t e) -> p t e", e=E)
                    chain(dve.tensor_reduce(top, src, AX, ALU.max))
                    chain(dve.tensor_tensor(g8[0], src, over(top, E), ALU.is_equal))
                    chain(dve.tensor_tensor(g8[1], g8[0], revb, ALU.mult))
                    chain(dve.tensor_reduce(rank[:, q, :], g8[1], AX, ALU.max))
                    chain(dve.tensor_tensor(mq, g8[1], over(rank[:, q, :], E), ALU.is_equal))
                    dve.nop().then_inc(sem("masks"), 1)
                    if q == 0:
                        chain(dve.scalar_tensor_tensor(g8[2], mq, LOWEST, lg, ALU.mult, ALU.add))
                    else:
                        dve.tensor_tensor(d21, m2, m1, ALU.subtract).then_inc(sem("g_diff"), 1)
                    dve.wait_ge(sem("counts"), 2 * m + q + 1)
                    at = slice(wide * q, wide * (q + 1))
                    before = TILES * (q + 1)
                    tv = pbank(6)[:, 0:wide * (q + 1)].rearrange("p (t e) -> p t e", e=E)
                    iv = incl[:, 0:wide * (q + 1)].rearrange("p (t e) -> p t e", e=E)
                    for e in range(E):
                        ins = dve.tensor_tensor_scan(iv[:, :, e], ones64[:, 0:before], tv[:, :, e], 0.0, ALU.mult, ALU.add)
                    chain(ins)
                    chain(dve.tensor_tensor(tmp[:, at], incl[:, at], pbank(6)[:, at], ALU.subtract))
                    chain(dve.tensor_tensor(loc[:, at], tmp[:, at], pbank(5)[:, at], ALU.add))
                    chain(dve.tensor_tensor(tmp[:, at], loc[:, at], mask[:, q, :], ALU.mult))
                    chain(dve.tensor_reduce(place[:, q, :], tmp[:, at].rearrange("p (t e) -> p t e", e=E), AX, ALU.add))
                    dve.tensor_scalar(ok[:, q, :], place[:, q, :], CAP + 0.5, None, ALU.is_lt)
                    dve.tensor_scalar(lc[:, q, :], place[:, q, :], float(CAP), -1.0, ALU.min, ALU.add)
                    chain(dve.tensor_scalar(base[:, q, :], rank[:, q, :], -float(CAP), float(SLOTS), ALU.mult, ALU.add))
                    dve.tensor_tensor(slot[:, q, :], base[:, q, :], lc[:, q, :], ALU.add)
                    chain(dve.tensor_scalar(far[:, q, :], ok[:, q, :], -FAR, FAR, ALU.mult, ALU.add))
                    dve.tensor_tensor(put_at[:, TILES * q:TILES * (q + 1)], far[:, q, :], slot[:, q, :], ALU.add)\
                        .then_inc(sem("slots"), 1)
                dve.wait_ge(sem("g_exp"), m + 1)
                chain(dve.tensor_scalar(den, e2, 1.0, None, ALU.add))
                chain(dve.reciprocal(gt1, den))
                chain(dve.tensor_tensor(gt2, e2, gt1, ALU.mult))
                for q, g in enumerate((gt1, gt2)):
                    chain(dve.scalar_tensor_tensor(gate[:, q, :], g, 0.5, ok[:, q, :], ALU.mult, ALU.mult))
                dve.nop().then_inc(sem("gates"), 1)
                if m == 0:
                    derive()
                for g in range(TILES // PUT):
                    dve.wait_ge(sem(f"put{g}"), 16 * PUT * (K * m + 1))
                    ids = XN[:, PUT * g:PUT * (g + 1), D]
                    dve.tensor_scalar(ids, ids, 1.0, None, ALU.add).then_inc(sem("second"), 1)

                sbase = 16 * m

                def places(v, c, loaded, used):
                    rows = dtile[:, c, :, D]
                    dve.wait_ge(sem(f"d_in{c}"), 16 * loaded)
                    if not below(v, 1):
                        dve.wait_ge(sem("y_at"), v)
                    if not below(used, 1):
                        dve.wait_ge(sem(f"y_put{c}"), 16 * PER_CHUNK * used)
                    dve.tensor_scalar(empty, rows, 0.5, FAR, ALU.is_lt, ALU.mult).then_inc(sem("empty"), 1)
                    dve.wait_ge(sem("empty"), v + 1)
                    dve.scalar_tensor_tensor(y_at[:, PER_CHUNK * c:PER_CHUNK * (c + 1)], rows, -1.0, empty, ALU.add, ALU.add)\
                        .then_inc(sem("y_at"), 1)

                def chunks(i, first):
                    for p in range(2):
                        for c in range(EC):
                            r = 4 * i + 2 * p + c
                            v = sbase + r
                            for hb in (1, 3):
                                dve.wait_ge(sem("l1"), HB * v + hb + 1)
                                dve.tensor_scalar(hT[:, c, hb, :], pbank(2 + hb),
                                                  b1[:, ds(2 * i + p, 1), hb:hb + 1].rearrange("p a b -> p (a b)"), 0.0,
                                                  ALU.add, ALU.max).then_inc(sem("hT_dve"), 1)
                            places(v, c, 8 * m + 2 * i + p + 1, 8 * m + 2 * i + p)
                            if not (first and p == 0 and c == 0):
                                e = 2 * i + p if c == 1 else 2 * i + p - 1
                                add_bias(v - 1, 1 - c, e, 8 * m + 2 * i + p if c == 1 else 8 * m + 2 * i + p - 1)

                def add_bias(v, c, e, stored):
                    dve.wait_ge(sem("l2"), v + 1)
                    if not below(stored, 1):
                        dve.wait_ge(sem(f"y_put{c}"), 16 * PER_CHUNK * stored)
                    dve.tensor_tensor(yo[:, c, :, :], pbank(6 + c).rearrange("p (j d) -> p j d", d=D),
                                      b2[:, ds(e, 1), :].to_broadcast([P, PER_CHUNK, D]), ALU.add).then_inc(sem("y_out"), 1)

                repeat(dve, E // 2, chunks)
                add_bias(sbase + 15, 1, E - 1, 8 * m + 7)
                for grp in range(TILES // GROUP):
                    dve.wait_ge(sem("y_sum"), 8 * m + grp + 1)
                    xb = X[:, GROUP * grp:GROUP * (grp + 1), :]
                    chain(dve.tensor_tensor(xb, xb, yg[:, GROUP * grp:GROUP * (grp + 1), 0, :], ALU.add))
                    ln_statistics(2 * m + 1, grp)
                    if grp:
                        ln_apply(2 * m + 1, grp - 1, (grp - 1) % 2)
                ln_apply(2 * m + 1, CHUNKS - 1, 1)
                stage_end(dve, k + 1)

            experts(0, 0)


            chain(dve.memset(u_pad[:, :, 0:CONV_PAD], 0.0))
            dve.nop().then_inc(sem("u_padded"), 1)

            def split_bc(v, b, h):
                S = BCs[:, ds(b * TIME + CHUNK * h, CHUNK)]
                dve.wait_ge(sem("dts"), 2 * (v + 1))
                if not below(v, 1):
                    dve.wait_ge(sem("BCs"), v)
                dve.tensor_tensor(bcf[0:96, :], pbank(6 + h)[0:96, :], S[0:96, :], ALU.subtract).then_inc(sem("bc_rest"), 1)
                dve.wait_ge(sem("bc_rest"), v + 1)
                dve.tensor_copy(bcm[64:96, :], bcf[64:96, :]).then_inc(sem("bc_mid"), 1)
                dve.tensor_copy(S[32:64, :], bcf[32:64, :])
                dve.wait_ge(sem("bc_mid"), v + 1)
                dve.tensor_tensor(S[64:96, :], bcf[64:96, :], bcm[64:96, :], ALU.subtract).then_inc(sem("BCs"), 1)

            def project(b, first):
                for h in range(HALVES):
                    v = 2 * b + h
                    for j in range(1, DCONV):
                        for d in range(DT):
                            dve.wait_ge(sem(f"tap{d}"), 3 * v + j)
                            dve.scalar_tensor_tensor(cacc[:, d, :], tap(d, h, j), conv_w[:, d, j:j + 1], cacc[:, d, :],
                                                     ALU.mult, ALU.add).then_inc(sem(f"conv{d}" if j == DCONV - 1 else f"tap{d}"), 1)
                    if not (first and h == 0):
                        split_bc(v - 1, b if h else b - 1, 1 - h)

            repeat(dve, BATCH, project)
            split_bc(CHUNKS - 1, BATCH - 1, 1)

            def deltas(b, first):
                for h in range(HALVES):
                    v = 2 * b + h
                    for d in range(DT):
                        dve.wait_ge(sem("sp1"), DT * v + d + 1)
                        dve.tensor_scalar(sp_relu[:, h, d, :], pbank(DT * h + d), b_dt[:, d:d + 1], 0.0, ALU.add, ALU.max)\
                            .then_inc(sem("relu"), 1)
                    dve.wait_ge(sem("relu"), DT * (v + 1))
                    dve.wait_ge(sem("sp3"), v + 1)
                    for d in range(DT):
                        dve.tensor_tensor(dlt[d][:, ds(b * TIME + CHUNK * h, CHUNK)], sp_relu[:, h, d, :], sp_ln[:, h, d, :],
                                          ALU.add).then_inc(sem("delta"), 1)

            repeat(dve, BATCH, deltas)
            dve.wait_ge(sem("delta"), DT * CHUNKS)
            dve.wait_ge(sem("BCs"), CHUNKS)
            dve.wait_ge(sem("uc"), DT * CHUNKS)
            dve.wait_ge(sem("x_ps"), DT * CHUNKS)
            dve.nop().then_inc(sem("pre_all"), 1)

            def steps_times_u(b):
                for d in range(DT):
                    ins = dve.tensor_tensor(dtu[:, d, :], dlt[d][:, ds(b * TIME, TIME)],
                                            uc[:, d, ds(b, 1), :].rearrange("p a t -> p (a t)"), ALU.mult)
                ins.then_inc(sem("dtu"), 1)

            def scans(b, first, last=False):
                ub = lambda d: uc[:, d, ds(b, 1), :].rearrange("p a t -> p (a t)")
                zb = lambda d: zs[:, d, ds(b, 1), :].rearrange("p a t -> p (a t)")
                if first:
                    steps_times_u(0)

                def scale(u):
                    n = u // DT
                    dve.wait_ge(sem("scan"), 32 * b + u + 1)
                    dve.wait_ge(sem("Cs"), DS * b + n + 1)
                    dve.tensor_tensor(w[:, u % NW, :], w[:, u % NW, :], Cs[:, n % 2, :], ALU.mult).then_inc(sem("hC"), 1)

                for u in range(DT * DS):
                    n, d = u // DT, u % DT
                    dve.wait_ge(sem("dA"), 32 * b + u + 1)
                    dve.wait_ge(sem("dBu"), 32 * b + u + 1)
                    dve.tensor_tensor_scan(w[:, u % NW, :], dA[:, d, :], w[:, u % NW, :], 0.0, ALU.mult, ALU.add)\
                        .then_inc(sem("scan"), 1)
                    scale(u)
                if not last:
                    dve.wait_ge(sem("dBu"), 32 * (b + 1))
                    steps_times_u(b + 1)
                dve.wait_ge(sem("ysum"), 32 * (b + 1))
                for d in range(DT):
                    ins = dve.tensor_tensor(ub(d), pbank(4 + 2 * d, 2), zb(d), ALU.mult)
                ins.then_inc(sem("yz"), 1)

            dve.wait_ge(sem("zs"), DT * CHUNKS)
            scans(0, True)
            with dve.Fori(1, BATCH - 1) as i:
                scans(i, False)
            scans(BATCH - 1, False, True)
            for c in range(CHUNKS):
                dve.wait_ge(sem("m_out"), c + 1)
                xb = X[:, 4 * c:4 * (c + 1), :]
                chain(dve.tensor_tensor(xb, xb, pbank(c % 4).rearrange("p (j d) -> p j d", d=D), ALU.add))
                dve.nop().then_inc(sem("m_add"), 1)
                ln_statistics(2, c)
                if c:
                    ln_apply(2, c - 1, (c - 1) % 2)
            ln_apply(2, CHUNKS - 1, 1)
            stage_end(dve, 2)

            experts(1, 2)

            def soft(s, k):
                base = UNITS * s

                def maxima(u, t, r):
                    dve.wait_ge(sem("Lc"), u + 1)
                    if not below(u, RING):
                        dve.wait_ge(sem("Es"), u + 1 - RING)
                    dve.tensor_reduce(mD[:, r, :], Lc[:, r, :].rearrange("p (n q) -> p n q", q=PSLOT), AX, ALU.max)\
                        .then_inc(sem("mD"), 1)
                    dve.tensor_reduce(mxC[:, r % 2, ds(t, 1), :].rearrange("p a q -> p (a q)"),
                                      Lc[:, r, :].rearrange("p (n q) -> p q n", q=PSLOT), AX, ALU.max).then_inc(sem("mxC"), 1)

                def sums(u, r):
                    dve.wait_ge(sem("Ed"), u + 1)
                    dve.tensor_reduce(sD[:, r, :], Ed[:, r, :].rearrange("p (n q) -> p n q", q=PSLOT), AX, ALU.add)\
                        .then_inc(sem("sD"), 1)
                    dve.wait_ge(sem("sD"), u + 1)
                    dve.reciprocal(rD[:, r, :], sD[:, r, :]).then_inc(sem("rD"), 1)

                def units(i):
                    for r in range(RING):
                        u = base + RING * i + r
                        maxima(u, 2 * i + r // 2, r)
                        if not below(RING * i + r, 1):
                            sums(u - 1, (r - 1) % RING)

                dispatch_loop(dve, units)
                sums(base + UNITS - 1, RING - 1)
                dve.wait_ge(sem("slotX"), UNITS * (s + 1))
                for h in range(2):
                    dve.tensor_scalar(slotX[:, HW * h:HW * (h + 1)], pbank(4 + 2 * h, 2), -33000.0, 65000.0,
                                      ALU.max, ALU.min).then_inc(sem("clipped"), 1)
                dve.wait_ge(sem("mxC"), UNITS * (s + 1))
                chain(dve.tensor_tensor(mxC[:, 0, :, :], mxC[:, 0, :, :], mxC[:, 1, :, :], ALU.max))
                chain(dve.tensor_scalar(mCs[:, :, 0:PSLOT], mxC[:, 0, :, :], -1.0, None, ALU.mult))
                dve.scalar_tensor_tensor(mCs[:, :, PSLOT:2 * PSLOT], mxC[:, 0, :, :], -1.0, mCs[:, :, 0:PSLOT],
                                         ALU.mult, ALU.subtract).then_inc(sem("mCs"), 1)
                for h in range(2):
                    dve.wait_ge(sem("slot_m"), 2 * s + h + 1)
                    dve.tensor_tensor(slotA[:, 1024 * h:1024 * (h + 1)], slotX[:, 1024 * h:1024 * (h + 1)], pbank(2 * h, 2),
                                      ALU.subtract).then_inc(sem("slot_c"), 1)
                for h in range(2):
                    dve.wait_ge(sem("slot_r"), 2 * s + h + 1)
                    dve.tensor_tensor(slotA[:, 1024 * h:1024 * (h + 1)], slotA[:, 1024 * h:1024 * (h + 1)],
                                      slotB[:, 1024 * h:1024 * (h + 1)], ALU.mult).then_inc(sem("slot_n"), 1)
                for g in range(4):
                    dve.wait_ge(sem("Yt_ps"), 4 * s + g + 1)
                    if g == 0:
                        dve.wait_ge(sem("we"), 16 * (1 + EPT) * (s + 1))
                    dve.tensor_tensor(Yt[:, 4 * g:4 * (g + 1), :], pbank(4 + g).rearrange("p (s h) -> p s h", h=D),
                                      eb[:, 4 * g:4 * (g + 1), :], ALU.add).then_inc(sem("Yt"), 1)
                base = CHUNKS * s

                def normalise(v, c):
                    ec = Ec[c]
                    for j, (dst, lo, hi) in enumerate(((t8[:, 0:4, :], ec[:, 0:4, :], ec[:, 4:8, :]),
                                                       (t8[:, 4:8, :], ec[:, 8:12, :], ec[:, 12:16, :]),
                                                       (t4, t8[:, 0:4, :], t8[:, 4:8, :]),
                                                       (t2, t4[:, 0:2, :], t4[:, 2:4, :]), (t1, t2[:, 0, :], t2[:, 1, :]))):
                        if j < 2:
                            dve.wait_ge(sem("Ec"), ST * v + 8 * (j + 1))
                        else:
                            dve.wait_ge(sem("tree"), 5 * v + j)
                        dve.tensor_tensor(dst, lo, hi, ALU.add).then_inc(sem("tree"), 1)
                    dve.wait_ge(sem("Rz"), v + 1)
                    for g in range(2):
                        half = ec[:, 8 * g:8 * (g + 1), :]
                        dve.tensor_tensor(half, half, Rz.unsqueeze(1).to_broadcast([P, ST // 2, CHUNK]), ALU.mult)\
                            .then_inc(sem("C"), 1)

                def residual(v, i2, c):
                    dve.wait_ge(sem("y_tok"), v + 1)
                    xb = X[:, ds(8 * i2 + 4 * c, 4), :]
                    dve.scalar_tensor_tensor(xb, pbank(6).rearrange("p (j d) -> p j d", d=D), 0.5, xb, ALU.mult, ALU.add)\
                        .then_inc(sem("s_add"), 1)
                    if s == 0:
                        dve.wait_ge(sem("s_add"), v + 1)
                        ln_statistics(4, 2 * i2 + c)

                normalise(base, 0)
                normalise(base + 1, 1)
                residual(base, 0, 0)

                with dve.Fori(1, CHUNKS // 2) as i:
                    if s == 0:
                        ln_apply(4, 2 * i - 2, 0)
                    normalise(base + 2 * i, 0)
                    residual(base + 2 * i - 1, i - 1, 1)
                    if s == 0:
                        ln_apply(4, 2 * i - 1, 1)
                    normalise(base + 2 * i + 1, 1)
                    residual(base + 2 * i, i, 0)
                if s == 0:
                    ln_apply(4, CHUNKS - 2, 0)
                residual(base + CHUNKS - 1, CHUNKS // 2 - 1, 1)
                if s == 0:
                    ln_apply(4, CHUNKS - 1, 1)
                if s == 0:
                    stage_end(dve, k + 1)

            soft(0, 3)

            for v in range(HD):
                ins = dve.tensor_copy(Wvv[:, v, :].rearrange("p (h k) -> p h k", k=HD),
                                      Wv[:, :].rearrange("p (h v) -> p h v", v=HD)[:, :, v:v + 1].to_broadcast([P, HEADS, HD]))
            ins.then_inc(sem("Wvv"), 1)

            def gla_in(b, first):
                for h in range(HALVES):
                    v = 2 * b + h
                    for j, (t, c) in enumerate(((q_s, float(HD) ** -0.5), (k_s, 1.0))):
                        dve.wait_ge(sem("qk_sig"), 2 * v + j + 1)
                        dve.scalar_tensor_tensor(t[:, ds(b, 1), CHUNK * h:CHUNK * (h + 1)].rearrange("p a t -> p (a t)"),
                                                 pbank(j), c, sg[:, j, :], ALU.mult, ALU.mult).then_inc(sem("qk"), 1)

            with dve.Fori(0, BATCH) as i:
                gla_in(i, False)
            dve.wait_ge(sem("fg"), 2 * CHUNKS)
            dve.wait_ge(sem("qk"), 2 * CHUNKS)

            def gated(b):
                dve.wait_ge(sem("osum"), HD * (b + 1))
                dve.tensor_tensor(og[:, ds(b, 1), :].rearrange("p a t -> p (a t)"), g_s[:, ds(b, 1), :].rearrange("p a t -> p (a t)"),
                                  pbank(4, 2), ALU.mult).then_inc(sem("og"), 1)

            def heads(v):
                dve.wait_ge(sem("rms"), v + 1)
                if v > 1:
                    dve.wait_ge(sem("a_out"), v - 1)
                dve.scalar_tensor_tensor(nrm[:, v % 2, :], og[:, v // 2, CHUNK * (v % 2):CHUNK * (v % 2 + 1)],
                                         norm_w[:, 0:1], rms[:, 1, :], ALU.mult, ALU.mult).then_inc(sem("nrm"), 1)

            def attended(v):
                dve.wait_ge(sem("a_out"), v + 1)
                xb = X[:, 4 * v:4 * (v + 1), :]
                dve.tensor_tensor(xb, xb, pbank(7).rearrange("p (j d) -> p j d", d=D), ALU.add).then_inc(sem("a_add"), 1)
                dve.wait_ge(sem("a_add"), v + 1)
                ln_statistics(5, v)

            def beside(b, step):
                c = 2 * b
                if step == 1:
                    gated(b)
                if step == 3:
                    heads(c)
                if step == 4:
                    heads(c + 1)
                if step == 5:
                    attended(c)
                if step == 6:
                    attended(c + 1)
                    ln_apply(5, c, 0)
                if step == 7:
                    ln_apply(5, c + 1, 1)

            for b in range(BATCH):
                kb, fb = k_s[:, b, :], f_s[:, b, :]
                for v in range(HD):
                    n = HD * b + v
                    dve.wait_ge(sem("vb"), n + 1)
                    if n >= NW:
                        dve.wait_ge(sem("osum"), n + 1 - NW)
                    dve.tensor_tensor(kv[:, v % NW, :], kb, pbank(2 * (v % 2), 2), ALU.mult).then_inc(sem("kv"), 1)
                    dve.wait_ge(sem("kv"), n + 1)
                    dve.tensor_tensor_scan(kv[:, v % NW, :], fb, kv[:, v % NW, :], 0.0, ALU.mult, ALU.add)\
                        .then_inc(sem("kv_scan"), 1)
                    if b:
                        beside(b - 1, v)
            for step in range(HD):
                beside(BATCH - 1, step)
            stage_end(dve, 5)
            soft(1, 5)

        @block.tensor
        def _(pe):
            pe.wait_ge(sem("ones"), 4)
            pe.wait_ge(sem("consts0"), 16 * len(loads[0]))

            def ln_turn(n, c, h, bank):
                v = 8 * n + c
                pe.wait_ge(sem("ln_x"), v + 1)
                if not (isinstance(v, int) and v == 0):
                    pe.wait_ge(sem("ln_XT"), v)
                for j in range(PER_CHUNK):
                    ins = pe.transpose(pbank(bank)[:, P * j:P * (j + 1)], stage[:, h, P * j:P * (j + 1)], ident[:, :])
                ins.then_inc(sem("ln_T"), 1)

            def gates(n, c):
                pe.wait_ge(sem("ln_XT"), 8 * n + c + 1)
                for t in range(PER_CHUNK * c, PER_CHUNK * (c + 1)):
                    b, j = t // PER_BATCH, t % PER_BATCH
                    ins = pe.matmul(pbank(7)[:, E * t:E * (t + 1)], XT[:, b, CONV_PAD + P * j:CONV_PAD + P * (j + 1)], wg[:, :],
                                    start=True, stop=True)
                if c == CHUNKS - 1:
                    ins.then_inc(sem("logits"), 1)

            for c in range(CHUNKS):
                ln_turn(0, c, c % 2, 0)
                if c:
                    gates(0, c - 1)
            gates(0, CHUNKS - 1)
            stage_end(pe, 0)

            def xt(b, h, shift=0):
                return XT[:, ds(b, 1), CONV_PAD + CHUNK * h - shift:CONV_PAD + CHUNK * (h + 1) - shift].rearrange("p a t -> p (a t)")

            def experts(m, k):
                for q in range(K):
                    at = slice(TILES * E * q, TILES * E * (q + 1))
                    pe.wait_ge(sem("masks"), K * m + q + 1)
                    pe.matmul(pbank(5)[:, at], tri[:, :], mask[:, q, :], start=True, stop=True)
                    pe.matmul(pbank(6)[:, at], onesb[:, :], mask[:, q, :], start=True, stop=True).then_inc(sem("counts"), 1)
                base = 16 * m

                def turn(v, c, loaded):
                    pe.wait_ge(sem(f"d_in{c}"), 16 * loaded)
                    if not (isinstance(v, int) and v < 2):
                        pe.wait_ge(sem("dT"), v - 1)
                    for j in range(PER_CHUNK):
                        ins = pe.transpose(pbank(c)[:, P * j:P * (j + 1)], dtile[:, c, j, 0:D], ident[:, :])
                    ins.then_inc(sem("d_T"), 1)

                def layer1(v, c, p):
                    pe.wait_ge(sem("dT"), v + 1)
                    for hb in range(HB):
                        if not (isinstance(v, int) and v == 0):
                            pe.wait_ge(sem("hT_act" if hb % 2 == 0 else "hT_dve"), 2 * v - 1 + hb // 2)
                        pe.matmul(pbank(2 + hb), w1s[:, p, P * hb:P * (hb + 1)], dT[:, c, :], start=True, stop=True)\
                            .then_inc(sem("l1"), 1)

                def layer2(v, c, p):
                    pe.wait_ge(sem("hT_act"), 2 * (v + 1))
                    pe.wait_ge(sem("hT_dve"), 2 * (v + 1))
                    if not (isinstance(v, int) and v < 2):
                        pe.wait_ge(sem("y_out"), v - 1)
                    for j in range(PER_CHUNK):
                        for hb in range(HB):
                            ins = pe.matmul(pbank(6 + c)[:, P * j:P * (j + 1)], hT[:, c, hb, P * j:P * (j + 1)], w2s[:, p, hb, :],
                                            start=(hb == 0), stop=(hb == HB - 1))
                    ins.then_inc(sem("l2"), 1)

                pe.wait_ge(sem("slots"), K * (m + 1))
                turn(base, 0, 8 * m + 1)

                def chunks(i, first, last=False):
                    for p in range(2):
                        for c in range(EC):
                            v = base + 4 * i + 2 * p + c
                            if c == 0:
                                pe.wait_ge(sem(f"w_in{p}"), 32 * (4 * m + i + 1))
                            layer1(v, c, p)
                            if not (last and p == 1 and c == 1):
                                turn(v + 1, 1 - c, 8 * m + 2 * i + p + 1 + c)
                            if not (first and p == 0 and c == 0):
                                layer2(v - 1, 1 - c, p if c == 1 else 1 - p)

                chunks(0, True)
                with pe.Fori(1, E // 2 - 1) as i:
                    chunks(i, False)
                chunks(E // 2 - 1, False, True)
                layer2(base + 15, 1, 1)
                for c in range(CHUNKS):
                    ln_turn(2 * m + 1, c, c % 2, 0)
                stage_end(pe, k + 1)

            experts(0, 0)


            def project(b, first):
                for h in range(HALVES):
                    v = 2 * b + h
                    for d in range(DT):
                        if not (first and h == 0):
                            pe.wait_ge(sem("u_sb"), DT * (v - 1) + d + 1)
                        pe.matmul(pbank(d), W_in[:, P * d:P * (d + 1)], xt(b, h), start=True, stop=True).then_inc(sem("u_ps"), 1)
                    for d in range(DT):
                        if not (first and h == 0):
                            pe.wait_ge(sem("zs"), DT * (v - 1) + d + 1)
                        pe.matmul(pbank(2 + d), W_in[:, DI + P * d:DI + P * (d + 1)], xt(b, h), start=True, stop=True)\
                            .then_inc(sem("z_ps"), 1)
                    if not (first and h == 0):
                        low_rank(v - 1, b if h else b - 1, 1 - h)

            def low_rank(v, b, h):
                pe.wait_ge(sem("uc"), DT * (v + 1))
                if not below(v, 2):
                    pe.wait_ge(sem("bc_rest"), v - 1)
                for d in range(DT):
                    ins = pe.matmul(pbank(6 + h)[0:96 + RANK, :], W_bc3[:, d, :],
                                    uc[:, d, ds(b, 1), CHUNK * h:CHUNK * (h + 1)].rearrange("p a t -> p (a t)"),
                                    start=(d == 0), stop=(d == DT - 1))
                ins.then_inc(sem("bc_ps"), 1)

            repeat(pe, BATCH, project)
            low_rank(CHUNKS - 1, BATCH - 1, 1)

            pe.wait_ge(sem("u_sb"), DT * CHUNKS)
            pe.wait_ge(sem("zs"), DT * CHUNKS)

            def steps(b, first):
                for h in range(HALVES):
                    v = 2 * b + h
                    hold(pe, sem("dts"), 2 * (v + 1))
                    for d in range(DT):
                        if not first:
                            hold(pe, sem("relu"), DT * (v - 2) + d + 1)
                        pe.matmul(pbank(DT * h + d), W_dt[:, P * d:P * (d + 1)],
                                  dts[0:RANK, ds(b, 1), CHUNK * h:CHUNK * (h + 1)].rearrange("p a t -> p (a t)"),
                                  start=True, stop=True).then_inc(sem("x_ps"), 1)

            repeat(pe, BATCH, steps)
            pe.wait_ge(sem("pre_all"), 1)

            def spread(v, b, n, early):
                for q, name in enumerate(("Bs", "Cs")):
                    if not early:
                        pe.wait_ge(sem(name), v)
                    for h in range(HALVES):
                        ins = pe.matmul(pbank(2 * q + h), row32[:, DS * q + n:DS * q + n + 1].to_broadcast([96, P]),
                                        BCs[0:96, ds(b * TIME + CHUNK * h, CHUNK)], start=True, stop=True)
                ins.then_inc(sem("bc"), 1)

            def scans(b, first, last=False):
                def add(u):
                    n, d = u // DT, u % DT
                    pe.wait_ge(sem("hC"), 32 * b + u + 1)
                    for h in range(HALVES):
                        ins = pe.matmul(pbank(4 + 2 * d + h), ident[:, :], w[:, u % NW, CHUNK * h:CHUNK * (h + 1)],
                                        start=False, stop=(n == DS - 1))
                    ins.then_inc(sem("ysum"), 1)

                if not first:
                    pe.wait_ge(sem("yz"), b)
                for d in range(DT):
                    for h in range(HALVES):
                        pe.matmul(pbank(4 + 2 * d + h), diag_D[:, d, :],
                                  uc[:, d, ds(b, 1), CHUNK * h:CHUNK * (h + 1)].rearrange("p a t -> p (a t)"), start=True, stop=False)
                for n in range(DS):
                    v = DS * b + n + 2
                    if n + 2 < DS:
                        spread(v, b, n + 2, False)
                    elif not last:
                        spread(v, b + 1, n + 2 - DS, False)
                    for d in range(DT):
                        add(DT * n + d)

            spread(0, 0, 0, True)
            spread(1, 0, 1, False)
            scans(0, True)
            with pe.Fori(1, BATCH - 1) as i:
                scans(i, False)
            scans(BATCH - 1, False, True)
            pe.wait_ge(sem("yz"), BATCH)
            for c in range(CHUNKS):
                if c >= 4:
                    pe.wait_ge(sem("m_add"), c - 3)
                for j in range(PER_CHUNK):
                    t = PER_CHUNK * c + j
                    at = P * (t % PER_BATCH)
                    for d in range(DT):
                        ins = pe.matmul(pbank(c % 4)[:, P * j:P * (j + 1)], uc[:, d, t // PER_BATCH, at:at + P], W_out[:, d, :],
                                        start=(d == 0), stop=(d == DT - 1))
                ins.then_inc(sem("m_out"), 1)
                if c > 1:
                    ln_turn(2, c - 2, c % 2, 6)
                if c > 2:
                    gates(2, c - 3)
            for c in range(CHUNKS - 3, CHUNKS):
                if c > CHUNKS - 3:
                    ln_turn(2, c, c % 2, 6)
                gates(2, c)
            stage_end(pe, 2)

            experts(1, 2)

            def soft(s, k):
                base = UNITS * s

                def logits(u, t, r):
                    h = r % 2
                    if h == 0:
                        pe.wait_ge(sem("xts"), TILES * s + t + 1)
                    if not below(u, 2):
                        pe.wait_ge(sem("Lc"), u - 1)
                    for c in range(2):
                        at = HW * h + CHUNK * c
                        pe.matmul(pbank(2 * h + c), xts[:, r // 2, :], phiT[:, at:at + CHUNK], start=True, stop=False)
                        ins = pe.matmul(pbank(2 * h + c), onesb[0:3, :], phi_b3[:, at:at + CHUNK], start=False, stop=True)
                    ins.then_inc(sem("L"), 1)

                def gather(u, t, r, start, stop):
                    h = r % 2
                    pe.wait_ge(sem("Dd"), u + 1)
                    if h == 0:
                        pe.wait_ge(sem("xns"), TILES * s + t + 1)
                    for c in range(2):
                        ins = pe.matmul(pbank(4 + 2 * h + c), xns[:, r // 2, :], Dd[:, r, CHUNK * c:CHUNK * (c + 1)],
                                        start=start, stop=stop, skip_group_check=True)
                    ins.then_inc(sem("slotX"), 1)

                def units(i):
                    for r in range(RING):
                        u = base + RING * i + r
                        t = 2 * i + r // 2
                        logits(u, t, r)
                        if not below(i, 1):
                            gather(u - RING, t - 2, r, below(t - 2, 1), False)

                dispatch_loop(pe, units)
                for r in range(RING):
                    gather(base + UNITS - RING + r, TILES - 2 + r // 2, r, False, r >= 2)
                for h in range(2):
                    pe.wait_ge(sem("clipped"), 2 * s + h + 1)
                    for c in range(2):
                        at = 1024 * h + CHUNK * c
                        ins = pe.matmul(pbank(2 * h + c), mean_w[:, :], slotX[:, at:at + CHUNK], start=True, stop=True)
                    ins.then_inc(sem("slot_m"), 1)
                pe.wait_ge(sem("mCs"), s + 1)
                for g in range(4):
                    for j in range(8):
                        ins = pe.transpose(pbank(4 + g).bitcast(BF16)[0:64, P * j:P * (j + 1)], mCs[:, 8 * g + j, :], identb[:, :])
                    ins.then_inc(sem("mCT_ps"), 1)
                for h in range(2):
                    pe.wait_ge(sem("mCT"), 4 * s + 2 * (h + 1))
                    pe.wait_ge(sem("slot_sq"), 2 * s + h + 1)
                    for c in range(2):
                        at = 1024 * h + CHUNK * c
                        ins = pe.matmul(pbank(4 + 2 * h + c), mean_w[:, :], slotB[:, at:at + CHUNK], start=True, stop=True)
                    ins.then_inc(sem("slot_v"), 1)
                base = CHUNKS * s

                def logits_T(v, b, c, early, beside=None):
                    for t in range(ST):
                        if beside and t == 9:
                            beside()
                        if not (early and t < 4):
                            pe.wait_ge(sem("Ec"), ST * v + t - 3)
                        pe.matmul(pbank(t % 4), phiT[:, P * t:P * (t + 1)], xt(b, c), start=True, stop=False)
                        pe.matmul(pbank(t % 4), row128[:, :],
                                  mCT[0:64, ds(b * TIME + CHUNK * c, CHUNK)], start=False, stop=True).then_inc(sem("LT"), 1)

                def slot_outputs():
                    pe.wait_ge(sem("slot_r"), 2 * (s + 1))
                    pe.wait_ge(sem("we"), 16 * (1 + EPT) * (s + 1))
                    for g in range(4):
                        pe.wait_ge(sem("slot_t"), 2 * s + g // 2 + 1)
                        for t in range(4):
                            for j in range(EPT):
                                n = EPT * (4 * g + t) + j
                                ins = pe.matmul(pbank(4 + g)[PSLOT * j:PSLOT * (j + 1), P * t:P * (t + 1)],
                                                slotA[:, PSLOT * n:PSLOT * (n + 1)], We[:, n, :], start=True, stop=True,
                                                skip_group_check=True)
                        ins.then_inc(sem("Yt_ps"), 1)

                def total(v):
                    pe.wait_ge(sem("tree"), 5 * (v + 1))
                    pe.matmul(pbank(4), same_p[:, :], t1, start=True, stop=True).then_inc(sem("Z"), 1)

                def combine(v, c, early):
                    if not early:
                        pe.wait_ge(sem("yT"), v)
                    for t in range(ST):
                        if t % 8 == 0:
                            pe.wait_ge(sem("C"), 2 * v + t // 8 + 1)
                        ins = pe.matmul(pbank(5), Yt[:, t, :], Ec[c][:, t, :], start=(t == 0), stop=(t == ST - 1))
                    ins.then_inc(sem("yT_ps"), 1)

                def turn_y(v, early):
                    pe.wait_ge(sem("yT"), v + 1)
                    if not early:
                        pe.wait_ge(sem("s_add"), v)
                    for j in range(PER_CHUNK):
                        ins = pe.transpose(pbank(6)[:, P * j:P * (j + 1)], yT[:, P * j:P * (j + 1)], ident[:, :])
                    ins.then_inc(sem("y_tok"), 1)

                e0 = s == 0
                pe.wait_ge(sem("slot_c"), 2 * (s + 1))
                logits_T(base, 0, 0, True)
                slot_outputs()
                logits_T(base + 1, 0, 1, False, lambda: total(base))
                combine(base, 0, e0)
                total(base + 1)
                turn_y(base, e0)

                with pe.Fori(1, CHUNKS // 2) as i:
                    for c in range(2):
                        v = base + 2 * i + c
                        logits_T(v, i, c, False)
                        combine(v - 1, 1 - c, False)
                        if s == 0:
                            ln_turn(4, 2 * (i - 1) + c, c, 7)
                        total(v)
                        turn_y(v - 1, False)
                combine(base + CHUNKS - 1, 1, False)
                turn_y(base + CHUNKS - 1, False)
                if s == 0:
                    for c in range(2):
                        ln_turn(4, CHUNKS - 2 + c, c, 7)
                if s == 0:
                    stage_end(pe, k + 1)

            soft(0, 3)

            def gla_in(b, first):
                for h in range(HALVES):
                    v = 2 * b + h
                    if not (first and h == 0):
                        pe.wait_ge(sem("low"), 2 * v)
                    pe.matmul(pbank(2)[0:HD, :], Wf1[:, :], xt(b, h), start=True, stop=True)
                    pe.matmul(pbank(3)[0:HD, :], Wg1[:, :], xt(b, h), start=True, stop=True).then_inc(sem("low_ps"), 1)
                    for j, W in enumerate((Wq, Wk)):
                        if not (first and h == 0):
                            pe.wait_ge(sem("qk"), 2 * (v - 1) + j + 1)
                        pe.matmul(pbank(j), W[:, :], xt(b, h), start=True, stop=True).then_inc(sem("qk_ps"), 1)
                    pe.wait_ge(sem("low"), 2 * (v + 1))
                    for j, W in enumerate((Wf2, Wg2)):
                        if not (first and h == 0):
                            pe.wait_ge(sem("fg"), 2 * (v - 1) + j + 1)
                        pe.matmul(pbank(4 + j), W[:, :], low[0:HD, j, :], start=True, stop=True).then_inc(sem("fg_ps"), 1)

            repeat(pe, BATCH, gla_in)
            pe.wait_ge(sem("fg"), 2 * CHUNKS)
            pe.wait_ge(sem("qk"), 2 * CHUNKS)

            def values(n, b, v):
                if not below(n, 2):
                    pe.wait_ge(sem("kv"), n - 1)
                for h in range(HALVES):
                    ins = pe.matmul(pbank(2 * (v % 2) + h), Wvv[:, v, :], xt(b, h), start=True, stop=True)
                ins.then_inc(sem("vb"), 1)

            def mean_square(v):
                pe.wait_ge(sem("sq"), v + 1)
                if v:
                    pe.wait_ge(sem("rms0"), v)
                if v > 1 and v % 2 == 0:
                    pe.wait_ge(sem("ln_XT"), 8 * 5 + v)
                pe.matmul(pbank(6), head_mean[:, :], sq[:, v % 2, :], start=True, stop=True).then_inc(sem("ms"), 1)

            def project_heads(v):
                pe.wait_ge(sem("nrm"), v + 1)
                if v:
                    pe.wait_ge(sem("a_add"), v)
                for j in range(PER_CHUNK):
                    ins = pe.matmul(pbank(7)[:, P * j:P * (j + 1)], nrm[:, v % 2, P * j:P * (j + 1)], Wo[:, :], start=True, stop=True)
                ins.then_inc(sem("a_out"), 1)

            def beside(b, step):
                c = 2 * b
                if step == 1:
                    mean_square(c)
                    mean_square(c + 1)
                if step == 3:
                    project_heads(c)
                if step == 4:
                    project_heads(c + 1)
                if step == 6:
                    pe.wait_ge(sem("rms0"), c + 2)
                    ln_turn(5, c, 0, 6)
                if step == 7:
                    ln_turn(5, c + 1, 1, 6)

            pe.wait_ge(sem("Wvv"), 1)
            pe.wait_ge(sem("head_sum"), 16)
            values(0, 0, 0)
            values(1, 0, 1)
            for n in range(HD * BATCH):
                b, v = n // HD, n % HD
                if n + 2 < HD * BATCH:
                    values(n + 2, (n + 2) // HD, (n + 2) % HD)
                pe.wait_ge(sem("qS"), n + 1)
                if v == 0 and b:
                    pe.wait_ge(sem("og"), b)
                for h in range(HALVES):
                    ins = pe.matmul(pbank(4 + h), head_sum[:, v, :], kv[:, v % NW, CHUNK * h:CHUNK * (h + 1)],
                                    start=(v == 0), stop=(v == HD - 1))
                ins.then_inc(sem("osum"), 1)
                if b:
                    beside(b - 1, v)
            for step in range(HD):
                beside(BATCH - 1, step)
            stage_end(pe, 5)
            soft(1, 5)


def constants():
    i = np.arange(P)
    f = np.float32
    hs = np.zeros((P, HD, P), f)
    for v in range(HD):
        for h in range(HEADS):
            hs[h * HD:(h + 1) * HD, v, h * HD + v] = 1.0
    return {
        "k_ident": np.eye(P, dtype=f),
        "k_tri": (i[:, None] <= i[None, :]).astype(f),
        "k_row_id": (K * np.arange(TOKENS).reshape(TILES, P).T + 1).astype(f),
        "k_rev": np.broadcast_to(np.arange(E, 0, -1).astype(f), (P, E)).copy(),
        "k_row32": (np.arange(96)[:, None] % 32 == np.arange(32)[None, :]).astype(f),
        "k_same_p": (i[:, None] % PSLOT == i[None, :] % PSLOT).astype(f),
        "k_head_mean": (i[:, None] // HD == i[None, :] // HD).astype(f) / HD,
        "k_head_sum": hs,
    }


def kernel(**inputs):
    import concourse.bacc as bacc
    from concourse.bass_utils import run_bass_kernel_spmd

    arr = {k: np.ascontiguousarray(v) for k, v in inputs.items()}
    col = lambda v: np.ascontiguousarray(v.reshape(-1, P).T)
    arrays = {k: arr[k] for k in (
        "L0_attn_x", "L0_attn_W_in", "L0_attn_conv_w", "L0_attn_W_xproj", "L0_attn_W_dt", "L0_attn_A_log", "L0_attn_W_out", "L0_ffn_wg",
        "L0_ffn_w1", "L0_ffn_w2", "L0_ffn_b2", "L1_attn_Wq", "L1_attn_Wk", "L1_attn_Wv", "L1_attn_Wo", "L1_attn_Wf1",
        "L1_attn_Wf2", "L1_attn_Wg1", "L1_attn_Wg2", "L1_ffn_phi_b", "L1_ffn_expert_w", "L1_ffn_expert_b")}
    arrays["h_b1"] = np.ascontiguousarray(arr["L0_ffn_b1"].reshape(E, HB, P).transpose(2, 0, 1))
    arrays["h_conv_b"] = col(arr["L0_attn_conv_b"])
    arrays["h_b_dt"] = col(arr["L0_attn_b_dt"])
    arrays["h_D"] = col(arr["L0_attn_D"])
    arrays["h_phi_wT"] = np.ascontiguousarray(arr["L1_ffn_phi_w"].T)
    arrays["h_phi_b"] = col(arr["L1_ffn_phi_b"])
    arrays["h_norm_w"] = col(arr["L1_attn_norm_weight"])
    arrays.update(constants())

    nc = bacc.Bacc("TRN2", target_bir_lowering=False, num_devices=1)
    a, named = {}, {}
    for name, v in arrays.items():
        named["in_" + name] = v
        a[name] = nc.dram_tensor("in_" + name, v.shape, mybir.dt.from_np(v.dtype), kind="ExternalInput").ap()
    out = nc.dram_tensor("out_x", (BATCH, TIME, D), F32, kind="ExternalOutput").ap()
    disp = [nc.dram_tensor(f"slot_inputs{m}", (SLOTS, ROW), F32, kind="Internal").ap() for m in range(2)]
    ytok = [nc.dram_tensor(f"token_outputs{m}", (K * TOKENS, D), F32, kind="Internal").ap() for m in range(2)]
    build(nc, a, out, disp, ytok)
    r = run_bass_kernel_spmd(nc, [named], core_ids=[0])
    return r.results[0]["out_x"]
```
